# Optimizing a Trainium2 kernel written in Bass

```python
import numpy as np
import jax
import jax.numpy as jnp

def _softmax(x, axis=-1):
    return jax.nn.softmax(x, axis=axis)

def _gelu(x):
    return jax.nn.gelu(x, approximate=True)

def _silu(x):
    return jax.nn.silu(x)

def _sigmoid(x):
    return jax.nn.sigmoid(x)

def _layernorm(x, axis=-1, eps=1e-05):
    m = jnp.mean(x, axis=axis, keepdims=True)
    v = jnp.var(x, axis=axis, keepdims=True)
    return (x - m) / jnp.sqrt(v + eps)

def _scatter_add(tgt, idx, src, axis=0):
    return tgt.at[idx].add(src)

def _segment_sum(src, seg, n):
    return jax.ops.segment_sum(src, seg, n)
kernel_name = 'mk_xattn_ffn_d2_seqx_r8_960f4d'

def setup_inputs(seed: int=0):
    np.random.seed(seed)
    _w = jnp.asarray

    def _rec_inputs():
        import jax
        import jax.numpy as jnp
        _rk = jax.random.key(seed)
        x = 7.22e-05 + 1 * jax.random.normal(jax.random.fold_in(_rk, 1), (16, 128, 128), jnp.float32)
        _lenS = 128 - jax.random.randint(jax.random.fold_in(_rk, 7), (16,), 0, max(1, 128 // 4) + 1, jnp.int32)
        _lenS2 = 77 - jax.random.randint(jax.random.fold_in(_rk, 8), (16,), 0, max(1, 77 // 4) + 1, jnp.int32)
        _ctx_1024P = jax.random.normal(jax.random.fold_in(_rk, 11), (16, 16, 128), jnp.float32)
        _ctx_1024c = jax.random.dirichlet(jax.random.fold_in(_rk, 511), 0.3 * jnp.ones((16,), jnp.float32), (16, 77))
        _ctx_1024t = jnp.einsum('bsk,bkd->bsd', _ctx_1024c, _ctx_1024P)
        _ctx_1024t = _ctx_1024t * jax.lax.rsqrt(jnp.mean(jnp.square(_ctx_1024t)) + 1e-12) * 0.953939
        ctx_1024 = 4.13588e-05 + 0.999923 * (_ctx_1024t + 0.3 * jax.random.normal(jax.random.fold_in(_rk, 611), (16, 77, 128), jnp.float32))
        return (x, ctx_1024)
    x, ctx_1024 = _rec_inputs()

    def _L0_xattn_setup():
        import math
        import jax, jax.numpy as jnp
        import numpy as np
        H = 16
        D_MODEL = 128
        DK = D_MODEL // H
        K_FACTOR = 2

        def _time_delay_agg_inference(v, corr):
            B, _, _, L = v.shape
            top_k = min(int(K_FACTOR * math.log(L)), L)
            mean_value = jnp.mean(corr, axis=(1, 2))
            weights, delay = jax.lax.top_k(mean_value, top_k)
            tmp_corr = jax.nn.softmax(weights, axis=-1)
            idx = (delay[:, :, None] + jnp.arange(L)) % L
            gathered = jnp.take_along_axis(v[:, None], idx[:, :, None, None, :], axis=-1)
            return jnp.einsum('bk,bkhdl->bhdl', tmp_corr, gathered)
        key = jax.random.key(seed)
        ks = jax.random.split(key, 11)
        B, L, D = (4, 256, D_MODEL)
        s = 1.0 / math.sqrt(D)
        return {'queries': jax.random.normal(ks[0], (B, L, D), jnp.float32), 'keys': jax.random.normal(ks[1], (B, L, D), jnp.float32), 'values': jax.random.normal(ks[2], (B, L, D), jnp.float32), 'Wq': jax.random.normal(ks[3], (D, H * DK), jnp.float32) * s, 'bq': jnp.zeros((H * DK,), jnp.float32), 'Wk': jax.random.normal(ks[4], (D, H * DK), jnp.float32) * s, 'bk': jnp.zeros((H * DK,), jnp.float32), 'Wv': jax.random.normal(ks[5], (D, H * DK), jnp.float32) * s, 'bv': jnp.zeros((H * DK,), jnp.float32), 'Wo': jax.random.normal(ks[6], (H * DK, D), jnp.float32) * s, 'bo': jnp.zeros((D,), jnp.float32)}
    _L0_xattn_all = _L0_xattn_setup()
    _L0_xattn_in = {k: v for k, v in _L0_xattn_all.items() if k in ('Wq', 'bq', 'Wk', 'bk', 'Wv', 'bv', 'Wo', 'bo')}
    del _L0_xattn_all

    def _L0_ffn_setup():
        import jax, jax.numpy as jnp
        import numpy as np
        DIM = 128
        DEPTH = 2
        HEADS = 8
        DIM_HEAD = 64
        WINDOW = 64
        INNER = HEADS * DIM_HEAD
        HID = int(DIM * 4 * 2 / 3)
        B, N = (2, 1024)
        QK_SCALE = 8.0

        def shift_token(t):
            t1, t2 = jnp.split(t, 2, axis=-1)
            t2 = jnp.pad(t2, ((0, 0), (1, 0), (0, 0)))[:, :-1]
            return jnp.concatenate([t1, t2], axis=-1)

        def l2norm(t):
            return t / jnp.clip(jnp.linalg.norm(t, axis=-1, keepdims=True), 1e-12)

        def rotate_half(x):
            x1, x2 = jnp.split(x, 2, axis=-1)
            return jnp.concatenate([-x2, x1], axis=-1)

        def rotary_xpos(q, k):
            n = q.shape[-2]
            half_idx = jnp.arange(0, DIM_HEAD, 2, dtype=jnp.float32)
            inv_freq = 1.0 / 10000.0 ** (half_idx / DIM_HEAD)
            t = jnp.arange(n, dtype=jnp.float32)
            freqs = t[:, None] * inv_freq[None, :]
            freqs = jnp.concatenate([freqs, freqs], axis=-1)
            base = (half_idx + 0.4 * DIM_HEAD) / (1.4 * DIM_HEAD)
            power = (t - n // 2) / float(WINDOW // 2)
            scale = base[None, :] ** power[:, None]
            scale = jnp.concatenate([scale, scale], axis=-1)
            cos, sin = (jnp.cos(freqs), jnp.sin(freqs))
            q = q * cos * scale + rotate_half(q) * sin * scale
            k = k * cos / scale + rotate_half(k) * sin / scale
            return (q, k)

        def local_attention(q, k, v):
            b, h, n, d = q.shape
            w = n // WINDOW
            bq = q.reshape(b, h, w, WINDOW, d) * QK_SCALE
            bk = k.reshape(b, h, w, WINDOW, d)
            bv = v.reshape(b, h, w, WINDOW, d)

            def look_around(t):
                p = jnp.pad(t, ((0, 0), (0, 0), (1, 0), (0, 0), (0, 0)))
                return jnp.concatenate([p[:, :, :w], p[:, :, 1:]], axis=3)
            bk, bv = (look_around(bk), look_around(bv))
            bt = jnp.arange(n).reshape(w, WINDOW)
            btp = jnp.pad(bt, ((1, 0), (0, 0)), constant_values=-1)
            btk = jnp.concatenate([btp[:w], btp[1:]], axis=1)
            sim = jnp.einsum('bhwid,bhwjd->bhwij', bq, bk)
            i = bt[:, :, None]
            j = btk[:, None, :]
            mask = (i < j) | (i > j + WINDOW) | (j == -1)
            sim = jnp.where(mask, -jnp.finfo(sim.dtype).max, sim)
            attn = jax.nn.softmax(sim, axis=-1)
            out = jnp.einsum('bhwij,bhwjd->bhwid', attn, bv)
            return out.reshape(b, h, n, d)

        def _layer(x, wqkv, qs, ksc, wo, lg, lb, w1, b1, w2, b2):
            b, n, _ = x.shape
            h = shift_token(x)
            qkv = h @ wqkv
            q, k, v = jnp.split(qkv, 3, axis=-1)
            to_heads = lambda t: t.reshape(b, n, HEADS, DIM_HEAD).transpose(0, 2, 1, 3)
            q, k, v = (to_heads(q), to_heads(k), to_heads(v))
            q = l2norm(q) * qs
            k = l2norm(k) * ksc
            q, k = rotary_xpos(q, k)
            o = local_attention(q, k, v)
            o = o.transpose(0, 2, 1, 3).reshape(b, n, INNER)
            x = x + o @ wo
            h = shift_token(x)
            mu = h.mean(-1, keepdims=True)
            var = h.var(-1, keepdims=True)
            h = (h - mu) / jnp.sqrt(var + 1e-05) * lg + lb
            h = h @ w1 + b1
            a, g = jnp.split(h, 2, axis=-1)
            h = a * jax.nn.gelu(g, approximate=False)
            x = x + h @ w2 + b2
            return x
        key = jax.random.key(seed)
        ks = jax.random.split(key, 6)
        return {'x': jax.random.normal(ks[0], (B, N, DIM), jnp.float32), 'wqkv': jax.random.normal(ks[1], (DEPTH, DIM, 3 * INNER), jnp.float32) * 0.02, 'q_scale': jnp.ones((DEPTH, DIM_HEAD), jnp.float32), 'k_scale': jnp.ones((DEPTH, DIM_HEAD), jnp.float32), 'wo': jax.random.normal(ks[2], (DEPTH, INNER, DIM), jnp.float32) * 0.02, 'ln_g': jnp.ones((DEPTH, DIM), jnp.float32), 'ln_b': jnp.zeros((DEPTH, DIM), jnp.float32), 'w1': jax.random.normal(ks[3], (DEPTH, DIM, 2 * HID), jnp.float32) * 0.02, 'b1': jnp.zeros((DEPTH, 2 * HID), jnp.float32), 'w2': jax.random.normal(ks[4], (DEPTH, HID, DIM), jnp.float32) * 0.02, 'b2': jnp.zeros((DEPTH, DIM), jnp.float32)}
    _L0_ffn_all = _L0_ffn_setup()
    _L0_ffn_in = {k: v for k, v in _L0_ffn_all.items() if k in ('wqkv', 'q_scale', 'k_scale', 'wo', 'ln_g', 'ln_b', 'w1', 'b1', 'w2', 'b2')}
    del _L0_ffn_all

    def _L1_xattn_setup():
        import jax, jax.numpy as jnp
        import numpy as np
        H = 128
        B = 8
        L_CHAR = 256
        L_SUB = 128

        def _linear(x, W, b):
            return jnp.einsum('blh,oh->blo', x, W) + b

        def _interp_linear(x, out_len):
            L_in = x.shape[1]
            pos = (jnp.arange(out_len, dtype=x.dtype) + 0.5) * (L_in / out_len) - 0.5
            pos = jnp.clip(pos, 0.0, L_in - 1)
            lo = jnp.floor(pos).astype(jnp.int32)
            hi = jnp.minimum(lo + 1, L_in - 1)
            w = (pos - lo.astype(x.dtype))[None, :, None]
            return x[:, lo] * (1 - w) + x[:, hi] * w
        key = jax.random.key(seed)
        ks = jax.random.split(key, 18)
        s = 0.02
        inp = {'char_emb': jax.random.normal(ks[0], (B, L_CHAR, H), jnp.float32), 'subword_emb': jax.random.normal(ks[1], (B, L_SUB, H), jnp.float32)}
        names = ['Wq_c', 'Wk_s', 'Wv_s', 'Wq_s', 'Wk_c', 'Wv_c']
        for i, n in enumerate(names):
            inp[n] = jax.random.normal(ks[2 + 2 * i], (H, H), jnp.float32) * s
            inp['b' + n[1:]] = jax.random.normal(ks[3 + 2 * i], (H,), jnp.float32) * s
        inp['Wg'] = jax.random.normal(ks[14], (H, 2 * H), jnp.float32) * s
        inp['bg'] = jax.random.normal(ks[15], (H,), jnp.float32) * s
        return inp
    _L1_xattn_all = _L1_xattn_setup()
    _L1_xattn_in = {k: v for k, v in _L1_xattn_all.items() if k in ('Wq_c', 'bq_c', 'Wk_s', 'bk_s', 'Wv_s', 'bv_s', 'Wq_s', 'bq_s', 'Wk_c', 'bk_c', 'Wv_c', 'bv_c', 'Wg', 'bg')}
    del _L1_xattn_all

    def _L1_ffn_setup():
        import jax, jax.numpy as jnp
        import numpy as np
        B, S, D_MODEL, D_HIDDEN = (4, 256, 128, 512)

        def act_quant(x):
            scale = 127.0 / jnp.clip(jnp.max(jnp.abs(x), axis=-1, keepdims=True), 1e-05)
            return jnp.clip(jnp.round(x * scale), -128, 127) / scale

        def weight_quant(w):
            scale = 1.0 / jnp.clip(jnp.mean(jnp.abs(w)), 1e-05)
            return jnp.clip(jnp.round(w * scale), -1, 1) / scale

        def bit_linear(x, w):
            xq = x + jax.lax.stop_gradient(act_quant(x) - x)
            wq = w + jax.lax.stop_gradient(weight_quant(w) - w)
            return jnp.einsum('bsd,hd->bsh', xq, wq)

        def depthwise_conv1d(x_bcl, w, b):
            y = jax.lax.conv_general_dilated(x_bcl, w, window_strides=(1,), padding=[(1, 1)], dimension_numbers=('NCH', 'OIH', 'NCH'), feature_group_count=x_bcl.shape[1])
            return y + b[None, :, None]
        key = jax.random.key(seed)
        ks = jax.random.split(key, 5)
        lim1 = 1.0 / np.sqrt(D_MODEL)
        lim2 = 1.0 / np.sqrt(D_HIDDEN)
        limc = 1.0 / np.sqrt(3.0)
        return {'x': jax.random.normal(ks[0], (B, S, D_MODEL), dtype=jnp.float32), 'w1': jax.random.uniform(ks[1], (D_HIDDEN, D_MODEL), jnp.float32, -lim1, lim1), 'conv_w': jax.random.uniform(ks[2], (D_HIDDEN, 1, 3), jnp.float32, -limc, limc), 'conv_b': jax.random.uniform(ks[3], (D_HIDDEN,), jnp.float32, -limc, limc), 'w2': jax.random.uniform(ks[4], (D_MODEL, D_HIDDEN), jnp.float32, -lim2, lim2)}
    _L1_ffn_all = _L1_ffn_setup()
    _L1_ffn_in = {k: v for k, v in _L1_ffn_all.items() if k in ('w1', 'conv_w', 'conv_b', 'w2')}
    del _L1_ffn_all
    return {'x': x, 'ctx_1024': ctx_1024, 'L0_xattn_Wq': _L0_xattn_in['Wq'], 'L0_xattn_bq': _L0_xattn_in['bq'], 'L0_xattn_Wk': _L0_xattn_in['Wk'], 'L0_xattn_bk': _L0_xattn_in['bk'], 'L0_xattn_Wv': _L0_xattn_in['Wv'], 'L0_xattn_bv': _L0_xattn_in['bv'], 'L0_xattn_Wo': _L0_xattn_in['Wo'], 'L0_xattn_bo': _L0_xattn_in['bo'], 'L0_ffn_wqkv': _L0_ffn_in['wqkv'], 'L0_ffn_q_scale': _L0_ffn_in['q_scale'], 'L0_ffn_k_scale': _L0_ffn_in['k_scale'], 'L0_ffn_wo': _L0_ffn_in['wo'], 'L0_ffn_ln_g': _L0_ffn_in['ln_g'], 'L0_ffn_ln_b': _L0_ffn_in['ln_b'], 'L0_ffn_w1': _L0_ffn_in['w1'], 'L0_ffn_b1': _L0_ffn_in['b1'], 'L0_ffn_w2': _L0_ffn_in['w2'], 'L0_ffn_b2': _L0_ffn_in['b2'], 'L1_xattn_Wq_c': _L1_xattn_in['Wq_c'], 'L1_xattn_bq_c': _L1_xattn_in['bq_c'], 'L1_xattn_Wk_s': _L1_xattn_in['Wk_s'], 'L1_xattn_bk_s': _L1_xattn_in['bk_s'], 'L1_xattn_Wv_s': _L1_xattn_in['Wv_s'], 'L1_xattn_bv_s': _L1_xattn_in['bv_s'], 'L1_xattn_Wq_s': _L1_xattn_in['Wq_s'], 'L1_xattn_bq_s': _L1_xattn_in['bq_s'], 'L1_xattn_Wk_c': _L1_xattn_in['Wk_c'], 'L1_xattn_bk_c': _L1_xattn_in['bk_c'], 'L1_xattn_Wv_c': _L1_xattn_in['Wv_c'], 'L1_xattn_bv_c': _L1_xattn_in['bv_c'], 'L1_xattn_Wg': _L1_xattn_in['Wg'], 'L1_xattn_bg': _L1_xattn_in['bg'], 'L1_ffn_w1': _L1_ffn_in['w1'], 'L1_ffn_conv_w': _L1_ffn_in['conv_w'], 'L1_ffn_conv_b': _L1_ffn_in['conv_b'], 'L1_ffn_w2': _L1_ffn_in['w2']}

def reference(x, ctx_1024, L0_xattn_Wq, L0_xattn_bq, L0_xattn_Wk, L0_xattn_bk, L0_xattn_Wv, L0_xattn_bv, L0_xattn_Wo, L0_xattn_bo, L0_ffn_wqkv, L0_ffn_q_scale, L0_ffn_k_scale, L0_ffn_wo, L0_ffn_ln_g, L0_ffn_ln_b, L0_ffn_w1, L0_ffn_b1, L0_ffn_w2, L0_ffn_b2, L1_xattn_Wq_c, L1_xattn_bq_c, L1_xattn_Wk_s, L1_xattn_bk_s, L1_xattn_Wv_s, L1_xattn_bv_s, L1_xattn_Wq_s, L1_xattn_bq_s, L1_xattn_Wk_c, L1_xattn_bk_c, L1_xattn_Wv_c, L1_xattn_bv_c, L1_xattn_Wg, L1_xattn_bg, L1_ffn_w1, L1_ffn_conv_w, L1_ffn_conv_b, L1_ffn_w2):
    import jax
    import jax.numpy as jnp

    def _L0_xattn_ref(queries, keys, values, Wq, bq, Wk, bk, Wv, bv, Wo, bo):
        import math
        import jax, jax.numpy as jnp
        import numpy as np
        H = 16
        D_MODEL = 128
        DK = D_MODEL // H
        K_FACTOR = 2

        def _time_delay_agg_inference(v, corr):
            B, _, _, L = v.shape
            top_k = min(int(K_FACTOR * math.log(L)), L)
            mean_value = jnp.mean(corr, axis=(1, 2))
            weights, delay = jax.lax.top_k(mean_value, top_k)
            tmp_corr = jax.nn.softmax(weights, axis=-1)
            idx = (delay[:, :, None] + jnp.arange(L)) % L
            gathered = jnp.take_along_axis(v[:, None], idx[:, :, None, None, :], axis=-1)
            return jnp.einsum('bk,bkhdl->bhdl', tmp_corr, gathered)
        B, Lq, _ = queries.shape
        Lk = keys.shape[1]
        q = (queries @ Wq + bq).reshape(B, Lq, H, DK)
        k = (keys @ Wk + bk).reshape(B, Lk, H, DK)
        v = (values @ Wv + bv).reshape(B, Lk, H, DK)
        if Lq > Lk:
            pad = ((0, 0), (0, Lq - Lk), (0, 0), (0, 0))
            k = jnp.pad(k, pad)
            v = jnp.pad(v, pad)
        else:
            k = k[:, :Lq]
            v = v[:, :Lq]
        qt = jnp.transpose(q, (0, 2, 3, 1))
        kt = jnp.transpose(k, (0, 2, 3, 1))
        vt = jnp.transpose(v, (0, 2, 3, 1))
        qf = jnp.fft.rfft(qt)
        kf = jnp.fft.rfft(kt)
        c = qf.real * kf.real + 1j * -(qf.imag * kf.imag)
        corr = jnp.fft.irfft(c, n=Lq).astype(qt.dtype)
        agg = _time_delay_agg_inference(vt, corr)
        out = jnp.transpose(agg, (0, 3, 1, 2)).reshape(B, Lq, H * DK)
        return out @ Wo + bo

    def _L0_ffn_ref(x, wqkv, q_scale, k_scale, wo, ln_g, ln_b, w1, b1, w2, b2):
        import jax, jax.numpy as jnp
        import numpy as np
        DIM = 128
        DEPTH = 2
        HEADS = 8
        DIM_HEAD = 64
        WINDOW = 64
        INNER = HEADS * DIM_HEAD
        HID = int(DIM * 4 * 2 / 3)
        B, N = (2, 1024)
        QK_SCALE = 8.0

        def shift_token(t):
            t1, t2 = jnp.split(t, 2, axis=-1)
            t2 = jnp.pad(t2, ((0, 0), (1, 0), (0, 0)))[:, :-1]
            return jnp.concatenate([t1, t2], axis=-1)

        def l2norm(t):
            return t / jnp.clip(jnp.linalg.norm(t, axis=-1, keepdims=True), 1e-12)

        def rotate_half(x):
            x1, x2 = jnp.split(x, 2, axis=-1)
            return jnp.concatenate([-x2, x1], axis=-1)

        def rotary_xpos(q, k):
            n = q.shape[-2]
            half_idx = jnp.arange(0, DIM_HEAD, 2, dtype=jnp.float32)
            inv_freq = 1.0 / 10000.0 ** (half_idx / DIM_HEAD)
            t = jnp.arange(n, dtype=jnp.float32)
            freqs = t[:, None] * inv_freq[None, :]
            freqs = jnp.concatenate([freqs, freqs], axis=-1)
            base = (half_idx + 0.4 * DIM_HEAD) / (1.4 * DIM_HEAD)
            power = (t - n // 2) / float(WINDOW // 2)
            scale = base[None, :] ** power[:, None]
            scale = jnp.concatenate([scale, scale], axis=-1)
            cos, sin = (jnp.cos(freqs), jnp.sin(freqs))
            q = q * cos * scale + rotate_half(q) * sin * scale
            k = k * cos / scale + rotate_half(k) * sin / scale
            return (q, k)

        def local_attention(q, k, v):
            b, h, n, d = q.shape
            w = n // WINDOW
            bq = q.reshape(b, h, w, WINDOW, d) * QK_SCALE
            bk = k.reshape(b, h, w, WINDOW, d)
            bv = v.reshape(b, h, w, WINDOW, d)

            def look_around(t):
                p = jnp.pad(t, ((0, 0), (0, 0), (1, 0), (0, 0), (0, 0)))
                return jnp.concatenate([p[:, :, :w], p[:, :, 1:]], axis=3)
            bk, bv = (look_around(bk), look_around(bv))
            bt = jnp.arange(n).reshape(w, WINDOW)
            btp = jnp.pad(bt, ((1, 0), (0, 0)), constant_values=-1)
            btk = jnp.concatenate([btp[:w], btp[1:]], axis=1)
            sim = jnp.einsum('bhwid,bhwjd->bhwij', bq, bk)
            i = bt[:, :, None]
            j = btk[:, None, :]
            mask = (i < j) | (i > j + WINDOW) | (j == -1)
            sim = jnp.where(mask, -jnp.finfo(sim.dtype).max, sim)
            attn = jax.nn.softmax(sim, axis=-1)
            out = jnp.einsum('bhwij,bhwjd->bhwid', attn, bv)
            return out.reshape(b, h, n, d)

        def _layer(x, wqkv, qs, ksc, wo, lg, lb, w1, b1, w2, b2):
            b, n, _ = x.shape
            h = shift_token(x)
            qkv = h @ wqkv
            q, k, v = jnp.split(qkv, 3, axis=-1)
            to_heads = lambda t: t.reshape(b, n, HEADS, DIM_HEAD).transpose(0, 2, 1, 3)
            q, k, v = (to_heads(q), to_heads(k), to_heads(v))
            q = l2norm(q) * qs
            k = l2norm(k) * ksc
            q, k = rotary_xpos(q, k)
            o = local_attention(q, k, v)
            o = o.transpose(0, 2, 1, 3).reshape(b, n, INNER)
            x = x + o @ wo
            h = shift_token(x)
            mu = h.mean(-1, keepdims=True)
            var = h.var(-1, keepdims=True)
            h = (h - mu) / jnp.sqrt(var + 1e-05) * lg + lb
            h = h @ w1 + b1
            a, g = jnp.split(h, 2, axis=-1)
            h = a * jax.nn.gelu(g, approximate=False)
            x = x + h @ w2 + b2
            return x
        for l in range(DEPTH):
            x = _layer(x, wqkv[l], q_scale[l], k_scale[l], wo[l], ln_g[l], ln_b[l], w1[l], b1[l], w2[l], b2[l])
        return x

    def _L1_xattn_ref(char_emb, subword_emb, Wq_c, bq_c, Wk_s, bk_s, Wv_s, bv_s, Wq_s, bq_s, Wk_c, bk_c, Wv_c, bv_c, Wg, bg):
        import jax, jax.numpy as jnp
        import numpy as np
        H = 128
        B = 8
        L_CHAR = 256
        L_SUB = 128

        def _linear(x, W, b):
            return jnp.einsum('blh,oh->blo', x, W) + b

        def _interp_linear(x, out_len):
            L_in = x.shape[1]
            pos = (jnp.arange(out_len, dtype=x.dtype) + 0.5) * (L_in / out_len) - 0.5
            pos = jnp.clip(pos, 0.0, L_in - 1)
            lo = jnp.floor(pos).astype(jnp.int32)
            hi = jnp.minimum(lo + 1, L_in - 1)
            w = (pos - lo.astype(x.dtype))[None, :, None]
            return x[:, lo] * (1 - w) + x[:, hi] * w
        h = char_emb.shape[-1]
        scale = 1.0 / jnp.sqrt(jnp.asarray(h, char_emb.dtype))
        Q_char = _linear(char_emb, Wq_c, bq_c)
        K_sub = _linear(subword_emb, Wk_s, bk_s)
        V_sub = _linear(subword_emb, Wv_s, bv_s)
        scores = jnp.einsum('bqh,bkh->bqk', Q_char, K_sub) * scale
        char2sub = jnp.einsum('bqk,bkh->bqh', jax.nn.softmax(scores, axis=-1), V_sub)
        Q_sub = _linear(subword_emb, Wq_s, bq_s)
        K_char = _linear(char_emb, Wk_c, bk_c)
        V_char = _linear(char_emb, Wv_c, bv_c)
        scores2 = jnp.einsum('bqh,bkh->bqk', Q_sub, K_char) * scale
        sub2char = jnp.einsum('bqk,bkh->bqh', jax.nn.softmax(scores2, axis=-1), V_char)
        L_char = char_emb.shape[1]
        if sub2char.shape[1] != L_char:
            sub2char = _interp_linear(sub2char, L_char)
        gate_in = jnp.concatenate([char2sub, sub2char], axis=-1)
        gate = jax.nn.sigmoid(jnp.einsum('blh,oh->blo', gate_in, Wg) + bg)
        return gate * char2sub + (1 - gate) * sub2char

    def _L1_ffn_ref(x, w1, conv_w, conv_b, w2):
        import jax, jax.numpy as jnp
        import numpy as np
        B, S, D_MODEL, D_HIDDEN = (4, 256, 128, 512)

        def act_quant(x):
            scale = 127.0 / jnp.clip(jnp.max(jnp.abs(x), axis=-1, keepdims=True), 1e-05)
            return jnp.clip(jnp.round(x * scale), -128, 127) / scale

        def weight_quant(w):
            scale = 1.0 / jnp.clip(jnp.mean(jnp.abs(w)), 1e-05)
            return jnp.clip(jnp.round(w * scale), -1, 1) / scale

        def bit_linear(x, w):
            xq = x + jax.lax.stop_gradient(act_quant(x) - x)
            wq = w + jax.lax.stop_gradient(weight_quant(w) - w)
            return jnp.einsum('bsd,hd->bsh', xq, wq)

        def depthwise_conv1d(x_bcl, w, b):
            y = jax.lax.conv_general_dilated(x_bcl, w, window_strides=(1,), padding=[(1, 1)], dimension_numbers=('NCH', 'OIH', 'NCH'), feature_group_count=x_bcl.shape[1])
            return y + b[None, :, None]
        h = bit_linear(x, w1)
        h = depthwise_conv1d(h.transpose(0, 2, 1), conv_w, conv_b)
        h = h.transpose(0, 2, 1)
        h = jax.nn.silu(h)
        return bit_linear(h, w2)
    x = x + _L0_xattn_ref(_layernorm(x, axis=-1), ctx_1024, ctx_1024, L0_xattn_Wq, L0_xattn_bq, L0_xattn_Wk, L0_xattn_bk, L0_xattn_Wv, L0_xattn_bv, L0_xattn_Wo, L0_xattn_bo)
    x = x + _L0_ffn_ref(_layernorm(x, axis=-1), L0_ffn_wqkv, L0_ffn_q_scale, L0_ffn_k_scale, L0_ffn_wo, L0_ffn_ln_g, L0_ffn_ln_b, L0_ffn_w1, L0_ffn_b1, L0_ffn_w2, L0_ffn_b2)
    x = x + _L1_xattn_ref(_layernorm(x, axis=-1), ctx_1024, L1_xattn_Wq_c, L1_xattn_bq_c, L1_xattn_Wk_s, L1_xattn_bk_s, L1_xattn_Wv_s, L1_xattn_bv_s, L1_xattn_Wq_s, L1_xattn_bq_s, L1_xattn_Wk_c, L1_xattn_bk_c, L1_xattn_Wv_c, L1_xattn_bv_c, L1_xattn_Wg, L1_xattn_bg)
    x = x + _L1_ffn_ref(_layernorm(x, axis=-1), L1_ffn_w1, L1_ffn_conv_w, L1_ffn_conv_b, L1_ffn_w2)
    return x

_drawn_inputs = setup_inputs


def setup_inputs(seed=0):
    import zlib

    import numpy as np

    out = dict(_drawn_inputs(seed))
    spreads = {'L0_xattn_bq': (0.0, 2.0),
     'L0_xattn_bk': (0.0, 0.1),
     'L0_xattn_bv': (0.0, 0.1),
     'L0_xattn_bo': (0.0, 0.1),
     'L0_ffn_q_scale': (1.0, 0.6),
     'L0_ffn_k_scale': (1.0, 0.6),
     'L0_ffn_ln_g': (1.0, 0.6),
     'L0_ffn_ln_b': (0.0, 0.8),
     'L0_ffn_b1': (0.0, 0.8),
     'L0_ffn_b2': (0.0, 0.619)}
    factors = {'L0_ffn_w1': 6.396,
     'L0_ffn_w2': 6.272,
     'L1_xattn_Wq_c': 64.0,
     'L1_xattn_bq_c': 64.0,
     'L1_xattn_Wk_s': 64.0,
     'L1_xattn_bk_s': 200.0,
     'L1_xattn_bv_s': 64.0,
     'L1_xattn_Wq_s': 38.295,
     'L1_xattn_bq_s': 64.0,
     'L1_xattn_Wk_c': 37.159,
     'L1_xattn_bk_c': 200.0,
     'L1_xattn_Wv_c': 11.222,
     'L1_xattn_bv_c': 64.0,
     'L1_xattn_Wg': 61.804,
     'L1_xattn_bg': 200.0,
     'L1_xattn_Wv_s': 7.503,
     'L1_ffn_w1': 8.0,
     'L1_ffn_conv_w': 8.0,
     'L1_ffn_conv_b': 8.0,
     'L1_ffn_w2': 8.0}
    for name, (base, spread) in spreads.items():
        noise = np.random.default_rng([zlib.crc32(name.encode()), seed]).standard_normal(out[name].shape)
        drawn = base * np.exp(spread * noise) if base else spread * noise
        out[name] = jnp.asarray(drawn.astype(out[name].dtype))
    for name, factor in factors.items():
        out[name] = (out[name] * factor).astype(out[name].dtype)
    return out
```

```python
from contextlib import ExitStack

import numpy as np

import concourse.bass as bass
from concourse import mybir

F32 = mybir.dt.float32
BF16 = mybir.dt.bfloat16
ALU = mybir.AluOpType
ACT = mybir.ActivationFunctionType
AX = mybir.AxisListType

B, T, D, S = 16, 128, 128, 77
NB = 4
NG = B // NB
LAYERS, HEADS, DH = 2, 8, 64
HALF = HEADS // 2
INNER = HEADS * DH
HID = 341
HT = (128, 128, HID - 256)
DHID = 512
TOPK = int(2 * np.log(T))
MAGIC = 1.5 * 2.0 ** 23
NEG = -1.0e30
LN_EPS = 1e-5
CORR_SCALE = 1.0 / np.sqrt(D)
NBANKS = 8

CONST_COLS = {}


def constant_array():
    t = np.arange(T, dtype=np.float64)
    cols = {}
    cols["ident"] = np.eye(128)
    cosines = np.cos(2 * np.pi * np.outer(t, np.arange(T // 2 + 1)) / T)
    sines = np.sin(2 * np.pi * np.outer(t, np.arange(1, T // 2)) / T)
    dft = np.concatenate([cosines, sines], axis=1)
    cols["dft"] = dft
    weight = np.full(T, 2.0)
    weight[0] = weight[T // 2] = 1.0
    cols["inverse_dft"] = (dft * weight[None, :] / T / D).T
    half = np.arange(0, DH, 2, dtype=np.float64)
    freqs = np.concatenate([np.outer(t, 10000.0 ** (-half / DH))] * 2, axis=1)
    base = (half + 0.4 * DH) / (1.4 * DH)
    scale = base[None, :] ** ((t[:, None] - T // 2) / 32.0)
    scale = np.concatenate([scale, scale], axis=1)
    sign = np.where(np.arange(DH) < DH // 2, -1.0, 1.0)[None, :]
    cols["rope"] = np.concatenate([8 * np.cos(freqs) * scale, 8 * sign * np.sin(freqs) * scale,
                                   np.cos(freqs) / scale, sign * np.sin(freqs) / scale], axis=1)
    i, j = t[:, None], t[None, :]
    cols["mask"] = np.where((i < j) | (i > j + 64), NEG, 0.0)
    pos = np.clip((t + 0.5) * (S / T) - 0.5, 0.0, S - 1)
    lo = np.floor(pos).astype(int)
    hi = np.minimum(lo + 1, S - 1)
    interp = np.zeros((T, T))
    np.add.at(interp, (S - 1 - lo, np.arange(T)), 1 - (pos - lo))
    np.add.at(interp, (S - 1 - hi, np.arange(T)), pos - lo)
    cols["interp"] = interp
    sums = np.zeros((128, 2 * T))
    sums[0, :T] = dft.sum(0)
    sums[0, T:] = dft[:S].sum(0)
    cols["sums"] = sums
    at = 0
    for name, a in cols.items():
        CONST_COLS[name] = (at, at + a.shape[1])
        at += a.shape[1]
    return np.concatenate(list(cols.values()), axis=1).astype(np.float32)


constant_array()
CONST_WIDTH = max(b for _, b in CONST_COLS.values())


WEIGHTS = {"corr_w": 4 * 128, "corr_bv": 1, "lngb": 2 * LAYERS, "b1": LAYERS * 6, "cb": 7,
           "w1": LAYERS * 2 * HID, "q1": DHID, "q2": DHID, "cw": 8 * 128, "wqkv": LAYERS * 3 * INNER,
           "wo": LAYERS * 4 * 128, "w2": LAYERS * 3 * 128}
ROWS = {"bq": 128, "bk": 128, "conv_b": DHID, "bo": 128, "scales": 2 * LAYERS * DH, "conv_w": 3 * DHID}


def places(widths):
    ends = np.cumsum(list(widths.values()))
    return {name: (int(b) - w, int(b)) for (name, w), b in zip(widths.items(), ends)}


WEIGHT_AT, ROW_AT = places(WEIGHTS), places(ROWS)


def weight_array(i):
    a = np.zeros((128, sum(WEIGHTS.values())), np.float32)

    def put(name, at, block):
        at += WEIGHT_AT[name][0]
        a[0:block.shape[0], at:at + block.shape[1]] = block

    for n, w in enumerate((i["L0_xattn_Wq"], i["L0_xattn_Wk"], i["L0_xattn_Wv"].T, i["L0_xattn_Wo"])):
        put("corr_w", n * 128, w)
    put("corr_bv", 0, i["L0_xattn_bv"][:, None])
    put("lngb", 0, i["L0_ffn_ln_g"].T)
    put("lngb", LAYERS, i["L0_ffn_ln_b"].T)
    for l in range(LAYERS):
        for j, rows in enumerate(HT):
            for part in range(2):
                at = part * HID + 128 * j
                put("b1", 6 * l + 3 * part + j, i["L0_ffn_b1"][l, at:at + rows, None])
            put("w2", (3 * l + j) * 128, i["L0_ffn_w2"][l, 128 * j:128 * j + rows])
        a[HT[2], WEIGHT_AT["w2"][0] + (3 * l + 2) * 128:][:128] = i["L0_ffn_b2"][l]
        put("w1", 2 * HID * l, i["L0_ffn_w1"][l])
        put("wqkv", 3 * INNER * l, i["L0_ffn_wqkv"][l])
        for t in range(4):
            put("wo", (4 * l + t) * 128, i["L0_ffn_wo"][l, 128 * t:128 * t + 128])
    cross = ("q_c", "k_s", "v_s", "q_s", "k_c", "v_c", "g")
    for n, name in enumerate(cross):
        w = i["L1_xattn_W" + name]
        for m in range(w.shape[1] // 128):
            put("cw", (n + m) * 128, w[:, 128 * m:128 * m + 128].T)
        put("cb", n, i["L1_xattn_b" + name][:, None])
    put("q1", 0, i["L1_ffn_w1"].T)
    for t in range(4):
        put("q2", 128 * t, i["L1_ffn_w2"][:, 128 * t:128 * t + 128].T)
    return a


def row_array(i):
    return np.concatenate([i["L0_xattn_bq"], i["L0_xattn_bk"], i["L1_ffn_conv_b"], i["L0_xattn_bo"],
                           i["L0_ffn_q_scale"].reshape(-1), i["L0_ffn_k_scale"].reshape(-1),
                           i["L1_ffn_conv_w"][:, 0, :].T.reshape(-1)])[None, :]


class Signal:

    def __init__(self, sem, per_group, step=1):
        self.sem, self.per_group, self.step = sem, per_group * step, step

    def raised_by(self, ins):
        ins.then_inc(self.sem, self.step)
        return ins

    def wait(self, eng, g, n):
        eng.wait_ge(self.sem, g * self.per_group + n * self.step)


class Chain(Signal):

    def __init__(self, sem, per_group):
        super().__init__(sem, per_group)
        self.n = 0

    def link(self, eng, g, ins):
        self.n += 1
        self.raised_by(ins)
        self.wait(eng, g, self.n)


def psum_order():
    order = ["vprime", "agg"]
    for l in range(LAYERS):
        order.append(("yT", l))

        def qkv(b):
            return [("q", l, b), ("k", l, b), ("v", l, b)] if b < NB else []

        def turn(b):
            return [("qT", l, b), ("kT", l, b)] if b < NB else []

        order += qkv(0) + qkv(1) + turn(0)
        for b in range(NB):
            order += [("sim", l, b, 0), ("sim", l, b, 1)] + qkv(b + 2) + [("pT", l, b, 0), ("pT", l, b, 1)]
            if b:
                order.append(("oT", l, b - 1))
            order.append(("o", l, b, 0))
            if b:
                order.append(("wo", l, b - 1))
            order.append(("o", l, b, 1))
            order += turn(b + 1)
        order += [("oT", l, NB - 1), ("wo", l, NB - 1), ("hT", l)]
        for j in range(3):
            order += [("gate", l, j), ("up", l, j)]
        order.append(("down", l))
    order += ["zT", "qc", "ks", "vs", "qs", "kc", "vc", "s1", "s2", "p1T", "c2s", "a", "s2c", "g", "mixT", "dT"]
    for b in range(NB):
        order.append(("h", b))
        if b:
            order.append(("hqT", b - 1))
    order += [("hqT", NB - 1), "ffn"]
    return order


class Banks:

    def __init__(self, tensors, filled, freed):
        self.tensors, self.filled, self.freed = tensors, filled, freed
        self.at = {name: n for n, name in enumerate(psum_order())}
        self.uses = [len(range(k, len(self.at), NBANKS)) for k in range(NBANKS)]

    def __getitem__(self, name):
        return self.tensors[self.at[name] % NBANKS]

    def wait_free(self, pe, g, name):
        k, n = self.at[name] % NBANKS, self.at[name] // NBANKS
        pe.wait_ge(self.freed[k], g * self.uses[k] + n + 1)

    def fills(self, name, ins):
        ins.then_inc(self.filled[self.at[name] % NBANKS], 1)

    def wait_read(self, eng, g, name):
        k, n = self.at[name] % NBANKS, self.at[name] // NBANKS
        eng.wait_ge(self.freed[k], g * self.uses[k] + n + 2)

    def wait_filled(self, eng, g, name):
        k, n = self.at[name] % NBANKS, self.at[name] // NBANKS
        eng.wait_ge(self.filled[k], g * self.uses[k] + n + 1)

    def frees(self, name, ins):
        ins.then_inc(self.freed[self.at[name] % NBANKS], 1)


def xattn_ffn_stack_kernel(nc, x, ctx_in, ctxT_in, consts, weights, rows_in, out):
    stack = ExitStack()
    with stack:
        def sb(name, shape, dt=F32):
            return stack.enter_context(nc.sbuf_tensor(name, shape, dt))

        def sem(name):
            return stack.enter_context(nc.semaphore(name))

        cst = sb("cst", [128, CONST_WIDTH])

        def const(name, rows=128):
            a, b = CONST_COLS[name]
            return cst[0:rows, a:b]

        ident = const("ident")
        ident_b = sb("ident_b", [128, 128], BF16)
        mask_b = sb("mask_b", [128, HALF, 128], BF16)
        ones = sb("ones", [128, 128])
        first = WEIGHT_AT["q2"][1]
        late = sb("late_weights", [128, sum(WEIGHTS.values()) - first])
        early = sb("early_weights", [128, WEIGHT_AT["cb"][1]])

        def weight(name):
            a, b = WEIGHT_AT[name]
            return early[:, a:b] if b <= WEIGHT_AT["cb"][1] else late[:, a - first:b - first]

        corr_w = weight("corr_w").rearrange("p (n o) -> p n o", n=4)
        corr_bv = weight("corr_bv")
        lngb = weight("lngb").rearrange("p (a l) -> p a l", a=2)
        b1 = weight("b1").rearrange("p (l a j) -> p l a j", l=LAYERS, a=2)
        cb = weight("cb")
        cw = weight("cw").rearrange("p (n o) -> p n o", n=8)
        wqkv = weight("wqkv").rearrange("p (l f) -> p l f", l=LAYERS)
        wo = weight("wo").rearrange("p (l a d) -> p l a d", l=LAYERS, a=4)
        w2 = weight("w2").rearrange("p (l a d) -> p l a d", l=LAYERS, a=3)
        corr_rows = sb("corr_rows", [1, 2, 128])
        bv_cols = sb("bv_cols", [128, S])
        wvo = sb("wvo", [128, 128])
        bvo = sb("bvo", [S, 128])
        bias_f = sb("bias_f", [128, 2, 128])
        scales = sb("scales", [128, 2, LAYERS, DH])
        rope = sb("rope", [128, LAYERS, 2, 2, DH])
        w1g = sb("w1g", [128, LAYERS, 2 * HID])
        cbs = sb("cbs", [128, 3])
        qsum = sb("qsum", [128, 2])
        qscale = sb("qscale", [128, 6])
        conv_b = sb("conv_b", [1, DHID])
        conv_tmp = sb("conv_tmp", [1, 2, DHID])
        conv_parts = sb("conv_parts", [1, 3, DHID], BF16)
        conv_b3 = sb("conv_b3", [3, DHID], BF16)
        ones3 = sb("ones3", [3, 128], BF16)
        wc = sb("wc", [128, 3, DHID])
        q2T = sb("q2T", [128, 4, 128], BF16)

        spec = sb("spec", [128, B])
        corr = sb("corr", [B, 128])
        left = sb("left", [B, 2, 128])
        top8 = sb("top8", [B, 3, 8])
        corr_e = sb("corr_e", [B, 2, 128])
        corr_s = sb("corr_s", [B, 4])
        delay_w = sb("delay_w", [B, 2, 128])

        x0 = sb("x0", [128, NB, 128])
        ctx = sb("ctx", [S, NB, 128])
        hank = sb("hank", [S + 1, NB, 128])
        ctxT = sb("ctxT", [128, NB, S])
        vprime = sb("vprime", [S + 1, NB, 128])
        x1 = sb("x1", [128, NB, 128])
        x2 = sb("x2", [128, NB, 128])
        x3 = sb("x3", [128, NB, 128])
        x4 = sb("x4", [128, NB, 128])
        xn = sb("xn", [128, NB, 128])
        y0 = sb("y0", [128, NB, 128])
        y1 = sb("y1", [128, NB, 128])
        hs = sb("hs", [128, NB, 128])
        stats = sb("stats", [128, NB, 6])
        meanvar = sb("meanvar", [128, NB, 2])
        pause = sb("pause", [128, 1])
        vareps = sb("vareps", [128, NB])
        rstd = sb("rstd", [128, NB])
        minus_half = sb("minus_half", [128, 2 * HEADS])
        yT = sb("yT", [128, NB, 128])
        sq = sb("sq", [128, 2, 2, INNER])
        ssq = sb("ssq", [128, 2, 2 * HEADS])
        ssqc = sb("ssqc", [128, 2, 2 * HEADS])
        rnorm = sb("rnorm", [128, 2, 2 * HEADS])
        t_cos = sb("t_cos", [128, 2, 2, INNER])
        t_sin = sb("t_sin", [128, 2, 2, INNER])
        t_sum = sb("t_sum", [128, 2 * INNER])
        qk = sb("qk", [128, 2, 2, INNER])
        vx = sb("vx", [128, NB, HEADS, DH + 1])
        qT = sb("qT", [128, 2, 4, 128])
        kT = sb("kT", [128, 2, 4, 128])
        nmax = sb("nmax", [128, 2, HEADS])
        prob = sb("prob", [128, 2, 2, HALF, 128])
        probT = sb("probT", [128, 2, HALF, 128])
        rsum = sb("rsum", [128, 2, HEADS])
        o = sb("o", [128, 2, HEADS, DH])
        oT = sb("oT", [128, 2, 4, 128])
        gel = sb("gel", [128, 3, NB * 128])
        hid = sb("hid", [128, 3, NB * 128])
        zT = sb("zT", [128, NB, 128])
        nm1 = sb("nm1", [128, 4, NB])
        amax = sb("amax", [128, 4, NB])
        ydT = sb("ydT", [128, NB, 130])
        silb = sb("silb", [128, 2, DHID], BF16)
        silT = sb("silT", [128, NB, 4, 128], BF16)
        amax2 = sb("amax2", [128, 4, NB])

        def within(tensor, at, shape, dt=F32):
            letters = "abcd"[:len(tensor.shape) - 1]
            flat = tensor[:, :] if len(tensor.shape) == 2 else \
                tensor[tuple([slice(None)] * len(tensor.shape))].rearrange(
                    f"p {' '.join(letters)} -> p ({' '.join(letters)})")
            size = int(np.prod(shape[1:]))
            flat = flat[0:shape[0], at:at + size]
            if len(shape) == 2:
                return flat
            letters = "abcd"[:len(shape) - 1]
            return flat.rearrange(f"p ({' '.join(letters)}) -> p {' '.join(letters)}",
                                  **{c: n for c, n in zip(letters, shape[1:])})

        conv_w = within(sq, 0, [128, 3, DHID])
        w1 = within(t_cos, 0, [128, LAYERS, 2 * HID])
        q1 = within(t_sin, 0, [128, DHID])
        q2 = within(t_sin, DHID, [128, DHID])
        spec_t = within(gel, 0, [128, 2, NB, 128])
        spec_q = within(prob, 0, [128, NB, 128])
        spec_k = within(prob, 512, [128, NB, 128])
        spec_junk = within(prob, 1024, [128, NB, 128])
        qcT, kcT, vc, aT = (within(qk, 512 * n, [128, NB, 128]) for n in range(4))
        c2sT, s2cT, gt = (within(prob, 512 * n, [128, NB, 128]) for n in range(3))
        mix = within(t_sum, 0, [128, 2, NB, 128])
        ksT, qsT = (within(qT, 512 * n, [128, NB, S]) for n in range(2))
        p1 = within(kT, 0, [128, NB, S])
        vs = within(kT, 512, [S, NB, 128])
        p1T, p2 = (within(probT, 512 * n, [S, NB, 128]) for n in range(2))
        yq, yd = (within(o, 512 * n, [128, NB, 128]) for n in range(2))
        sil = within(gel, 0, [128, 2, DHID])
        silq = within(oT, 0, [128, 2, DHID])

        psum = [stack.enter_context(nc.psum_tensor(f"bank{k}", [128, 512], F32)) for k in range(NBANKS)]
        banks = Banks(psum, [sem(f"bank{k}_filled") for k in range(NBANKS)],
                      [sem(f"bank{k}_freed") for k in range(NBANKS)])
        delays = nc.dram_tensor("delay_weights", [B, 2 * 128], F32, kind="Internal").ap()

        w_loaded = sem("weights_loaded")
        c_loaded = sem("constants_loaded")
        conv_loaded = sem("conv_bias_parts_loaded")
        pool_set = sem("pool_constants_set")
        prep_pe = sem("prep_products_ready")
        prep_dve = Chain(sem("prep_vector_steps"), 0)
        prep_act = sem("prep_scalar_steps")
        f_loaded = sem("search_inputs_loaded")
        f_var = sem("search_variance_ready")
        f_rstd = sem("search_rstd_ready")
        f_norm = sem("search_tokens_normalised")
        f_spec = sem("search_tokens_transformed")
        f_copied = sem("search_transform_copied")
        f_proj = sem("search_projected")
        f_taken = sem("search_projection_taken")
        f_chain = Chain(sem("search_vector_steps"), 4)
        s_spec = sem("spectra_ready")
        s_corr = sem("correlation_ready")
        s_shift = sem("correlation_shift_ready")
        s_exp = sem("delay_exponentials_ready")
        s_delay = sem("delay_weights_ready")
        s_stored = sem("delay_weights_stored")
        x_loaded = Signal(sem("x_loaded"), 1, 16)
        ctx_loaded = Signal(sem("ctx_loaded"), 1, 16)
        hank_loaded = Signal(sem("hankel_loaded"), 1, 16)
        var_ready = Signal(sem("variance_ready"), 3 + LAYERS)
        rstd_ready = Signal(sem("rstd_ready"), 3 + LAYERS)
        y_ready = Signal(sem("stack_input_ready"), 1)
        sq_ready = Signal(sem("squares_ready"), 2 * NB * LAYERS)
        ssq_ready = Signal(sem("square_sums_ready"), NB * LAYERS)
        qk_ready = Signal(sem("qk_ready"), NB * LAYERS)
        nmax_ready = Signal(sem("score_max_ready"), 2 * NB * LAYERS)
        shifted = [Signal(sem(f"shifted{b}"), 2 * LAYERS, 16) for b in range(NB)]
        hn_ready = Signal(sem("hn_ready"), LAYERS)
        x2_ready = Signal(sem("x2_ready"), 1)
        z_ready = Signal(sem("z_ready"), 1)
        cmax_ready = Signal(sem("cross_max_ready"), 2)
        cprob_ready = Signal(sem("cross_prob_ready"), 2)
        diff_ready = Signal(sem("cross_difference_ready"), 1)
        mix_ready = Signal(sem("mix_ready"), 1)
        yd_ready = Signal(sem("quantised_input_ready"), 1)
        silq_ready = Signal(sem("quantised_hidden_ready"), NB)
        x4_stored = Signal(sem("x4_stored"), 1, 16)
        steps = Chain(sem("vector_steps"), VECTOR_STEPS)
        pool_steps = Chain(sem("pool_steps"), POOL_STEPS)

        block = stack.enter_context(nc.Block())
        weight_loads = [0]
        prep_steps = []

        @block.sync
        def _(sp):
            def load(dst, src):
                sp.dma_start(dst, src).then_inc(w_loaded, 16)
                weight_loads[0] += 1

            sp.dma_start(cst[:, :], consts).then_inc(c_loaded, 16)
            def packed(name, last=None):
                return weights[:, WEIGHT_AT[name][0]:WEIGHT_AT[last or name][1]]

            def row(name):
                return rows_in[:, ROW_AT[name][0]:ROW_AT[name][1]]

            load(early[:, :], packed("corr_w", "cb"))
            load(corr_rows[:, :, :].rearrange("p a n -> p (a n)"), rows_in[:, 0:256])
            load(scales[:, :, :, :].rearrange("p a l d -> p (a l d)"), row("scales")[0].partition_broadcast(128))
            load(w1.rearrange("p l f -> p (l f)"), packed("w1"))
            load(q1, packed("q1"))
            load(q2, packed("q2"))
            load(conv_w.rearrange("p k c -> p (k c)"), row("conv_w")[0].partition_broadcast(128))
            load(conv_b[:, :], row("conv_b"))
            for b in range(NB):
                load(vprime[S:S + 1, b, :], row("bo"))
            load(late[:, :], packed("cw", "w2"))

            with sp.Fori(0, NG) as g:
                sp.wait_ge(f_spec, g + 1)
                sp.dma_start(x0[:, :, :], x.rearrange("(g b) t d -> g t b d", b=NB)[g]).then_inc(f_loaded, 16)
                sp.dma_start(ctx[:, :, :], ctx_in.rearrange("(g b) t d -> g t b d", b=NB)[g]).then_inc(f_loaded, 16)
            sp.wait_ge(s_delay, 1)
            sp.dma_start(delays, delay_w[:, :, :].rearrange("b a t -> b (a t)")).then_inc(s_stored, 16)
            sp.wait_ge(s_stored, 16)

            def load_tokens(g):
                at_x, at_w = g[0], g[1]
                x_loaded.raised_by(sp.dma_start(
                    x0[:, :, :], bass.AP(x.tensor, at_x, [[D, T], [T * D, NB], [1, D]])))
                hank_loaded.raised_by(sp.dma_start(
                    hank[0:S, :, :], bass.AP(delays.tensor, at_w, [[1, S], [2 * T, NB], [1, T]])))

            def load_context(g):
                ctx_loaded.raised_by(sp.dma_start(
                    ctxT[:, :, :], bass.AP(ctxT_in.tensor, g[2], [[B * S, D], [S, NB], [1, S]])))

            def addresses(g, hold=lambda v: v):
                return hold(g * (NB * T * D)), hold(g * (NB * 2 * T) + T - S), hold(g * (NB * S))

            def turn(g, more):
                hold = sp.snap if more else (lambda v: v)
                here = addresses(g, hold)
                if more:
                    ahead = addresses(g + 1, hold)
                    banks.wait_read(sp, g, "agg")
                    load_tokens(ahead)
                for l in range(LAYERS):
                    for b in range(NB):
                        banks.wait_read(sp, g, ("wo", l, b))
                        shifted[b].raised_by(sp.dma_start(hs[:, b, 0:64], y1[:, b, 0:64]))
                        shifted[b].raised_by(sp.dma_start(hs[1:128, b, 64:128], y1[0:127, b, 64:128]))
                if more:
                    banks.wait_read(sp, g, "qs")
                    load_context(ahead)
                banks.wait_read(sp, g, "ffn")
                x4_stored.raised_by(sp.dma_start(
                    bass.AP(out.tensor, here[0], [[D, T], [T * D, NB], [1, D]]), x4[:, :, :]))

            load_tokens(addresses(0))
            load_context(addresses(0))
            with sp.Fori(0, NG - 1) as g:
                turn(g, True)
            turn(NG - 1, False)
            sp.wait_ge(x4_stored.sem, 16 * (NG + 1))

        @block.gpsimd
        def _(pool):
            for k in range(NBANKS):
                pool.sem_inc(banks.freed[k], 1)
            pool.sem_inc(f_spec, 1)
            pool.sem_inc(s_spec, 1)
            pool.sem_inc(x4_stored.sem, 16)
            pool.memset(minus_half[:, :], -0.5)
            pool.memset(ones[:, :], 1.0)
            pool.memset(ones3[:, :], 1.0)
            pool.memset(hank[:, :, :], 1.0)
            pool.memset(vx[:, :, :, :], 1.0)
            pool.memset(hid[:, 2, :], 1.0)
            pool.memset(yT[:, :, :], 0.0)
            pool.memset(hs[:, :, :], 0.0)
            pool.memset(ydT[:, :, :], 0.0).then_inc(pool_set, 1)

            def power(src, dst, raised, target):
                n = src.shape[1]
                return pool.tensor_tensor(dst, src, minus_half[:, 0:n], ALU.pow)

            pool.wait_ge(pool_set, 1)
            with pool.Fori(0, NG) as g:
                pool.wait_ge(f_var, g + 1)
                pool.tensor_tensor(rstd[:, :], vareps[:, :], minus_half[:, 0:NB], ALU.pow).then_inc(f_rstd, 1)

            with pool.Fori(0, NG) as g:
                def ln(n):
                    var_ready.wait(pool, g, n)
                    rstd_ready.raised_by(
                        pool.tensor_tensor(rstd[:, :], vareps[:, :], minus_half[:, 0:NB], ALU.pow))

                ln(1)
                for l in range(LAYERS):
                    for b in range(NB):
                        n, p = l * NB + b + 1, b % 2
                        ssq_ready.wait(pool, g, n)
                        pool_steps.link(pool, g, pool.tensor_tensor(
                            rnorm[:, p, :], ssqc[:, p, :], minus_half[:, :], ALU.pow))
                        banks.wait_read(pool, g, ("k", l, b))
                        pool_steps.link(pool, g, pool.tensor_tensor(
                            t_sum[:, :], t_cos[:, p, :, :].rearrange("p a f -> p (a f)"),
                            t_sin[:, p, :, :].rearrange("p a f -> p (a f)"), ALU.add))
                        if b >= 2:
                            banks.wait_read(pool, g, ("kT", l, b - 2))
                        qk_ready.raised_by(pool.tensor_tensor(
                            qk[:, p, :, :].rearrange("p a (h d) -> p (a h) d", h=HEADS),
                            t_sum[:, :].rearrange("p (h d) -> p h d", d=DH),
                            rnorm[:, p, :].unsqueeze(2).to_broadcast([128, 2 * HEADS, DH]), ALU.mult))
                    ln(2 + l)
                ln(2 + LAYERS)
                banks.wait_read(pool, g, "s2c")
                diff_ready.raised_by(pool.tensor_tensor(mix[:, 0, :, :], c2sT[:, :, :], s2cT[:, :, :],
                                                        ALU.subtract))
                ln(3 + LAYERS)
            assert pool_steps.n == POOL_STEPS, pool_steps.n

        @block.vector
        def _(dve):
            def link0(ins):
                prep_dve.n += 1
                ins.then_inc(prep_dve.sem, 1)
                dve.wait_ge(prep_dve.sem, prep_dve.n)

            dve.wait_ge(c_loaded, 16)
            dve.wait_ge(w_loaded, 16 * weight_loads[0])
            dve.wait_ge(pool_set, 1)
            dve.tensor_copy(ident_b[:, :], ident)
            dve.tensor_copy(mask_b[:, :, :], const("mask").unsqueeze(1).to_broadcast([128, HALF, 128]))
            dve.tensor_copy(bv_cols[:, :], corr_bv[:, 0:1].to_broadcast([128, S]))
            table = const("rope").rearrange("p (a c d) -> p a c d", a=2, c=2)
            for l in range(LAYERS):
                for part in range(2):
                    dve.tensor_tensor(rope[:, l, part, 0, :], table[:, part, 0, :], scales[:, part, l, :],
                                      ALU.mult)
                    dve.tensor_tensor(
                        rope[:, l, part, 1, :].rearrange("p (c d) -> p c d", c=2),
                        table[:, part, 1, :].rearrange("p (c d) -> p c d", c=2),
                        scales[:, part, l, :].rearrange("p (c d) -> p c d", c=2)[:, ::-1, :], ALU.mult)
                dve.tensor_scalar(w1g[:, l, :], w1[:, l, :], lngb[:, 0, l:l + 1], None, ALU.mult)
            dve.tensor_scalar(cbs[:, 0:1], cb[:, 0:1], CORR_SCALE, None, ALU.mult)
            dve.tensor_scalar(cbs[:, 1:2], cb[:, 3:4], CORR_SCALE, None, ALU.mult)
            dve.tensor_scalar(cbs[:, 2:3], cb[:, 6:7], 0.5, None, ALU.mult)
            link0(dve.tensor_copy(conv_parts[:, 0, :], conv_b[:, :]))
            link0(dve.tensor_tensor(conv_tmp[:, 0, :], conv_b[:, :], conv_parts[:, 0, :], ALU.subtract))
            link0(dve.tensor_copy(conv_parts[:, 1, :], conv_tmp[:, 0, :]))
            link0(dve.tensor_tensor(conv_tmp[:, 1, :], conv_tmp[:, 0, :], conv_parts[:, 1, :], ALU.subtract))
            link0(dve.tensor_copy(conv_parts[:, 2, :], conv_tmp[:, 1, :]))
            for n, w in enumerate((q1, q2)):
                last = dve.tensor_reduce(qsum[:, n:n + 1], w, AX.X,
                                         ALU.add, apply_absolute_value=True)
            link0(last)
            dve.wait_ge(prep_pe, 1)
            link0(dve.tensor_scalar(qscale[:, 0:2], psum[0][:, 0:2], 1.0 / (DHID * D), 1e-5, ALU.mult, ALU.max))
            link0(dve.reciprocal(qscale[:, 2:4], qscale[:, 0:2]))
            for n, w in enumerate((q1, q2)):
                link0(dve.tensor_scalar(w, w, qscale[:, 2 + n:3 + n], MAGIC, ALU.mult, ALU.add))
                link0(dve.tensor_scalar(w, w, MAGIC, 1.0, ALU.subtract, ALU.min))
            link0(dve.tensor_scalar(q1, q1, -1.0, None, ALU.max))
            dve.tensor_scalar(q2T[:, :, :].rearrange("p a o -> p (a o)"), q2, -1.0, None, ALU.max)
            dve.tensor_scalar(qscale[:, 4:5], qscale[:, 1:2], 1.0 / 127.0, None, ALU.mult)
            link0(dve.tensor_scalar(conv_w, conv_w, qscale[:, 0:1], None, ALU.mult))
            for k in range(3):
                dve.tensor_tensor(wc[:, k, :], q1, conv_w[:, k, :], ALU.mult)
            dve.wait_ge(prep_pe, 2)
            dve.tensor_copy(bias_f[:, :, :].rearrange("p a o -> p (a o)"), psum[6][:, 0:256])
            for l in range(LAYERS):
                for part in range(2):
                    at = 6 * l + 3 * part
                    dve.tensor_tensor(b1[:, l, part, 0:2], b1[:, l, part, 0:2],
                                      psum[7][:, at:at + 2], ALU.add)
                    last = dve.tensor_tensor(b1[0:HT[2], l, part, 2:3], b1[0:HT[2], l, part, 2:3],
                                             psum[7][0:HT[2], at + 2:at + 3], ALU.add)
            link0(last)
            dve.tensor_copy(wvo[:, :], psum[3][:, 0:128])
            link0(dve.tensor_copy(bvo[:, :], psum[3][0:S, 128:256]))
            prep_steps.append(prep_dve.n)

            with dve.Fori(0, NG) as g:
                f_chain.n = 0
                dve.wait_ge(f_loaded, g * 32 + 32)
                for b in range(NB):
                    last = dve.bn_stats(stats[:, b, :], x0[:, b, :])
                f_chain.link(dve, g, last)
                dve.memset(pause[:, :], 0.0)
                for b in range(NB):
                    last = dve.bn_aggr(meanvar[:, b, :], stats[:, b, :])
                f_chain.link(dve, g, last)
                dve.tensor_scalar(vareps[:, :], meanvar[:, :, 1], LN_EPS, None, ALU.add).then_inc(f_var, 1)
                dve.wait_ge(f_rstd, g + 1)
                for b in range(NB):
                    last = dve.tensor_scalar(xn[:, b, :], x0[:, b, :], meanvar[:, b, 0:1], rstd[:, b:b + 1],
                                             ALU.subtract, ALU.mult)
                last.then_inc(f_norm, 1)
                dve.wait_ge(f_proj, g + 1)
                dve.tensor_tensor(spec_q[:, :, :], psum[2][:, :].rearrange("p (b c) -> p b c", b=NB),
                                  bias_f[:, 0, :].unsqueeze(1).to_broadcast([128, NB, 128]), ALU.add)
                f_chain.link(dve, g, dve.tensor_tensor(
                    spec_k[:, :, :], psum[3][:, :].rearrange("p (b c) -> p b c", b=NB),
                    bias_f[:, 1, :].unsqueeze(1).to_broadcast([128, NB, 128]), ALU.add))
                f_chain.link(dve, g, dve.tensor_tensor(spec_junk[:, :, :], spec_q[:, :, :], spec_k[:, :, :],
                                                       ALU.mult))
                dve.tensor_reduce(spec[:, bass.ds(g * NB, NB)], spec_junk[:, :, :], AX.X,
                                  ALU.add).then_inc(s_spec, 1)
            dve.wait_ge(s_corr, 1)
            link0(dve.tensor_copy(corr[:, :], psum[0][0:B, 0:128]))
            link0(dve.max(top8[:, 0, :], corr[:, :]))
            link0(dve.match_replace(left[:, 0, :], top8[:, 0, :], corr[:, :], -3.0e38))
            link0(dve.max(top8[:, 1, :], left[:, 0, :]))
            link0(dve.memset(top8[:, 2, :], -3.0e38))
            link0(dve.tensor_copy(top8[:, 2, 0:TOPK - 8], top8[:, 1, 0:TOPK - 8]))
            link0(dve.match_replace(left[:, 1, :], top8[:, 2, :], left[:, 0, :], -3.0e38))
            dve.tensor_scalar(corr_s[:, 0:1], top8[:, 0, 0:1], -1.0, None, ALU.mult).then_inc(s_shift, 1)
            dve.wait_ge(s_exp, 1)
            link0(dve.scalar_tensor_tensor(corr_e[:, 1, :], left[:, 1, :], -2.9e38, corr_e[:, 0, :],
                                           ALU.is_le, ALU.mult))
            link0(dve.tensor_reduce(corr_s[:, 1:2], corr_e[:, 1, :], AX.X, ALU.add))
            link0(dve.reciprocal(corr_s[:, 2:3], corr_s[:, 1:2]))
            dve.tensor_scalar(delay_w[:, :, :], corr_e[:, 1, ::-1].unsqueeze(1).to_broadcast([B, 2, 128]),
                              corr_s[:, 2:3], None, ALU.mult).then_inc(s_delay, 1)

            with dve.Fori(0, NG) as g:
                def norm(n, src, dst, raised):
                    for b in range(NB):
                        last = dve.bn_stats(stats[:, b, :], src[:, b, :])
                    steps.link(dve, g, last)
                    dve.memset(pause[:, :], 0.0)
                    for b in range(NB):
                        last = dve.bn_aggr(meanvar[:, b, :], stats[:, b, :])
                    steps.link(dve, g, last)
                    var_ready.raised_by(
                        dve.tensor_scalar(vareps[:, :], meanvar[:, :, 1], LN_EPS, None, ALU.add))
                    rstd_ready.wait(dve, g, n)
                    for b in range(NB):
                        last = dve.tensor_scalar(dst[:, b, :], src[:, b, :], meanvar[:, b, 0:1],
                                                 rstd[:, b:b + 1], ALU.subtract, ALU.mult)
                    raised.raised_by(last)

                banks.wait_filled(dve, g, "vprime")
                u = banks["vprime"]
                ins = dve.tensor_tensor(vprime[0:S, :, :], u[0:S, :].rearrange("p (b e) -> p b e", b=NB),
                                        bvo[:, :].unsqueeze(1).to_broadcast([S, NB, 128]), ALU.add)
                banks.frees("vprime", ins)
                banks.wait_filled(dve, g, "agg")
                x_loaded.wait(dve, g, 1)
                ins = dve.tensor_tensor(x1[:, :, :].rearrange("p b d -> p (b d)"), banks["agg"][:, :],
                                        x0[:, :, :].rearrange("p b d -> p (b d)"), ALU.add)
                banks.frees("agg", ins)
                banks.wait_read(dve, g, "agg")
                norm(1, x1, y0, y_ready)

                for l in range(LAYERS):
                    def rotary(b):
                        if b >= NB:
                            return
                        n, p = l * NB + b, b % 2
                        sq_ready.wait(dve, g, 2 * n + 2)
                        steps.link(dve, g, dve.tensor_reduce(
                            ssq[:, p, :], sq[:, p, :, :].rearrange("p a (h d) -> p (a h) d", h=HEADS),
                            AX.X, ALU.add))
                        ssq_ready.raised_by(dve.tensor_scalar(ssqc[:, p, :], ssq[:, p, :], 1e-24, None, ALU.max))
                        if b >= 2:
                            qk_ready.wait(dve, g, n - 1)
                        for part, name in enumerate(("q", "k")):
                            u = banks[(name, l, b)]
                            cos = rope[:, l, part, 0, :].unsqueeze(1).to_broadcast([128, HEADS, DH])
                            sin = rope[:, l, part, 1, :].rearrange("p (c d) -> p c d", c=2)\
                                .unsqueeze(1).to_broadcast([128, HEADS, 2, DH // 2])
                            dve.tensor_tensor(t_cos[:, p, part, :].rearrange("p (h d) -> p h d", d=DH),
                                              u[:, :].rearrange("p (h d) -> p h d", d=DH), cos, ALU.mult)
                            ins = dve.tensor_tensor(
                                t_sin[:, p, part, :].rearrange("p (h c d) -> p h c d", c=2, d=DH // 2),
                                u[:, :].rearrange("p (h c d) -> p h c d", c=2, d=DH // 2)[:, :, ::-1, :],
                                sin, ALU.mult)
                            banks.frees((name, l, b), ins)

                    def attended(b):
                        banks.wait_filled(dve, g, ("wo", l, b))
                        ins = dve.tensor_tensor(y1[:, b, :], banks[("wo", l, b)][:, 0:128], y0[:, b, :], ALU.add)
                        banks.frees(("wo", l, b), ins)

                    rotary(0)
                    rotary(1)
                    for b in range(NB):
                        n, p = l * NB + b, b % 2
                        for s in range(2):
                            banks.wait_filled(dve, g, ("sim", l, b, s))
                            nmax_ready.raised_by(dve.tensor_reduce(
                                nmax[:, p, HALF * s:HALF * s + HALF],
                                banks[("sim", l, b, s)][:, :].rearrange("p (h j) -> p h j", h=HALF),
                                AX.X, ALU.max, negate=True))
                        rotary(b + 2)
                        for s in range(2):
                            banks.wait_filled(dve, g, ("o", l, b, s))
                            u = banks[("o", l, b, s)][:, 0:HALF * (DH + 1)].rearrange("p (h d) -> p h d", h=HALF)
                            steps.link(dve, g, dve.reciprocal(rsum[:, p, HALF * s:HALF * s + HALF], u[:, :, DH]))
                            ins = dve.tensor_tensor(
                                o[:, p, s::2, :], u[:, :, 0:DH],
                                rsum[:, p, HALF * s:HALF * s + HALF].unsqueeze(2).to_broadcast([128, HALF, DH]),
                                ALU.mult)
                            banks.frees(("o", l, b, s), ins)
                            if s == 0 and b:
                                attended(b - 1)
                    attended(NB - 1)
                    for b in range(NB):
                        shifted[b].wait(dve, g, 2 * l + 2)
                    norm(2 + l, hs, xn, hn_ready)
                    for j in range(3):
                        rows = HT[j]
                        banks.wait_filled(dve, g, ("up", l, j))
                        banks.wait_read(dve, g, ("gate", l, j))
                        ins = dve.scalar_tensor_tensor(
                            hid[0:rows, j, :], banks[("up", l, j)][0:rows, :], b1[0:rows, l, 0, j:j + 1],
                            gel[0:rows, j, :], ALU.add, ALU.mult)
                        banks.frees(("up", l, j), ins)
                    banks.wait_filled(dve, g, ("down", l))
                    ins = dve.tensor_tensor(y0[:, :, :].rearrange("p b d -> p (b d)"), banks[("down", l)][:, :],
                                            y1[:, :, :].rearrange("p b d -> p (b d)"), ALU.add)
                    banks.frees(("down", l), ins)
                banks.wait_read(dve, g, ("down", LAYERS - 1))
                x2_ready.raised_by(dve.tensor_tensor(x2[:, :, :], x1[:, :, :], y0[:, :, :], ALU.add))
                x2_ready.wait(dve, g, 1)
                norm(2 + LAYERS, x2, xn, z_ready)

                for n, (name, rows, keys) in enumerate((("s1", 128, S), ("s2", S, 128))):
                    banks.wait_filled(dve, g, name)
                    cmax_ready.raised_by(dve.tensor_reduce(
                        nm1[0:rows, n, :],
                        banks[name][0:rows, 0:NB * keys].rearrange("p (b j) -> p b j", b=NB),
                        AX.X, ALU.max, negate=True))
                for n, (p, rows, keys) in enumerate(((p1, 128, S), (p2, S, 128))):
                    banks.wait_read(dve, g, ("s1", "s2")[n])
                    steps.link(dve, g, dve.tensor_reduce(amax[0:rows, 2, :], p[:, :, :], AX.X, ALU.add))
                    steps.link(dve, g, dve.reciprocal(amax[0:rows, 3, :], amax[0:rows, 2, :]))
                    cprob_ready.raised_by(dve.tensor_tensor(
                        p[:, :, :], p[:, :, :],
                        amax[0:rows, 3, :].unsqueeze(2).to_broadcast([rows, NB, keys]), ALU.mult))
                    if n == 0:
                        cprob_ready.wait(dve, g, 1)
                banks.wait_read(dve, g, "g")
                diff_ready.wait(dve, g, 1)
                steps.link(dve, g, dve.scalar_tensor_tensor(mix[:, 1, :, :], gt[:, :, :], 1.0, mix[:, 0, :, :],
                                                            ALU.add, ALU.mult))
                mix_ready.raised_by(dve.scalar_tensor_tensor(gt[:, :, :], mix[:, 1, :, :], 0.5, s2cT[:, :, :],
                                                             ALU.mult, ALU.add))
                banks.wait_filled(dve, g, "mixT")
                ins = dve.tensor_tensor(x3[:, :, :].rearrange("p b d -> p (b d)"), banks["mixT"][:, :],
                                        x2[:, :, :].rearrange("p b d -> p (b d)"), ALU.add)
                banks.frees("mixT", ins)
                banks.wait_read(dve, g, "mixT")

                norm(3 + LAYERS, x3, xn, steps)
                steps.n += 1
                steps.wait(dve, g, steps.n)

                def token_scales(am):
                    steps.link(dve, g, dve.tensor_scalar(am[:, 0, :], am[:, 0, :], 1e-5, None, ALU.max))
                    steps.link(dve, g, dve.reciprocal(am[:, 2, :], am[:, 0, :]))
                    dve.tensor_scalar(am[:, 1, :], am[:, 2, :], 127.0, None, ALU.mult)

                steps.link(dve, g, dve.tensor_reduce(amax[:, 0, :], xn[:, :, :], AX.X, ALU.max,
                                                     apply_absolute_value=True))
                token_scales(amax)
                steps.link(dve, g, dve.tensor_scalar(amax[:, 3, :], amax[:, 0, :], 1.0 / 127.0, None, ALU.mult))
                for b in range(NB):
                    last = dve.tensor_scalar(yq[:, b, :], xn[:, b, :], amax[:, 1, b:b + 1], MAGIC,
                                             ALU.mult, ALU.add)
                steps.link(dve, g, last)
                for b in range(NB):
                    last = dve.tensor_scalar(yd[:, b, :], yq[:, b, :], MAGIC, amax[:, 3, b:b + 1],
                                             ALU.subtract, ALU.mult)
                yd_ready.raised_by(last)
                for b in range(NB):
                    p = b % 2
                    am = amax2[:, :, b:b + 1]
                    banks.wait_read(dve, g, ("h", b))
                    steps.link(dve, g, dve.tensor_reduce(am[:, 0, :], sil[:, p, :], AX.X, ALU.max,
                                                         apply_absolute_value=True))
                    token_scales(am)
                    steps.link(dve, g, dve.tensor_scalar(am[:, 3, :], am[:, 0, :], qscale[:, 4:5], None, ALU.mult))
                    steps.link(dve, g, dve.tensor_scalar(silq[:, p, :], sil[:, p, :], am[:, 1, :], MAGIC,
                                                         ALU.mult, ALU.add))
                    silq_ready.raised_by(dve.tensor_scalar(silb[:, p, :], silq[:, p, :], MAGIC, 127.0,
                                                           ALU.subtract, ALU.min))
                banks.wait_filled(dve, g, "ffn")
                x4_stored.wait(dve, g, 1)
                for b in range(NB):
                    last = dve.scalar_tensor_tensor(x4[:, b, :], banks["ffn"][:, b * 128:b * 128 + 128],
                                                    amax2[:, 3, b:b + 1], x3[:, b, :], ALU.mult, ALU.add)
                banks.frees("ffn", last)
            assert steps.n == VECTOR_STEPS, steps.n

        @block.scalar
        def _(act):
            act.wait_ge(prep_dve.sem, 5)
            for n in range(3):
                act.dma_start(conv_b3[n:n + 1, :], conv_parts[:, n, :]).then_inc(conv_loaded, 16)
            with act.Fori(0, NG) as g:
                act.wait_ge(f_spec, g + 2)
                act.activation(spec_t[:, 0, :, :].rearrange("p b f -> p (b f)"), psum[0][:, :], ACT.Copy)
                act.activation(spec_t[:, 1, :, :].rearrange("p b f -> p (b f)"), psum[1][:, :],
                               ACT.Copy).then_inc(f_copied, 1)
            act.wait_ge(s_shift, 1)
            act.activation(corr_e[:, 0, :], corr[:, :], ACT.Exp, bias=corr_s[:, 0:1]).then_inc(s_exp, 1)

            with act.Fori(0, NG) as g:
                def copy(name, dst, rows=128, cols=512):
                    banks.wait_filled(act, g, name)
                    ins = act.activation(dst, banks[name][0:rows, 0:cols], ACT.Copy)
                    banks.frees(name, ins)

                for l in range(LAYERS):
                    banks.wait_filled(act, g, ("yT", l))
                    u = banks[("yT", l)]
                    act.activation(yT[0:64, :, :].rearrange("p b t -> p (b t)"), u[0:64, :], ACT.Copy)
                    ins = act.activation(yT[64:128, :, 1:T],
                                         u[64:128, :].rearrange("p (b t) -> p b t", b=NB)[:, :, 0:T - 1], ACT.Copy)
                    banks.frees(("yT", l), ins)

                    def squares(b):
                        if b >= NB:
                            return
                        n, p = l * NB + b, b % 2
                        if b >= 2:
                            ssq_ready.wait(act, g, n - 1)
                        for part, name in enumerate(("q", "k")):
                            banks.wait_filled(act, g, (name, l, b))
                            sq_ready.raised_by(act.activation(sq[:, p, part, :], banks[(name, l, b)][:, :],
                                                              ACT.Square))
                        banks.wait_filled(act, g, ("v", l, b))
                        ins = act.activation(vx[:, b, :, 0:DH],
                                             banks[("v", l, b)][:, :].rearrange("p (h d) -> p h d", h=HEADS),
                                             ACT.Copy)
                        banks.frees(("v", l, b), ins)

                    def turned(b):
                        if b >= NB:
                            return
                        copy(("qT", l, b), qT[:, b % 2, :, :].rearrange("p a t -> p (a t)"))
                        copy(("kT", l, b), kT[:, b % 2, :, :].rearrange("p a t -> p (a t)"))

                    def out_turned(b):
                        copy(("oT", l, b), oT[:, b % 2, :, :].rearrange("p a t -> p (a t)"))

                    squares(0)
                    squares(1)
                    turned(0)
                    for b in range(NB):
                        n, p = l * NB + b, b % 2
                        for s in range(2):
                            nmax_ready.wait(act, g, 2 * n + s + 1)
                            for h in range(HALF):
                                ins = act.activation(prob[:, p, s, h, :],
                                                     banks[("sim", l, b, s)][:, h * 128:h * 128 + 128], ACT.Exp,
                                                     bias=nmax[:, p, HALF * s + h:HALF * s + h + 1])
                            banks.frees(("sim", l, b, s), ins)
                        squares(b + 2)
                        for s in range(2):
                            copy(("pT", l, b, s), probT[:, s, :, :].rearrange("p h i -> p (h i)"))
                        if b:
                            out_turned(b - 1)
                        turned(b + 1)
                    out_turned(NB - 1)
                    copy(("hT", l), zT[:, :, :].rearrange("p b t -> p (b t)"))
                    for j in range(3):
                        rows = HT[j]
                        banks.wait_filled(act, g, ("gate", l, j))
                        ins = act.activation(gel[0:rows, j, :], banks[("gate", l, j)][0:rows, :], ACT.Gelu,
                                             bias=b1[0:rows, l, 1, j:j + 1])
                        banks.frees(("gate", l, j), ins)

                copy("zT", zT[:, :, :].rearrange("p b t -> p (b t)"))

                def shifted_copy(name, dst, bias, cols=512, scale=1.0):
                    banks.wait_filled(act, g, name)
                    ins = act.activation(dst.rearrange("p b t -> p (b t)"), banks[name][:, 0:cols], ACT.Identity,
                                         bias=bias, scale=scale)
                    banks.frees(name, ins)

                shifted_copy("qc", qcT[:, :, :], cbs[:, 0:1], scale=CORR_SCALE)
                shifted_copy("ks", ksT[:, :, :], cb[:, 1:2], cols=NB * S)
                copy("vs", vs[:, :, :].rearrange("p b o -> p (b o)"), rows=S)
                shifted_copy("qs", qsT[:, :, :], cbs[:, 1:2], cols=NB * S, scale=CORR_SCALE)
                shifted_copy("kc", kcT[:, :, :], cb[:, 4:5])
                copy("vc", vc[:, :, :].rearrange("p b o -> p (b o)"))
                for n, (name, p, rows, keys) in enumerate((("s1", p1, 128, S), ("s2", p2, S, 128))):
                    cmax_ready.wait(act, g, n + 1)
                    for b in range(NB):
                        ins = act.activation(p[:, b, :], banks[name][0:rows, b * keys:(b + 1) * keys], ACT.Exp,
                                             bias=nm1[0:rows, n, b:b + 1])
                    banks.frees(name, ins)
                copy("p1T", p1T[:, :, :].rearrange("p b t -> p (b t)"), rows=S)
                shifted_copy("c2s", c2sT[:, :, :], cb[:, 2:3])
                copy("a", aT[:, :, :].rearrange("p b t -> p (b t)"))
                shifted_copy("s2c", s2cT[:, :, :], cb[:, 5:6])
                banks.wait_filled(act, g, "g")
                ins = act.activation(gt[:, :, :].rearrange("p b t -> p (b t)"), banks["g"][:, :], ACT.Tanh,
                                     bias=cbs[:, 2:3], scale=0.5)
                banks.frees("g", ins)
                banks.wait_filled(act, g, "dT")
                ins = act.activation(ydT[:, :, 1:T + 1], banks["dT"][:, :].rearrange("p (b t) -> p b t", b=NB),
                                     ACT.Copy)
                banks.frees("dT", ins)

                def hidden_turned(b):
                    banks.wait_filled(act, g, ("hqT", b))
                    ins = act.activation(silT[:, b, :, :].rearrange("p a t -> p (a t)"),
                                         banks[("hqT", b)][:, :].bitcast(BF16)[:, 0:512], ACT.Copy)
                    banks.frees(("hqT", b), ins)

                for b in range(NB):
                    banks.wait_filled(act, g, ("h", b))
                    if b >= 2:
                        silq_ready.wait(act, g, b - 1)
                    ins = act.activation(sil[:, b % 2, :], banks[("h", b)][:, :], ACT.Silu)
                    banks.frees(("h", b), ins)
                    if b:
                        hidden_turned(b - 1)
                hidden_turned(NB - 1)

        @block.tensor
        def _(pe):
            pe.wait_ge(pool_set, 1)
            pe.wait_ge(c_loaded, 16)
            pe.wait_ge(w_loaded, 16 * weight_loads[0])
            pe.wait_ge(prep_dve.sem, 6)
            pe.matmul(psum[0][:, 0:2], ones[:, :], qsum[:, :], start=True, stop=True).then_inc(prep_pe, 1)
            sums = const("sums", 1)
            for n in range(2):
                pe.matmul(psum[6][:, n * 128:n * 128 + 128], sums[:, n * 128:n * 128 + 128],
                          corr_rows[:, n, :], start=True, stop=True)
            for l in range(LAYERS):
                for part in range(2):
                    for j in range(3):
                        at, c = part * HID + j * 128, 6 * l + 3 * part + j
                        ins = pe.matmul(psum[7][0:HT[j], c:c + 1], w1[:, l, at:at + HT[j]], lngb[:, 1, l:l + 1],
                                        start=True, stop=True)
            pe.matmul(psum[3][:, 0:128], corr_w[:, 2, :], corr_w[:, 3, :], start=True, stop=True)
            pe.matmul(psum[3][0:S, 128:256], bv_cols[:, :], corr_w[:, 3, :], start=True,
                      stop=True).then_inc(prep_pe, 1)
            pe.wait_ge(prep_dve.sem, prep_steps[0])

            dft = const("dft")
            with pe.Fori(0, NG) as g:
                pe.wait_ge(f_norm, g + 1)
                for b in range(NB):
                    pe.matmul(psum[0][:, b * 128:b * 128 + 128], xn[:, b, :], dft, start=True, stop=True)
                    ins = pe.matmul(psum[1][:, b * 128:b * 128 + 128], ctx[:, b, :], dft[0:S, :], start=True,
                                    stop=True)
                ins.then_inc(f_spec, 1)
                pe.wait_ge(f_copied, g + 1)
                pe.wait_ge(s_spec, g + 1)
                for b in range(NB):
                    pe.matmul(psum[2][:, b * 128:b * 128 + 128], spec_t[:, 0, b, :], corr_w[:, 0, :], start=True,
                              stop=True)
                    ins = pe.matmul(psum[3][:, b * 128:b * 128 + 128], spec_t[:, 1, b, :], corr_w[:, 1, :],
                                    start=True, stop=True)
                ins.then_inc(f_proj, 1)
            pe.wait_ge(s_spec, NG + 1)
            pe.matmul(psum[0][0:B, 0:128], spec[:, :], const("inverse_dft"), start=True,
                      stop=True).then_inc(s_corr, 1)
            pe.wait_ge(s_delay, 1)
            pe.wait_ge(conv_loaded, 48)

            with pe.Fori(0, NG) as g:
                def turn(name, parts, rows=128, width=128, idn=None, dt=None):
                    banks.wait_free(pe, g, name)
                    u = banks[name] if dt is None else banks[name][:, :].bitcast(dt)
                    for n, part in enumerate(parts):
                        ins = pe.transpose(u[0:rows, n * width:(n + 1) * width], part,
                                           (ident if idn is None else idn)[0:width, 0:width])
                    banks.fills(name, ins)

                def whole(name, pairs, rows=128, cols=512):
                    banks.wait_free(pe, g, name)
                    for n, (lhsT, rhs) in enumerate(pairs):
                        ins = pe.matmul(banks[name][0:rows, 0:cols], lhsT, rhs, start=(n == 0),
                                        stop=(n == len(pairs) - 1))
                    banks.fills(name, ins)

                def each(name, products, rows=128, width=128):
                    banks.wait_free(pe, g, name)
                    for m, pairs in enumerate(products):
                        for n, (lhsT, rhs) in enumerate(pairs):
                            ins = pe.matmul(banks[name][0:rows, m * width:(m + 1) * width], lhsT, rhs,
                                            start=(n == 0), stop=(n == len(pairs) - 1))
                    banks.fills(name, ins)

                ctx_loaded.wait(pe, g, 1)
                each("vprime", [[(ctxT[:, b, :], wvo[:, :])] for b in range(NB)], rows=S)
                banks.wait_read(pe, g, "vprime")
                hank_loaded.wait(pe, g, 1)
                each("agg", [[(hank[:, b, :], vprime[:, b, :])] for b in range(NB)])

                for l in range(LAYERS):
                    if l:
                        banks.wait_read(pe, g, ("down", l - 1))
                    else:
                        y_ready.wait(pe, g, 1)
                    turn(("yT", l), [y0[:, b, :] for b in range(NB)])

                    def qkv(b):
                        if b >= NB:
                            return
                        for n, name in enumerate(("q", "k", "v")):
                            whole((name, l, b), [(yT[:, b, :], wqkv[:, l, n * INNER:(n + 1) * INNER])])

                    def turns(b):
                        if b >= NB:
                            return
                        qk_ready.wait(pe, g, l * NB + b + 1)
                        for n, name in enumerate(("qT", "kT")):
                            turn((name, l, b), [qk[:, b % 2, n, a * 128:a * 128 + 128] for a in range(4)])

                    def scores(b):
                        names = [("sim", l, b, s) for s in range(2)]
                        for name in names:
                            banks.wait_free(pe, g, name)
                            pe.matmul(banks[name][:, :], ident_b[:, :],
                                      mask_b[:, :, :].rearrange("p h j -> p (h j)"),
                                      start=True, stop=False, skip_group_check=True)
                        for h in range(HALF):
                            for s, name in enumerate(names):
                                ins = pe.matmul(banks[name][:, h * 128:h * 128 + 128],
                                                qT[64 * s:64 * s + 64, b % 2, h, :],
                                                kT[64 * s:64 * s + 64, b % 2, h, :], start=False,
                                                stop=(h == HALF - 1), skip_group_check=True)
                                if h == HALF - 1:
                                    banks.fills(name, ins)

                    def weighted(b, s):
                        banks.wait_read(pe, g, ("pT", l, b, s))
                        each(("o", l, b, s), [[(probT[:, s, h, :], vx[:, b, 2 * h + s, :])]
                                              for h in range(HALF)], width=DH + 1)

                    def out_turns(b):
                        banks.wait_read(pe, g, ("o", l, b, 1))
                        turn(("oT", l, b), [o[:, b % 2, 2 * a:2 * a + 2, :].rearrange("p h d -> p (h d)")
                                            for a in range(4)])

                    def project(b):
                        banks.wait_read(pe, g, ("oT", l, b))
                        whole(("wo", l, b), [(oT[:, b % 2, a, :], wo[:, l, a, :]) for a in range(4)], cols=128)

                    banks.wait_read(pe, g, ("yT", l))
                    qkv(0)
                    qkv(1)
                    turns(0)
                    for b in range(NB):
                        banks.wait_read(pe, g, ("qT", l, b))
                        banks.wait_read(pe, g, ("kT", l, b))
                        scores(b)
                        qkv(b + 2)
                        for s in range(2):
                            banks.wait_read(pe, g, ("sim", l, b, s))
                            turn(("pT", l, b, s), [prob[:, b % 2, s, h, :] for h in range(HALF)])
                        if b:
                            out_turns(b - 1)
                        banks.wait_read(pe, g, ("v", l, b))
                        weighted(b, 0)
                        if b:
                            project(b - 1)
                        weighted(b, 1)
                        turns(b + 1)
                    out_turns(NB - 1)
                    project(NB - 1)
                    hn_ready.wait(pe, g, l + 1)
                    turn(("hT", l), [xn[:, b, :] for b in range(NB)])
                    banks.wait_read(pe, g, ("hT", l))
                    tokens = zT[:, :, :].rearrange("p b t -> p (b t)")
                    for j in range(3):
                        for part, name in ((1, "gate"), (0, "up")):
                            at = part * HID + j * 128
                            whole((name, l, j), [(w1g[:, l, at:at + HT[j]], tokens)], rows=HT[j])
                    for j in range(3):
                        banks.wait_read(pe, g, ("up", l, j))
                    k3 = HT[2] + 1
                    each(("down", l), [[(hid[:, 0, b * 128:b * 128 + 128], w2[:, l, 0, :]),
                                        (hid[:, 1, b * 128:b * 128 + 128], w2[:, l, 1, :]),
                                        (hid[0:k3, 2, b * 128:b * 128 + 128], w2[0:k3, l, 2, :])]
                                       for b in range(NB)])

                z_ready.wait(pe, g, 1)
                turn("zT", [xn[:, b, :] for b in range(NB)])
                banks.wait_read(pe, g, "zT")
                tokens = zT[:, :, :].rearrange("p b t -> p (b t)")
                contexts = ctxT[:, :, :].rearrange("p b s -> p (b s)")
                whole("qc", [(cw[:, 0, :], tokens)])
                whole("ks", [(cw[:, 1, :], contexts)], cols=NB * S)
                each("vs", [[(ctxT[:, b, :], cw[:, 2, :])] for b in range(NB)], rows=S)
                whole("qs", [(cw[:, 3, :], contexts)], cols=NB * S)
                whole("kc", [(cw[:, 4, :], tokens)])
                each("vc", [[(zT[:, b, :], cw[:, 5, :])] for b in range(NB)])
                for name in ("qc", "ks"):
                    banks.wait_read(pe, g, name)
                each("s1", [[(qcT[:, b, :], ksT[:, b, :])] for b in range(NB)], width=S)
                for name in ("qs", "kc"):
                    banks.wait_read(pe, g, name)
                each("s2", [[(qsT[:, b, :], kcT[:, b, :])] for b in range(NB)], rows=S)
                cprob_ready.wait(pe, g, 1)
                turn("p1T", [p1[:, b, :] for b in range(NB)], rows=S)
                for name in ("p1T", "vs"):
                    banks.wait_read(pe, g, name)
                each("c2s", [[(vs[:, b, :], p1T[:, b, :])] for b in range(NB)])
                cprob_ready.wait(pe, g, 2)
                each("a", [[(p2[:, b, :], const("interp", S))] for b in range(NB)])
                for name in ("a", "vc"):
                    banks.wait_read(pe, g, name)
                each("s2c", [[(vc[:, b, :], aT[:, b, :])] for b in range(NB)])
                for name in ("c2s", "s2c"):
                    banks.wait_read(pe, g, name)
                whole("g", [(cw[:, 6, :], c2sT[:, :, :].rearrange("p b t -> p (b t)")),
                            (cw[:, 7, :], s2cT[:, :, :].rearrange("p b t -> p (b t)"))])
                mix_ready.wait(pe, g, 1)
                turn("mixT", [gt[:, b, :] for b in range(NB)])

                yd_ready.wait(pe, g, 1)
                turn("dT", [yd[:, b, :] for b in range(NB)])

                def hidden_turns(b):
                    silq_ready.wait(pe, g, b + 1)
                    turn(("hqT", b), [silb[:, b % 2, a * 128:a * 128 + 128] for a in range(4)],
                         idn=ident_b, dt=BF16)

                banks.wait_read(pe, g, "dT")
                for b in range(NB):
                    whole(("h", b), [(ydT[:, b, k:k + T], wc[:, k, :]) for k in range(3)]
                          + [(ones3[:, :], conv_b3[:, :])])
                    if b:
                        hidden_turns(b - 1)
                hidden_turns(NB - 1)
                for b in range(NB):
                    banks.wait_read(pe, g, ("hqT", b))
                each("ffn", [[(silT[:, b, a, :], q2T[:, a, :]) for a in range(4)] for b in range(NB)])


VECTOR_STEPS = 65
POOL_STEPS = 2 * NB * LAYERS

_INS = ['x', 'ctx', 'ctxT', 'constants', 'weights', 'rows']
_OUTS = [((B, T, D), 'float32')]


def kernel(**inputs):
    import numpy as _np
    import concourse.bacc as _bacc
    from concourse import mybir as _mybir
    from concourse.bass_utils import run_bass_kernel_spmd as _run

    nc = _bacc.Bacc("TRN2", target_bir_lowering=False, num_devices=1)
    arrays, args = {}, []
    given = {k: _np.asarray(v) for k, v in inputs.items()}
    laid = {'x': given['x'], 'ctx': given['ctx_1024'], 'ctxT': given['ctx_1024'][:, ::-1].transpose(2, 0, 1),
            'constants': constant_array(), 'weights': weight_array(given), 'rows': row_array(given)}
    for name in _INS:
        a = _np.ascontiguousarray(laid[name])
        arrays[f"in_{name}_dram"] = a
        args.append(nc.dram_tensor(f"in_{name}_dram", a.shape, _mybir.dt.from_np(a.dtype), kind="ExternalInput").ap())
    for i, (shape, dtype) in enumerate(_OUTS):
        dt = _mybir.dt.from_np(_np.dtype(dtype))
        args.append(nc.dram_tensor(f"out_{i}_dram", shape, dt, kind="ExternalOutput").ap())
    xattn_ffn_stack_kernel(nc, *args)
    r = _run(nc, [arrays], core_ids=[0])
    return r.results[0]["out_0_dram"]
```

```python
from contextlib import ExitStack

import numpy as np

import concourse.bass as bass
from concourse import mybir

F32 = mybir.dt.float32
BF16 = mybir.dt.bfloat16
ALU = mybir.AluOpType
ACT = mybir.ActivationFunctionType
AX = mybir.AxisListType

B, T, D, S = 16, 128, 128, 77
NB = 4
NG = B // NB
LAYERS, HEADS, DH = 2, 8, 64
HALF = HEADS // 2
INNER = HEADS * DH
HID = 341
HT = (128, 128, HID - 256)
DHID = 512
TOPK = int(2 * np.log(T))
MAGIC = 1.5 * 2.0 ** 23
NEG = -1.0e30
LN_EPS = 1e-5
CORR_SCALE = 1.0 / np.sqrt(D)
NBANKS = 8

CONST_COLS = {}


def constant_array():
    t = np.arange(T, dtype=np.float64)
    cols = {}
    cols["zero"] = np.zeros((128, 1))
    cols["ident"] = np.eye(128)
    cosines = np.cos(2 * np.pi * np.outer(t, np.arange(T // 2 + 1)) / T)
    sines = np.sin(2 * np.pi * np.outer(t, np.arange(1, T // 2)) / T)
    dft = np.concatenate([cosines, sines], axis=1)
    cols["dft"] = dft
    weight = np.full(T, 2.0)
    weight[0] = weight[T // 2] = 1.0
    cols["inverse_dft"] = (dft * weight[None, :] / T / D).T
    half = np.arange(0, DH, 2, dtype=np.float64)
    freqs = np.concatenate([np.outer(t, 10000.0 ** (-half / DH))] * 2, axis=1)
    base = (half + 0.4 * DH) / (1.4 * DH)
    scale = base[None, :] ** ((t[:, None] - T // 2) / 32.0)
    scale = np.concatenate([scale, scale], axis=1)
    sign = np.where(np.arange(DH) < DH // 2, -1.0, 1.0)[None, :]
    cols["rope"] = np.concatenate([8 * np.cos(freqs) * scale, 8 * sign * np.sin(freqs) * scale,
                                   np.cos(freqs) / scale, sign * np.sin(freqs) / scale], axis=1)
    i, j = t[:, None], t[None, :]
    cols["mask"] = np.where((i < j) | (i > j + 64), NEG, 0.0)
    pos = np.clip((t + 0.5) * (S / T) - 0.5, 0.0, S - 1)
    lo = np.floor(pos).astype(int)
    hi = np.minimum(lo + 1, S - 1)
    interp = np.zeros((T, T))
    np.add.at(interp, (S - 1 - lo, np.arange(T)), 1 - (pos - lo))
    np.add.at(interp, (S - 1 - hi, np.arange(T)), pos - lo)
    cols["interp"] = interp
    sums = np.zeros((128, 2 * T))
    sums[0, :T] = dft.sum(0)
    sums[0, T:] = dft[:S].sum(0)
    cols["sums"] = sums
    at = 0
    for name, a in cols.items():
        CONST_COLS[name] = (at, at + a.shape[1])
        at += a.shape[1]
    return np.concatenate(list(cols.values()), axis=1).astype(np.float32)


constant_array()
CONST_WIDTH = max(b for _, b in CONST_COLS.values())


WEIGHTS = {"corr_w": 4 * 128, "corr_bv": 1, "lngb": 2 * LAYERS, "b1": LAYERS * 6, "cb": 7,
           "w1": LAYERS * 2 * HID, "q1": DHID, "q2": DHID, "cw": 8 * 128, "wqkv": LAYERS * 3 * INNER,
           "wo": LAYERS * 4 * 128, "w2": LAYERS * 3 * 128}
ROWS = {"bq": 128, "bk": 128, "conv_b": DHID, "bo": 128, "scales": 2 * LAYERS * DH, "conv_w": 3 * DHID}


def places(widths):
    ends = np.cumsum(list(widths.values()))
    return {name: (int(b) - w, int(b)) for (name, w), b in zip(widths.items(), ends)}


WEIGHT_AT, ROW_AT = places(WEIGHTS), places(ROWS)


def weight_array(i):
    a = np.zeros((128, sum(WEIGHTS.values())), np.float32)

    def put(name, at, block):
        at += WEIGHT_AT[name][0]
        a[0:block.shape[0], at:at + block.shape[1]] = block

    for n, w in enumerate((i["L0_xattn_Wq"], i["L0_xattn_Wk"], i["L0_xattn_Wv"].T, i["L0_xattn_Wo"])):
        put("corr_w", n * 128, w)
    put("corr_bv", 0, i["L0_xattn_bv"][:, None])
    put("lngb", 0, i["L0_ffn_ln_g"].T)
    put("lngb", LAYERS, i["L0_ffn_ln_b"].T)
    for l in range(LAYERS):
        for j, rows in enumerate(HT):
            for part in range(2):
                at = part * HID + 128 * j
                put("b1", 6 * l + 3 * part + j, i["L0_ffn_b1"][l, at:at + rows, None])
            put("w2", (3 * l + j) * 128, i["L0_ffn_w2"][l, 128 * j:128 * j + rows])
        a[HT[2], WEIGHT_AT["w2"][0] + (3 * l + 2) * 128:][:128] = i["L0_ffn_b2"][l]
        put("w1", 2 * HID * l, i["L0_ffn_w1"][l])
        put("wqkv", 3 * INNER * l, i["L0_ffn_wqkv"][l])
        for t in range(4):
            put("wo", (4 * l + t) * 128, i["L0_ffn_wo"][l, 128 * t:128 * t + 128])
    cross = ("q_c", "k_s", "v_s", "q_s", "k_c", "v_c", "g")
    for n, name in enumerate(cross):
        w = i["L1_xattn_W" + name]
        for m in range(w.shape[1] // 128):
            put("cw", (n + m) * 128, w[:, 128 * m:128 * m + 128].T)
        put("cb", n, i["L1_xattn_b" + name][:, None])
    put("q1", 0, i["L1_ffn_w1"].T)
    for t in range(4):
        put("q2", 128 * t, i["L1_ffn_w2"][:, 128 * t:128 * t + 128].T)
    return a


def row_array(i):
    return np.concatenate([i["L0_xattn_bq"], i["L0_xattn_bk"], i["L1_ffn_conv_b"], i["L0_xattn_bo"],
                           i["L0_ffn_q_scale"].reshape(-1), i["L0_ffn_k_scale"].reshape(-1),
                           i["L1_ffn_conv_w"][:, 0, :].T.reshape(-1)])[None, :]


class Signal:

    def __init__(self, sem, per_group, step=1):
        self.sem, self.per_group, self.step = sem, per_group * step, step

    def raised_by(self, ins):
        ins.then_inc(self.sem, self.step)
        return ins

    def wait(self, eng, g, n):
        eng.wait_ge(self.sem, g * self.per_group + n * self.step)


class Chain(Signal):

    def __init__(self, sem, per_group):
        super().__init__(sem, per_group)
        self.n = 0

    def link(self, eng, g, ins):
        self.n += 1
        self.raised_by(ins)
        self.wait(eng, g, self.n)


ATTN_BANKS, FF_BANKS, FINISH_BANKS = 4, 2, 2
PAIRS = NB // 2

ORDER = """
    vprime agg yT.0.0 yT.0.1 ff:hs.1.1 qkv.0 rot.0.0 ff:hT.1.1 rot.0.1 fin:vs ff:gu.1.1.0 qkv.1 rot.1.0
    ff:gu.1.1.1 ff:gu.1.1.2 rot.1.1 turns.0 fin:ks scores.0 sm.0.0 ff:down.1.1 fin:z_moments qkv.2 sm.0.1
    rot.2.0 pT.0 rot.2.1 turns.1 o.0.0 fin:zn o.0.1 scores.1 fin:zT sm.1.0 qkv.3 sm.1.1 fin:qc fin:kc
    rot.3.0 pT.1 rot.3.1 fin:s1 o.1.0 o.1.1 oT.0 turns.2 oT.1 wo.0 scores.2 sm.2.0 wo.1 fin:qs sm.2.1
    ff:hs.0.0 fin:vc turns.3 ff:hT.0.0 pT.2 ff:gu.0.0.0 scores.3 fin:p1 ff:gu.0.0.1 ff:gu.0.0.2 fin:p1T
    sm.3.0 o.2.0 sm.3.1 fin:s2 ff:down.0.0 o.2.1 fin:p2 yT.1.0 pT.3 oT.2 qkv.4 rot.4.0 fin:a rot.4.1 fin:c2s
    fin:s2c qkv.5 fin:g rot.5.0 rot.5.1 o.3.0 o.3.1 turns.4 wo.2 fin:mix oT.3 scores.4 sm.4.0 sm.4.1 wo.3
    ff:hs.0.1 turns.5 fin:mixT pT.4 scores.5 ff:hT.0.1 sm.5.0 sm.5.1 o.4.0 ff:gu.0.1.0 ff:gu.0.1.1 o.4.1
    pT.5 ff:gu.0.1.2 o.5.0 o.5.1 ff:down.0.1 oT.4 fin:quant oT.5 yT.1.1 wo.4 wo.5 qkv.6 fin:dT rot.6.0
    rot.6.1 qkv.7 rot.7.0 rot.7.1 fin:h.0 turns.6 fin:hq.0 fin:h.1 scores.6 sm.6.0 sm.6.1 turns.7 ff:hs.1.0
    fin:hqT.0 fin:h.2 pT.6 ff:hT.1.0 scores.7 fin:hq.1 fin:hqT.1 sm.7.0 sm.7.1 fin:hq.2 fin:h.3 o.6.0 o.6.1
    fin:hq.3 pT.7 ff:gu.1.0.0 oT.6 o.7.0 fin:hqT.2 ff:gu.1.0.1 fin:hqT.3 o.7.1 ff:gu.1.0.2 fin:ffn oT.7 wo.6
    ff:down.1.0 wo.7
"""


def schedule():
    for word in ORDER.split():
        part, _, step = word.rpartition(":")
        name, *numbers = step.split(".")
        yield (part or "attn", name, *(int(n) for n in numbers))


def psum_units(part):
    units = []
    for p, name, *args in schedule():
        if p != part:
            continue
        if name == "qkv":
            l, b = divmod(args[0], NB)
            units += [("q", l, b), ("k", l, b), ("v", l, b)]
        elif name == "turns":
            units += [("qT", args[0]), ("kT", args[0])]
        elif name == "scores":
            units += [("sim", args[0], s) for s in range(2)]
        elif name == "pT":
            units += [("pT", args[0], s) for s in range(2)]
        elif name in ("o", "oT", "wo", "yT", "hs", "hT", "gu", "down", "h", "hqT"):
            units.append((name, *args))
        elif name not in ("rot", "sm", "z_moments", "zn", "p1", "p2", "mix", "quant", "hq"):
            units.append(name)
    if part == "ff":
        last = [u for u in units if u[1:3] == (LAYERS - 1, PAIRS - 1)]
        units = [u for u in units if u not in last] + last
    return units


VECTOR_STEPS = 2 + 3 * NB * LAYERS
POOL_STEPS = 3 * NB * LAYERS
FINISH_STEPS = 35


class Banks:

    def __init__(self, order, tensors, filled, freed):
        self.tensors, self.filled, self.freed = tensors, filled, freed
        self.at = {name: n for n, name in enumerate(order)}
        self.nbanks = len(tensors)
        self.uses = [len(range(k, len(self.at), self.nbanks)) for k in range(self.nbanks)]

    def __getitem__(self, name):
        return self.tensors[self.at[name] % self.nbanks]

    def wait_for(self, pe, g, free=None, read=()):
        need = {}
        for name, more in [(name, 2) for name in read] + ([(free, 1)] if free is not None else []):
            k, n = self.at[name] % self.nbanks, self.at[name] // self.nbanks
            need[k] = max(need.get(k, 0), n + more)
        for k, n in need.items():
            pe.wait_ge(self.freed[k], g * self.uses[k] + n)

    def fills(self, name, ins):
        ins.then_inc(self.filled[self.at[name] % self.nbanks], 1)

    def wait_read(self, eng, g, name):
        k, n = self.at[name] % self.nbanks, self.at[name] // self.nbanks
        eng.wait_ge(self.freed[k], g * self.uses[k] + n + 2)

    def wait_filled(self, eng, g, name):
        k, n = self.at[name] % self.nbanks, self.at[name] // self.nbanks
        eng.wait_ge(self.filled[k], g * self.uses[k] + n + 1)

    def frees(self, name, ins):
        ins.then_inc(self.freed[self.at[name] % self.nbanks], 1)


def xattn_ffn_stack_kernel(nc, x, ctx_in, ctxT_in, consts, weights, rows_in, out):
    stack = ExitStack()
    with stack:
        def sb(name, shape, dt=F32):
            return stack.enter_context(nc.sbuf_tensor(name, shape, dt))

        def sem(name):
            return stack.enter_context(nc.semaphore(name))

        cst = sb("cst", [128, CONST_WIDTH])

        def const(name, rows=128):
            a, b = CONST_COLS[name]
            return cst[0:rows, a:b]

        ident = const("ident")
        ident_b = sb("ident_b", [128, 128], BF16)
        mask_b = sb("mask_b", [128, HALF, 128], BF16)
        ones = sb("ones", [128, 128])
        first = WEIGHT_AT["q2"][1]
        late = sb("late_weights", [128, sum(WEIGHTS.values()) - first])
        early = sb("early_weights", [128, WEIGHT_AT["cb"][1]])

        def weight(name):
            a, b = WEIGHT_AT[name]
            return early[:, a:b] if b <= WEIGHT_AT["cb"][1] else late[:, a - first:b - first]

        corr_w = weight("corr_w").rearrange("p (n o) -> p n o", n=4)
        corr_bv = weight("corr_bv")
        lngb = weight("lngb").rearrange("p (a l) -> p a l", a=2)
        b1 = weight("b1").rearrange("p (l a j) -> p l a j", l=LAYERS, a=2)
        cb = weight("cb")
        cw = weight("cw").rearrange("p (n o) -> p n o", n=8)
        wqkv = weight("wqkv").rearrange("p (l f) -> p l f", l=LAYERS)
        wo = weight("wo").rearrange("p (l a d) -> p l a d", l=LAYERS, a=4)
        w2 = weight("w2").rearrange("p (l a d) -> p l a d", l=LAYERS, a=3)
        corr_rows = sb("corr_rows", [1, 2, 128])
        bv_cols = sb("bv_cols", [128, S])
        wvo = sb("wvo", [128, 128])
        bvo = sb("bvo", [S, 128])
        bias_f = sb("bias_f", [128, 2, 128])
        scales = sb("scales", [128, 2, LAYERS, DH])
        rope = sb("rope", [128, LAYERS, 2, 2, DH])
        w1g = sb("w1g", [128, LAYERS, 2 * HID])
        cbs = sb("cbs", [128, 3])
        qsum = sb("qsum", [128, 2])
        qscale = sb("qscale", [128, 6])
        conv_parts = sb("conv_parts", [1, 3, DHID], BF16)
        conv_b3 = sb("conv_b3", [3, DHID], BF16)
        ones3 = sb("ones3", [3, 128], BF16)
        wc = sb("wc", [128, 3, DHID])
        q2T = sb("q2T", [128, 4, 128], BF16)

        spec = sb("spec", [128, B])
        corr = sb("corr", [B, 128])
        left = sb("left", [B, 2, 128])
        top8 = sb("top8", [B, 3, 8])
        corr_e = sb("corr_e", [B, 2, 128])
        corr_s = sb("corr_s", [B, 4])
        delay_w = sb("delay_w", [B, 2, 128])

        x0 = sb("x0", [128, NB, 128])
        hank = sb("hank", [S + 1, NB, 128])
        ctxT = sb("ctxT", [128, NB, S])
        ctxF = sb("ctxF", [128, NB, S])
        vprime = sb("vprime", [S + 1, NB, 128])
        x1 = sb("x1", [128, NB, 128])
        x2 = sb("x2", [128, NB, 128])
        x3 = sb("x3", [128, NB, 128])
        xs = sb("xs", [128, NB, 128])
        xn = sb("xn", [128, NB, 128])
        y0 = sb("y0", [128, NB, 128])
        y1 = sb("y1", [128, NB, 128])
        stats = sb("stats", [128, NB, 6])
        meanvar = sb("meanvar", [128, NB, 2])
        hstats = sb("hstats", [128, NB, 6])
        hmeanvar = sb("hmeanvar", [128, NB, 2])
        hvareps = sb("hvareps", [128, NB])
        hrstd = sb("hrstd", [128, NB])
        fstats = sb("fstats", [128, NB, 6])
        fmeanvar = sb("fmeanvar", [128, NB, 2])
        fvareps = sb("fvareps", [128, NB])
        frstd = sb("frstd", [128, NB])
        zn = sb("zn", [128, NB, 128])
        znT = sb("znT", [128, NB, 128])
        pause = sb("pause", [128, 1])
        vareps = sb("vareps", [128, NB])
        rstd = sb("rstd", [128, NB])
        minus_half = sb("minus_half", [128, 2 * HEADS])
        yT = sb("yT", [128, NB, 128])
        sq = sb("sq", [128, 2, 2, INNER])
        ssq = sb("ssq", [128, 2, 2 * HEADS])
        ssqc = sb("ssqc", [128, 2, 2 * HEADS])
        rnorm = sb("rnorm", [128, 2, 2 * HEADS])
        t_cos = sb("t_cos", [128, 2, 2, INNER])
        t_sin = sb("t_sin", [128, 2, 2, INNER])
        qk = sb("qk", [128, 2, 2, INNER])
        vx = sb("vx", [128, NB, HEADS, DH + 1])
        qT = sb("qT", [128, 2, 4, 128])
        kT = sb("kT", [128, 2, 4, 128])
        nmax = sb("nmax", [128, 2, HEADS])
        prob = sb("prob", [128, 2, 2, HALF, 128])
        probT = sb("probT", [128, 2, HALF, 128])
        rsum = sb("rsum", [128, 2, HEADS])
        o = sb("o", [128, 2, HEADS, DH])
        oT = sb("oT", [128, 2, 4, 128])
        gel = sb("gel", [128, 3, NB * 128])
        hid = sb("hid", [128, 3, NB * 128])
        zT = sb("zT", [128, NB, 128])
        nm1 = sb("nm1", [128, 4, NB])
        amax = sb("amax", [128, 4, NB])
        ydT = sb("ydT", [128, NB, 130])
        silb = sb("silb", [128, 2, DHID], BF16)
        silT = sb("silT", [128, NB, 4, 128], BF16)
        amax2 = sb("amax2", [128, 4, NB])

        def within(tensor, at, shape, dt=F32):
            letters = "abcd"[:len(tensor.shape) - 1]
            flat = tensor[:, :] if len(tensor.shape) == 2 else \
                tensor[tuple([slice(None)] * len(tensor.shape))].rearrange(
                    f"p {' '.join(letters)} -> p ({' '.join(letters)})")
            size = int(np.prod(shape[1:]))
            flat = flat[0:shape[0], at:at + size]
            if len(shape) == 2:
                return flat
            letters = "abcd"[:len(shape) - 1]
            return flat.rearrange(f"p ({' '.join(letters)}) -> p {' '.join(letters)}",
                                  **{c: n for c, n in zip(letters, shape[1:])})

        conv_w = within(sq, 0, [128, 3, DHID])
        ctx = within(sq, 3 * DHID, [S, NB, 128])
        w1 = within(t_cos, 0, [128, LAYERS, 2 * HID])
        conv_b = within(gel, 1024, [1, DHID])
        conv_tmp = within(hid, 0, [1, 2, DHID])
        q1 = within(t_sin, 0, [128, DHID])
        q2 = within(t_sin, DHID, [128, DHID])
        spec_t = within(gel, 0, [128, 2, NB, 128])
        spec_q = within(prob, 0, [128, NB, 128])
        spec_k = within(prob, 512, [128, NB, 128])
        spec_junk = within(prob, 1024, [128, NB, 128])
        cross = sb("cross", [128, 4 * 512])
        gated = sb("gated", [128, 5 * 512])
        attn = sb("attn", [128, 3 * NB * S + 3 * 512])
        qcT, kcT, vc, aT = (within(cross, 512 * n, [128, NB, 128]) for n in range(4))
        c2sT, s2cT, gt = (within(gated, 512 * n, [128, NB, 128]) for n in range(3))
        mix = within(gated, 3 * 512, [128, 2, NB, 128])
        ksT, qsT, p1 = (within(attn, NB * S * n, [128, NB, S]) for n in range(3))
        vs, p1T, p2 = (within(attn, 3 * NB * S + 512 * n, [S, NB, 128]) for n in range(3))
        yq, yd = (within(gated, 512 * n, [128, NB, 128]) for n in range(2))
        sil = within(cross, 0, [128, 2, DHID])
        silq = within(cross, 1024, [128, 2, DHID])

        psum = [stack.enter_context(nc.psum_tensor(f"bank{k}", [128, 512], F32)) for k in range(NBANKS)]
        filled = [sem(f"bank{k}_filled") for k in range(NBANKS)]
        freed = [sem(f"bank{k}_freed") for k in range(NBANKS)]
        at = (0, ATTN_BANKS, ATTN_BANKS + FF_BANKS, NBANKS)
        banks, hbanks, fbanks = (Banks(psum_units(part), psum[a:b], filled[a:b], freed[a:b])
                                 for part, a, b in zip(("attn", "ff", "fin"), at, at[1:]))
        delays = nc.dram_tensor("delay_weights", [B, 2 * 128], F32, kind="Internal").ap()

        w_loaded = sem("weights_loaded")
        c_loaded = sem("constants_loaded")
        conv_loaded = sem("conv_bias_parts_loaded")
        pool_set = sem("pool_constants_set")
        prep_pe = sem("prep_products_ready")
        prep_dve = Chain(sem("prep_vector_steps"), 0)
        prep_act = sem("prep_scalar_steps")
        f_loaded = sem("search_inputs_loaded")
        f_var = sem("search_variance_ready")
        f_rstd = sem("search_rstd_ready")
        f_norm = sem("search_tokens_normalised")
        f_spec = sem("search_tokens_transformed")
        f_copied = sem("search_transform_copied")
        f_proj = sem("search_projected")
        f_taken = sem("search_projection_taken")
        f_chain = Chain(sem("search_vector_steps"), 4)
        s_spec = sem("spectra_ready")
        s_corr = sem("correlation_ready")
        s_shift = sem("correlation_shift_ready")
        s_exp = sem("delay_exponentials_ready")
        s_delay = sem("delay_weights_ready")
        s_stored = sem("delay_weights_stored")
        x_loaded = Signal(sem("x_loaded"), 1, 16)
        ctx_loaded = Signal(sem("ctx_loaded"), 1, 16)
        hank_loaded = Signal(sem("hankel_loaded"), 1, 16)
        ctxF_loaded = Signal(sem("second_part_ctx_loaded"), 1, 16)
        var_ready = Signal(sem("variance_ready"), 1)
        rstd_ready = Signal(sem("rstd_ready"), 1)
        hvar_ready = Signal(sem("feed_forward_variance_ready"), LAYERS * PAIRS)
        hrstd_ready = Signal(sem("feed_forward_rstd_ready"), LAYERS * PAIRS)
        gel_ready = Signal(sem("gate_ready"), 3 * LAYERS * PAIRS)
        xs_ready = Signal(sem("x1_added"), PAIRS)
        fvar_ready = Signal(sem("second_part_variance_ready"), 2)
        frstd_ready = Signal(sem("second_part_rstd_ready"), 2)
        y_ready = Signal(sem("stack_input_ready"), 1)
        sq_ready = Signal(sem("squares_ready"), 2 * NB * LAYERS)
        ssq_ready = Signal(sem("square_sums_ready"), NB * LAYERS)
        qk_ready = Signal(sem("qk_ready"), 2 * NB * LAYERS)
        nmax_ready = Signal(sem("score_max_ready"), 2 * NB * LAYERS)
        z_ready = Signal(sem("z_ready"), 1)
        cmax_ready = Signal(sem("cross_max_ready"), 2)
        cprob_ready = Signal(sem("cross_prob_ready"), 2)
        diff_ready = Signal(sem("cross_difference_ready"), 1)
        mix_ready = Signal(sem("mix_ready"), 1)
        yd_ready = Signal(sem("quantised_input_ready"), 1)
        silq_ready = Signal(sem("quantised_hidden_ready"), NB)
        x3_stored = Signal(sem("result_stored"), 1, 16)
        steps = Chain(sem("vector_steps"), VECTOR_STEPS)
        hsteps = Chain(sem("feed_forward_vector_steps"), 2 * LAYERS * PAIRS)
        fsteps = Chain(sem("second_part_vector_steps"), FINISH_STEPS)
        pool_steps = Chain(sem("pool_steps"), POOL_STEPS)

        block = stack.enter_context(nc.Block())
        weight_loads = [0]
        prep_steps = []

        @block.sync
        def _(sp):
            def load(dst, src):
                sp.dma_start(dst, src).then_inc(w_loaded, 16)
                weight_loads[0] += 1

            sp.dma_start(cst[:, :], consts).then_inc(c_loaded, 16)
            def packed(name, last=None):
                return weights[:, WEIGHT_AT[name][0]:WEIGHT_AT[last or name][1]]

            def row(name):
                return rows_in[:, ROW_AT[name][0]:ROW_AT[name][1]]

            load(early[:, :], packed("corr_w", "cb"))
            load(corr_rows[:, :, :].rearrange("p a n -> p (a n)"), rows_in[:, 0:256])
            load(scales[:, :, :, :].rearrange("p a l d -> p (a l d)"), row("scales")[0].partition_broadcast(128))
            load(w1.rearrange("p l f -> p (l f)"), packed("w1"))
            load(q1, packed("q1"))
            load(q2, packed("q2"))
            load(conv_w.rearrange("p k c -> p (k c)"), row("conv_w")[0].partition_broadcast(128))
            load(conv_b[:, :], row("conv_b"))
            for b in range(NB):
                load(vprime[S:S + 1, b, :], row("bo"))
            load(late[:, :], packed("cw", "w2"))

            with sp.Fori(0, NG) as g:
                sp.wait_ge(f_spec, g + 1)
                sp.dma_start(x0[:, :, :], x.rearrange("(g b) t d -> g t b d", b=NB)[g]).then_inc(f_loaded, 16)
                sp.dma_start(ctx[:, :, :], ctx_in.rearrange("(g b) t d -> g t b d", b=NB)[g]).then_inc(f_loaded, 16)
            sp.wait_ge(s_delay, 1)
            sp.dma_start(delays, delay_w[:, :, :].rearrange("b a t -> b (a t)")).then_inc(s_stored, 16)
            sp.wait_ge(s_stored, 16)

            def load_tokens(g):
                at_x, at_w = g[0], g[1]
                x_loaded.raised_by(sp.dma_start(
                    x0[:, :, :], bass.AP(x.tensor, at_x, [[D, T], [T * D, NB], [1, D]])))
                hank_loaded.raised_by(sp.dma_start(
                    hank[0:S, :, :], bass.AP(delays.tensor, at_w, [[1, S], [2 * T, NB], [1, T]])))

            def load_context(g, dst, loaded):
                loaded.raised_by(sp.dma_start(
                    dst[:, :, :], bass.AP(ctxT_in.tensor, g[2], [[B * S, D], [S, NB], [1, S]])))

            def addresses(g, hold=lambda v: v):
                return hold(g * (NB * T * D)), hold(g * (NB * 2 * T) + T - S), hold(g * (NB * S))

            def turn(ga, gb, more):
                hold = sp.snap if more and gb is not None else (lambda v: v)
                if gb is not None:
                    out_at = addresses(gb, hold)
                if ga is not None:
                    here = addresses(ga, hold)
                if more:
                    ahead = addresses(ga + 1, hold)
                if ga is not None:
                    if more:
                        banks.wait_read(sp, ga, "vprime")
                        load_context(ahead, ctxT, ctx_loaded)
                        banks.wait_read(sp, ga, "agg")
                        load_tokens(ahead)
                    if gb is not None:
                        fbanks.wait_read(sp, gb, "g")
                        load_context(here, ctxF, ctxF_loaded)
                if gb is not None:
                    fbanks.wait_read(sp, gb, "ffn")
                    x3_stored.raised_by(sp.dma_start(
                        bass.AP(out.tensor, out_at[0], [[D, T], [T * D, NB], [1, D]]), x3[:, :, :]))

            load_tokens(addresses(0))
            load_context(addresses(0), ctxT, ctx_loaded)
            load_context(addresses(0), ctxF, ctxF_loaded)
            turn(0, None, True)
            with sp.Fori(0, NG - 2) as g:
                turn(g + 1, g, True)
            turn(NG - 1, NG - 2, False)
            turn(None, NG - 1, False)
            sp.wait_ge(x3_stored.sem, 16 * (NG + 1))

        @block.gpsimd
        def _(pool):
            for k in range(NBANKS):
                pool.sem_inc(freed[k], 1)
            pool.sem_inc(f_spec, 1)
            pool.sem_inc(s_spec, 1)
            pool.sem_inc(x3_stored.sem, 16)
            pool.memset(minus_half[:, :], -0.5)
            pool.memset(ones[:, :], 1.0)
            pool.memset(ones3[:, :], 1.0)
            pool.memset(hank[:, :, :], 1.0)
            pool.memset(vx[:, :, :, :], 1.0)
            pool.memset(hid[:, 2, :], 1.0)
            pool.memset(yT[:, :, :], 0.0)
            pool.memset(ydT[:, :, :], 0.0).then_inc(pool_set, 1)

            pool.wait_ge(pool_set, 1)
            with pool.Fori(0, NG) as g:
                pool.wait_ge(f_var, g + 1)
                pool.tensor_tensor(rstd[:, :], vareps[:, :], minus_half[:, 0:NB], ALU.pow).then_inc(f_rstd, 1)

            def deviation(g, n, ready, ve, rs, raised, a, b):
                ready.wait(pool, g, n)
                raised.raised_by(pool.tensor_tensor(rs[:, a:b], ve[:, a:b], minus_half[:, a:b], ALU.pow))

            def rotated(g, i, part):
                (l, b), p = divmod(i, NB), i % 2
                if part == 0:
                    ssq_ready.wait(pool, g, i + 1)
                    pool_steps.link(pool, g, pool.tensor_tensor(rnorm[:, p, :], ssqc[:, p, :], minus_half[:, :],
                                                                ALU.pow))
                banks.wait_read(pool, g, (("q", "k")[part], l, b))
                pool_steps.link(pool, g, pool.tensor_tensor(t_cos[:, p, part, :], t_cos[:, p, part, :],
                                                            t_sin[:, p, part, :], ALU.add))
                if i >= 2:
                    banks.wait_read(pool, g, (("qT", "kT")[part], i - 2))
                qk_ready.raised_by(pool.tensor_tensor(
                    qk[:, p, part, :].rearrange("p (h d) -> p h d", h=HEADS),
                    t_cos[:, p, part, :].rearrange("p (h d) -> p h d", d=DH),
                    rnorm[:, p, part * HEADS:(part + 1) * HEADS].unsqueeze(2).to_broadcast([128, HEADS, DH]),
                    ALU.mult))

            def with_first_residual(g, l, pair):
                if l == 0:
                    hbanks.wait_read(pool, g, ("down", 0, pair))
                    a, b = 2 * pair, 2 * pair + 2
                    xs_ready.raised_by(pool.tensor_tensor(xs[:, a:b, :], x1[:, a:b, :], y0[:, a:b, :], ALU.add))

            def difference(g):
                fbanks.wait_read(pool, g, "s2c")
                diff_ready.raised_by(pool.tensor_tensor(mix[:, 0, :, :], c2sT[:, :, :], s2cT[:, :, :],
                                                        ALU.subtract))

            work = {
                "agg": lambda g: deviation(g, 1, var_ready, vareps, rstd, rstd_ready, 0, NB),
                "rot": rotated,
                "hs": lambda g, l, pair: deviation(g, PAIRS * l + pair + 1, hvar_ready, hvareps, hrstd,
                                                   hrstd_ready, 2 * pair, 2 * pair + 2),
                "down": with_first_residual,
                "z_moments": lambda g: deviation(g, 1, fvar_ready, fvareps, frstd, frstd_ready, 0, NB),
                "s2c": difference,
                "mixT": lambda g: deviation(g, 2, fvar_ready, fvareps, frstd, frstd_ready, 0, NB)}

            def group_turn(ga, gb):
                pool_steps.n = 0
                for part, name, *args in schedule():
                    before = part == "fin" or part == "ff" and tuple(args[0:2]) == (LAYERS - 1, PAIRS - 1)
                    g = gb if before else ga
                    if g is not None and name in work:
                        work[name](g, *args)
                assert ga is None or pool_steps.n == POOL_STEPS, pool_steps.n

            group_turn(0, None)
            with pool.Fori(0, NG - 1) as g:
                group_turn(g + 1, g)
            group_turn(None, NG - 1)

        @block.vector
        def _(dve):
            def link0(ins):
                prep_dve.n += 1
                ins.then_inc(prep_dve.sem, 1)
                dve.wait_ge(prep_dve.sem, prep_dve.n)

            dve.wait_ge(c_loaded, 16)
            dve.wait_ge(w_loaded, 16 * weight_loads[0])
            dve.wait_ge(pool_set, 1)
            dve.tensor_copy(ident_b[:, :], ident)
            dve.tensor_copy(mask_b[:, :, :], const("mask").unsqueeze(1).to_broadcast([128, HALF, 128]))
            dve.tensor_copy(bv_cols[:, :], corr_bv[:, 0:1].to_broadcast([128, S]))
            table = const("rope").rearrange("p (a c d) -> p a c d", a=2, c=2)
            for l in range(LAYERS):
                for part in range(2):
                    dve.tensor_tensor(rope[:, l, part, 0, :], table[:, part, 0, :], scales[:, part, l, :],
                                      ALU.mult)
                    dve.tensor_tensor(
                        rope[:, l, part, 1, :].rearrange("p (c d) -> p c d", c=2),
                        table[:, part, 1, :].rearrange("p (c d) -> p c d", c=2),
                        scales[:, part, l, :].rearrange("p (c d) -> p c d", c=2)[:, ::-1, :], ALU.mult)
                dve.tensor_scalar(w1g[:, l, :], w1[:, l, :], lngb[:, 0, l:l + 1], None, ALU.mult)
            dve.tensor_scalar(cbs[:, 0:1], cb[:, 0:1], CORR_SCALE, None, ALU.mult)
            dve.tensor_scalar(cbs[:, 1:2], cb[:, 3:4], CORR_SCALE, None, ALU.mult)
            dve.tensor_scalar(cbs[:, 2:3], cb[:, 6:7], 0.5, None, ALU.mult)
            link0(dve.tensor_copy(conv_parts[:, 0, :], conv_b[:, :]))
            link0(dve.tensor_tensor(conv_tmp[:, 0, :], conv_b[:, :], conv_parts[:, 0, :], ALU.subtract))
            link0(dve.tensor_copy(conv_parts[:, 1, :], conv_tmp[:, 0, :]))
            link0(dve.tensor_tensor(conv_tmp[:, 1, :], conv_tmp[:, 0, :], conv_parts[:, 1, :], ALU.subtract))
            link0(dve.tensor_copy(conv_parts[:, 2, :], conv_tmp[:, 1, :]))
            for n, w in enumerate((q1, q2)):
                last = dve.tensor_reduce(qsum[:, n:n + 1], w, AX.X,
                                         ALU.add, apply_absolute_value=True)
            link0(last)
            dve.wait_ge(prep_pe, 1)
            link0(dve.tensor_scalar(qscale[:, 0:2], psum[0][:, 0:2], 1.0 / (DHID * D), 1e-5, ALU.mult, ALU.max))
            link0(dve.reciprocal(qscale[:, 2:4], qscale[:, 0:2]))
            for n, w in enumerate((q1, q2)):
                link0(dve.tensor_scalar(w, w, qscale[:, 2 + n:3 + n], MAGIC, ALU.mult, ALU.add))
                link0(dve.tensor_scalar(w, w, MAGIC, 1.0, ALU.subtract, ALU.min))
            link0(dve.tensor_scalar(q1, q1, -1.0, None, ALU.max))
            dve.tensor_scalar(q2T[:, :, :].rearrange("p a o -> p (a o)"), q2, -1.0, None, ALU.max)
            dve.tensor_scalar(qscale[:, 4:5], qscale[:, 1:2], 1.0 / 127.0, None, ALU.mult)
            link0(dve.tensor_scalar(conv_w, conv_w, qscale[:, 0:1], None, ALU.mult))
            for k in range(3):
                dve.tensor_tensor(wc[:, k, :], q1, conv_w[:, k, :], ALU.mult)
            dve.wait_ge(prep_pe, 2)
            dve.tensor_copy(bias_f[:, :, :].rearrange("p a o -> p (a o)"), psum[6][:, 0:256])
            for l in range(LAYERS):
                for part in range(2):
                    at = 6 * l + 3 * part
                    dve.tensor_tensor(b1[:, l, part, 0:2], b1[:, l, part, 0:2],
                                      psum[7][:, at:at + 2], ALU.add)
                    last = dve.tensor_tensor(b1[0:HT[2], l, part, 2:3], b1[0:HT[2], l, part, 2:3],
                                             psum[7][0:HT[2], at + 2:at + 3], ALU.add)
            link0(last)
            dve.tensor_copy(wvo[:, :], psum[3][:, 0:128])
            link0(dve.tensor_copy(bvo[:, :], psum[3][0:S, 128:256]))
            prep_steps.append(prep_dve.n)

            with dve.Fori(0, NG) as g:
                f_chain.n = 0
                dve.wait_ge(f_loaded, g * 32 + 32)
                for b in range(NB):
                    last = dve.bn_stats(stats[:, b, :], x0[:, b, :])
                f_chain.link(dve, g, last)
                dve.memset(pause[:, :], 0.0)
                for b in range(NB):
                    last = dve.bn_aggr(meanvar[:, b, :], stats[:, b, :])
                f_chain.link(dve, g, last)
                dve.tensor_scalar(vareps[:, :], meanvar[:, :, 1], LN_EPS, None, ALU.add).then_inc(f_var, 1)
                dve.wait_ge(f_rstd, g + 1)
                for b in range(NB):
                    last = dve.tensor_scalar(xn[:, b, :], x0[:, b, :], meanvar[:, b, 0:1], rstd[:, b:b + 1],
                                             ALU.subtract, ALU.mult)
                last.then_inc(f_norm, 1)
                dve.wait_ge(f_proj, g + 1)
                dve.tensor_tensor(spec_q[:, :, :], psum[2][:, :].rearrange("p (b c) -> p b c", b=NB),
                                  bias_f[:, 0, :].unsqueeze(1).to_broadcast([128, NB, 128]), ALU.add)
                f_chain.link(dve, g, dve.tensor_tensor(
                    spec_k[:, :, :], psum[3][:, :].rearrange("p (b c) -> p b c", b=NB),
                    bias_f[:, 1, :].unsqueeze(1).to_broadcast([128, NB, 128]), ALU.add))
                f_chain.link(dve, g, dve.tensor_tensor(spec_junk[:, :, :], spec_q[:, :, :], spec_k[:, :, :],
                                                       ALU.mult))
                dve.tensor_reduce(spec[:, bass.ds(g * NB, NB)], spec_junk[:, :, :], AX.X,
                                  ALU.add).then_inc(s_spec, 1)
            dve.wait_ge(s_corr, 1)
            link0(dve.tensor_copy(corr[:, :], psum[0][0:B, 0:128]))
            link0(dve.max(top8[:, 0, :], corr[:, :]))
            link0(dve.match_replace(left[:, 0, :], top8[:, 0, :], corr[:, :], -3.0e38))
            link0(dve.max(top8[:, 1, :], left[:, 0, :]))
            link0(dve.memset(top8[:, 2, :], -3.0e38))
            link0(dve.tensor_copy(top8[:, 2, 0:TOPK - 8], top8[:, 1, 0:TOPK - 8]))
            link0(dve.match_replace(left[:, 1, :], top8[:, 2, :], left[:, 0, :], -3.0e38))
            dve.tensor_scalar(corr_s[:, 0:1], top8[:, 0, 0:1], -1.0, None, ALU.mult).then_inc(s_shift, 1)
            dve.wait_ge(s_exp, 1)
            link0(dve.scalar_tensor_tensor(corr_e[:, 1, :], left[:, 1, :], -2.9e38, corr_e[:, 0, :],
                                           ALU.is_le, ALU.mult))
            link0(dve.tensor_reduce(corr_s[:, 1:2], corr_e[:, 1, :], AX.X, ALU.add))
            link0(dve.reciprocal(corr_s[:, 2:3], corr_s[:, 1:2]))
            dve.tensor_scalar(delay_w[:, :, :], corr_e[:, 1, ::-1].unsqueeze(1).to_broadcast([B, 2, 128]),
                              corr_s[:, 2:3], None, ALU.mult).then_inc(s_delay, 1)

            def moments(g, src, chain, st, mv, ve, ready, batches=range(NB)):
                for b in batches:
                    last = dve.bn_stats(st[:, b, :], src(b))
                chain.link(dve, g, last)
                dve.memset(pause[:, :], 0.0)
                for b in batches:
                    last = dve.bn_aggr(mv[:, b, :], st[:, b, :])
                chain.link(dve, g, last)
                ready.raised_by(dve.tensor_scalar(ve[:, batches[0]:batches[-1] + 1],
                                                  mv[:, batches[0]:batches[-1] + 1, 1], LN_EPS, None, ALU.add))

            def normalise(g, n, src, dst, mv, rs, rs_ready, batches=range(NB)):
                rs_ready.wait(dve, g, n)
                for b in batches:
                    last = dve.tensor_scalar(dst[:, b, :], src(b), mv[:, b, 0:1], rs[:, b:b + 1],
                                             ALU.subtract, ALU.mult)
                return last

            def context_values(g):
                banks.wait_filled(dve, g, "vprime")
                u = banks["vprime"]
                ins = dve.tensor_tensor(vprime[0:S, :, :], u[0:S, :].rearrange("p (b e) -> p b e", b=NB),
                                        bvo[:, :].unsqueeze(1).to_broadcast([S, NB, 128]), ALU.add)
                banks.frees("vprime", ins)

            def correlated(g):
                banks.wait_filled(dve, g, "agg")
                x_loaded.wait(dve, g, 1)
                ins = dve.tensor_tensor(x1[:, :, :].rearrange("p b d -> p (b d)"), banks["agg"][:, :],
                                        x0[:, :, :].rearrange("p b d -> p (b d)"), ALU.add)
                banks.frees("agg", ins)
                banks.wait_read(dve, g, "agg")
                moments(g, lambda b: x1[:, b, :], steps, stats, meanvar, vareps, var_ready)
                y_ready.raised_by(normalise(g, 1, lambda b: x1[:, b, :], y0, meanvar, rstd, rstd_ready))

            def rotary(g, i, part):
                (l, b), p = divmod(i, NB), i % 2
                if part == 0:
                    sq_ready.wait(dve, g, 2 * i + 2)
                    steps.link(dve, g, dve.tensor_reduce(
                        ssq[:, p, :], sq[:, p, :, :].rearrange("p a (h d) -> p (a h) d", h=HEADS), AX.X, ALU.add))
                    if i >= 2:
                        qk_ready.wait(dve, g, 2 * i - 2)
                    ssq_ready.raised_by(dve.tensor_scalar(ssqc[:, p, :], ssq[:, p, :], 1e-24, None, ALU.max))
                name = ("q", "k")[part]
                banks.wait_filled(dve, g, (name, l, b))
                u = banks[(name, l, b)]
                cos = rope[:, l, part, 0, :].unsqueeze(1).to_broadcast([128, HEADS, DH])
                sin = rope[:, l, part, 1, :].rearrange("p (c d) -> p c d", c=2)\
                    .unsqueeze(1).to_broadcast([128, HEADS, 2, DH // 2])
                dve.tensor_tensor(t_cos[:, p, part, :].rearrange("p (h d) -> p h d", d=DH),
                                  u[:, :].rearrange("p (h d) -> p h d", d=DH), cos, ALU.mult)
                ins = dve.tensor_tensor(
                    t_sin[:, p, part, :].rearrange("p (h c d) -> p h c d", c=2, d=DH // 2),
                    u[:, :].rearrange("p (h c d) -> p h c d", c=2, d=DH // 2)[:, :, ::-1, :], sin, ALU.mult)
                banks.frees((name, l, b), ins)

            def largest(g, i, s):
                banks.wait_filled(dve, g, ("sim", i, s))
                nmax_ready.raised_by(dve.tensor_reduce(
                    nmax[:, i % 2, HALF * s:HALF * s + HALF],
                    banks[("sim", i, s)][:, :].rearrange("p (h j) -> p h j", h=HALF), AX.X, ALU.max, negate=True))

            def outputs(g, i, s):
                p = i % 2
                banks.wait_filled(dve, g, ("o", i, s))
                u = banks[("o", i, s)][:, 0:HALF * (DH + 1)].rearrange("p (h d) -> p h d", h=HALF)
                steps.link(dve, g, dve.reciprocal(rsum[:, p, HALF * s:HALF * s + HALF], u[:, :, DH]))
                ins = dve.tensor_tensor(
                    o[:, p, s::2, :], u[:, :, 0:DH],
                    rsum[:, p, HALF * s:HALF * s + HALF].unsqueeze(2).to_broadcast([128, HALF, DH]), ALU.mult)
                banks.frees(("o", i, s), ins)

            def attended(g, i):
                l, b = divmod(i, NB)
                banks.wait_filled(dve, g, ("wo", i))
                u = banks[("wo", i)][:, 0:128]
                if l == LAYERS - 1:
                    xs_ready.wait(dve, g, b // 2 + 1)
                    dve.tensor_tensor(xs[:, b, :], u, xs[:, b, :], ALU.add)
                ins = dve.tensor_tensor(y1[:, b, :], u, y0[:, b, :], ALU.add)
                banks.frees(("wo", i), ins)

            def shifted_norm(g, l, pair):
                hsteps.n = 2 * (PAIRS * l + pair)
                batches = range(2 * pair, 2 * pair + 2)
                hbanks.wait_filled(dve, g, ("hs", l, pair))

                def src(b):
                    return hbanks[("hs", l, pair)][:, (b % 2) * 128:(b % 2) * 128 + 128]

                moments(g, src, hsteps, hstats, hmeanvar, hvareps, hvar_ready, batches)
                hbanks.frees(("hs", l, pair), normalise(g, PAIRS * l + pair + 1, src, xn, hmeanvar, hrstd,
                                                        hrstd_ready, batches))

            def gated_hidden(g, l, pair, j):
                rows, a = HT[j], 256 * pair
                name = ("gu", l, pair, j)
                gel_ready.wait(dve, g, 3 * (PAIRS * l + pair) + j + 1)
                ins = dve.scalar_tensor_tensor(
                    hid[0:rows, j, a:a + 256], hbanks[name][0:rows, 256:512], b1[0:rows, l, 0, j:j + 1],
                    gel[0:rows, j, a:a + 256], ALU.add, ALU.mult)
                hbanks.frees(name, ins)

            def stack_output(g, l, pair):
                name, a, b = ("down", l, pair), 2 * pair, 2 * pair + 2
                hbanks.wait_filled(dve, g, name)
                dst, src = (y0, y1) if l < LAYERS - 1 else (x2, xs)
                ins = dve.tensor_tensor(dst[:, a:b, :].rearrange("p b d -> p (b d)"), hbanks[name][:, 0:256],
                                        src[:, a:b, :].rearrange("p b d -> p (b d)"), ALU.add)
                hbanks.frees(name, ins)

            def z_moments(g):
                hbanks.wait_read(dve, g, ("down", LAYERS - 1, PAIRS - 1))
                moments(g, lambda b: x2[:, b, :], fsteps, fstats, fmeanvar, fvareps, fvar_ready)

            def cross_tokens(g):
                z_ready.raised_by(normalise(g, 1, lambda b: x2[:, b, :], zn, fmeanvar, frstd, frstd_ready))

            def largest_scores(g, n):
                name, rows, keys = (("s1", 128, S), ("s2", S, 128))[n]
                fbanks.wait_filled(dve, g, name)
                cmax_ready.raised_by(dve.tensor_reduce(
                    nm1[0:rows, n, :], fbanks[name][0:rows, 0:NB * keys].rearrange("p (b j) -> p b j", b=NB),
                    AX.X, ALU.max, negate=True))

            def probabilities(g, n):
                p, rows, keys = ((p1, 128, S), (p2, S, 128))[n]
                fbanks.wait_read(dve, g, ("s1", "s2")[n])
                fsteps.link(dve, g, dve.tensor_reduce(amax[0:rows, 2 * n, :], p[:, :, :], AX.X, ALU.add))
                fsteps.link(dve, g, dve.reciprocal(amax[0:rows, 2 * n + 1, :], amax[0:rows, 2 * n, :]))
                cprob_ready.raised_by(dve.tensor_tensor(
                    p[:, :, :], p[:, :, :],
                    amax[0:rows, 2 * n + 1, :].unsqueeze(2).to_broadcast([rows, NB, keys]), ALU.mult))

            def gated_sum(g):
                fbanks.wait_read(dve, g, "g")
                diff_ready.wait(dve, g, 1)
                fsteps.link(dve, g, dve.scalar_tensor_tensor(mix[:, 1, :, :], gt[:, :, :], 1.0, mix[:, 0, :, :],
                                                            ALU.add, ALU.mult))
                mix_ready.raised_by(dve.scalar_tensor_tensor(gt[:, :, :], mix[:, 1, :, :], 0.5, s2cT[:, :, :],
                                                             ALU.mult, ALU.add))

            def mixed(g):
                fbanks.wait_filled(dve, g, "mixT")
                x3_stored.wait(dve, g, 1)
                ins = dve.tensor_tensor(x3[:, :, :].rearrange("p b d -> p (b d)"), fbanks["mixT"][:, :],
                                        x2[:, :, :].rearrange("p b d -> p (b d)"), ALU.add)
                fbanks.frees("mixT", ins)
                fbanks.wait_read(dve, g, "mixT")
                moments(g, lambda b: x3[:, b, :], fsteps, fstats, fmeanvar, fvareps, fvar_ready)

            def token_scales(g, am):
                fsteps.link(dve, g, dve.tensor_scalar(am[:, 0, :], am[:, 0, :], 1e-5, None, ALU.max))
                fsteps.link(dve, g, dve.reciprocal(am[:, 2, :], am[:, 0, :]))
                dve.tensor_scalar(am[:, 1, :], am[:, 2, :], 127.0, None, ALU.mult)

            def quantised_tokens(g):
                fsteps.link(dve, g, normalise(g, 2, lambda b: x3[:, b, :], zn, fmeanvar, frstd, frstd_ready))

                fsteps.link(dve, g, dve.tensor_reduce(amax[:, 0, :], zn[:, :, :], AX.X, ALU.max,
                                                     apply_absolute_value=True))
                token_scales(g, amax)
                fsteps.link(dve, g, dve.tensor_scalar(amax[:, 3, :], amax[:, 0, :], 1.0 / 127.0, None, ALU.mult))
                for b in range(NB):
                    last = dve.tensor_scalar(yq[:, b, :], zn[:, b, :], amax[:, 1, b:b + 1], MAGIC,
                                             ALU.mult, ALU.add)
                fsteps.link(dve, g, last)
                for b in range(NB):
                    last = dve.tensor_scalar(yd[:, b, :], yq[:, b, :], MAGIC, amax[:, 3, b:b + 1],
                                             ALU.subtract, ALU.mult)
                yd_ready.raised_by(last)

            def quantised_hidden(g, b):
                p = b % 2
                am = amax2[:, :, b:b + 1]
                fbanks.wait_read(dve, g, ("h", b))
                fsteps.link(dve, g, dve.tensor_reduce(am[:, 0, :], sil[:, p, :], AX.X, ALU.max,
                                                     apply_absolute_value=True))
                token_scales(g, am)
                fsteps.link(dve, g, dve.tensor_scalar(am[:, 3, :], am[:, 0, :], qscale[:, 4:5], None, ALU.mult))
                fsteps.link(dve, g, dve.tensor_scalar(silq[:, p, :], sil[:, p, :], am[:, 1, :], MAGIC,
                                                     ALU.mult, ALU.add))
                silq_ready.raised_by(dve.tensor_scalar(silb[:, p, :], silq[:, p, :], MAGIC, 127.0,
                                                       ALU.subtract, ALU.min))

            def result(g):
                fbanks.wait_filled(dve, g, "ffn")
                for b in range(NB):
                    last = dve.scalar_tensor_tensor(x3[:, b, :], fbanks["ffn"][:, b * 128:b * 128 + 128],
                                                    amax2[:, 3, b:b + 1], x3[:, b, :], ALU.mult, ALU.add)
                fbanks.frees("ffn", last)

            work = {
                "vprime": context_values, "agg": correlated, "rot": rotary, "sm": largest, "o": outputs,
                "wo": attended, "hs": shifted_norm, "gu": gated_hidden, "down": stack_output,
                "z_moments": z_moments, "zn": cross_tokens,
                "s1": lambda g: largest_scores(g, 0), "s2": lambda g: largest_scores(g, 1),
                "p1": lambda g: probabilities(g, 0), "p2": lambda g: probabilities(g, 1),
                "mix": gated_sum, "mixT": mixed, "quant": quantised_tokens, "hq": quantised_hidden,
                "ffn": result}

            def group_turn(ga, gb):
                steps.n = fsteps.n = 0
                for part, name, *args in schedule():
                    before = part == "fin" or part == "ff" and tuple(args[0:2]) == (LAYERS - 1, PAIRS - 1)
                    g = gb if before else ga
                    if g is not None and name in work:
                        work[name](g, *args)
                assert ga is None or steps.n == VECTOR_STEPS, steps.n
                assert gb is None or fsteps.n == FINISH_STEPS, fsteps.n

            group_turn(0, None)
            with dve.Fori(0, NG - 1) as g:
                group_turn(g + 1, g)
            group_turn(None, NG - 1)

        @block.scalar
        def _(act):
            act.wait_ge(prep_dve.sem, 5)
            for n in range(3):
                act.dma_start(conv_b3[n:n + 1, :], conv_parts[:, n, :]).then_inc(conv_loaded, 16)
            with act.Fori(0, NG) as g:
                act.wait_ge(f_spec, g + 2)
                act.activation(spec_t[:, 0, :, :].rearrange("p b f -> p (b f)"), psum[0][:, :], ACT.Copy)
                act.activation(spec_t[:, 1, :, :].rearrange("p b f -> p (b f)"), psum[1][:, :],
                               ACT.Copy).then_inc(f_copied, 1)
            act.wait_ge(s_shift, 1)
            act.activation(corr_e[:, 0, :], corr[:, :], ACT.Exp, bias=corr_s[:, 0:1]).then_inc(s_exp, 1)

            def copy(g, bk, name, dst, rows=128, cols=512):
                bk.wait_filled(act, g, name)
                ins = act.activation(dst, bk[name][0:rows, 0:cols], ACT.Copy)
                bk.frees(name, ins)

            def tokens_in(g, l, pair):
                name, a, b = ("yT", l, pair), 2 * pair, 2 * pair + 2
                banks.wait_filled(act, g, name)
                u = banks[name]
                act.activation(yT[0:64, a:b, :].rearrange("p b t -> p (b t)"), u[0:64, 0:256], ACT.Copy)
                ins = act.activation(yT[64:128, a:b, 1:T],
                                     u[64:128, 0:256].rearrange("p (b t) -> p b t", b=2)[:, :, 0:T - 1], ACT.Copy)
                banks.frees(name, ins)

            def squares(g, i):
                (l, b), p = divmod(i, NB), i % 2
                if i >= 2:
                    ssq_ready.wait(act, g, i - 1)
                for part, name in enumerate(("q", "k")):
                    banks.wait_filled(act, g, (name, l, b))
                    sq_ready.raised_by(act.activation(sq[:, p, part, :], banks[(name, l, b)][:, :], ACT.Square))
                banks.wait_filled(act, g, ("v", l, b))
                ins = act.activation(vx[:, b, :, 0:DH],
                                     banks[("v", l, b)][:, :].rearrange("p (h d) -> p h d", h=HEADS), ACT.Copy)
                banks.frees(("v", l, b), ins)

            def turned(g, i):
                copy(g, banks, ("qT", i), qT[:, i % 2, :, :].rearrange("p a t -> p (a t)"))
                copy(g, banks, ("kT", i), kT[:, i % 2, :, :].rearrange("p a t -> p (a t)"))

            def weights(g, i, s):
                p = i % 2
                nmax_ready.wait(act, g, 2 * i + s + 1)
                for h in range(HALF):
                    ins = act.activation(prob[:, p, s, h, :], banks[("sim", i, s)][:, h * 128:h * 128 + 128],
                                         ACT.Exp, bias=nmax[:, p, HALF * s + h:HALF * s + h + 1])
                banks.frees(("sim", i, s), ins)

            def weights_turned(g, i):
                for s in range(2):
                    copy(g, banks, ("pT", i, s), probT[:, s, :, :].rearrange("p h i -> p (h i)"))

            def out_turned(g, i):
                copy(g, banks, ("oT", i), oT[:, i % 2, :, :].rearrange("p a t -> p (a t)"))

            def hidden_in(g, l, pair):
                copy(g, hbanks, ("hT", l, pair), zT[:, 2 * pair:2 * pair + 2, :].rearrange("p b t -> p (b t)"),
                     cols=256)

            def gates(g, l, pair, j):
                rows, a = HT[j], 256 * pair
                hbanks.wait_filled(act, g, ("gu", l, pair, j))
                gel_ready.raised_by(act.activation(
                    gel[0:rows, j, a:a + 256], hbanks[("gu", l, pair, j)][0:rows, 0:256], ACT.Gelu,
                    bias=b1[0:rows, l, 1, j:j + 1]))

            def shifted_copy(g, name, dst, bias, cols=512, scale=1.0):
                fbanks.wait_filled(act, g, name)
                ins = act.activation(dst.rearrange("p b t -> p (b t)"), fbanks[name][:, 0:cols], ACT.Identity,
                                     bias=bias, scale=scale)
                fbanks.frees(name, ins)

            def exponentials(g, n):
                name, p, rows, keys = (("s1", p1, 128, S), ("s2", p2, S, 128))[n]
                cmax_ready.wait(act, g, n + 1)
                for b in range(NB):
                    ins = act.activation(p[:, b, :], fbanks[name][0:rows, b * keys:(b + 1) * keys], ACT.Exp,
                                         bias=nm1[0:rows, n, b:b + 1])
                fbanks.frees(name, ins)

            def gate(g):
                fbanks.wait_filled(act, g, "g")
                ins = act.activation(gt[:, :, :].rearrange("p b t -> p (b t)"), fbanks["g"][:, :], ACT.Tanh,
                                     bias=cbs[:, 2:3], scale=0.5)
                fbanks.frees("g", ins)

            def quantised_turned(g):
                fbanks.wait_filled(act, g, "dT")
                ins = act.activation(ydT[:, :, 1:T + 1], fbanks["dT"][:, :].rearrange("p (b t) -> p b t", b=NB),
                                     ACT.Copy)
                fbanks.frees("dT", ins)

            def hidden_turned(g, b):
                fbanks.wait_filled(act, g, ("hqT", b))
                ins = act.activation(silT[:, b, :, :].rearrange("p a t -> p (a t)"),
                                     fbanks[("hqT", b)][:, :].bitcast(BF16)[:, 0:512], ACT.Copy)
                fbanks.frees(("hqT", b), ins)

            def hidden(g, b):
                fbanks.wait_filled(act, g, ("h", b))
                if b >= 2:
                    silq_ready.wait(act, g, b - 1)
                ins = act.activation(sil[:, b % 2, :], fbanks[("h", b)][:, :], ACT.Silu)
                fbanks.frees(("h", b), ins)

            def flat(t):
                return t[:, :, :].rearrange("p b t -> p (b t)")

            work = {
                "yT": tokens_in, "qkv": squares, "turns": turned, "sm": weights, "pT": weights_turned,
                "oT": out_turned, "hT": hidden_in, "gu": gates,
                "zT": lambda g: copy(g, fbanks, "zT", flat(znT)),
                "qc": lambda g: shifted_copy(g, "qc", qcT, cbs[:, 0:1], scale=CORR_SCALE),
                "ks": lambda g: shifted_copy(g, "ks", ksT, cb[:, 1:2], cols=NB * S),
                "vs": lambda g: copy(g, fbanks, "vs", flat(vs), rows=S),
                "qs": lambda g: shifted_copy(g, "qs", qsT, cbs[:, 1:2], cols=NB * S, scale=CORR_SCALE),
                "kc": lambda g: shifted_copy(g, "kc", kcT, cb[:, 4:5]),
                "vc": lambda g: copy(g, fbanks, "vc", flat(vc)),
                "s1": lambda g: exponentials(g, 0), "s2": lambda g: exponentials(g, 1),
                "p1T": lambda g: copy(g, fbanks, "p1T", flat(p1T), rows=S),
                "c2s": lambda g: shifted_copy(g, "c2s", c2sT, cb[:, 2:3]),
                "a": lambda g: copy(g, fbanks, "a", flat(aT)),
                "s2c": lambda g: shifted_copy(g, "s2c", s2cT, cb[:, 5:6]),
                "g": gate, "dT": quantised_turned, "h": hidden, "hqT": hidden_turned}

            def group_turn(ga, gb):
                for part, name, *args in schedule():
                    before = part == "fin" or part == "ff" and tuple(args[0:2]) == (LAYERS - 1, PAIRS - 1)
                    g = gb if before else ga
                    if g is not None and name in work:
                        work[name](g, *args)

            group_turn(0, None)
            with act.Fori(0, NG - 1) as g:
                group_turn(g + 1, g)
            group_turn(None, NG - 1)

        @block.tensor
        def _(pe):
            pe.wait_ge(pool_set, 1)
            pe.wait_ge(c_loaded, 16)
            pe.wait_ge(w_loaded, 16 * weight_loads[0])
            pe.wait_ge(prep_dve.sem, 6)
            pe.matmul(psum[0][:, 0:2], ones[:, :], qsum[:, :], start=True, stop=True).then_inc(prep_pe, 1)
            sums = const("sums", 1)
            for n in range(2):
                pe.matmul(psum[6][:, n * 128:n * 128 + 128], sums[:, n * 128:n * 128 + 128],
                          corr_rows[:, n, :], start=True, stop=True)
            for l in range(LAYERS):
                for part in range(2):
                    for j in range(3):
                        at, c = part * HID + j * 128, 6 * l + 3 * part + j
                        ins = pe.matmul(psum[7][0:HT[j], c:c + 1], w1[:, l, at:at + HT[j]], lngb[:, 1, l:l + 1],
                                        start=True, stop=True)
            pe.matmul(psum[3][:, 0:128], corr_w[:, 2, :], corr_w[:, 3, :], start=True, stop=True)
            pe.matmul(psum[3][0:S, 128:256], bv_cols[:, :], corr_w[:, 3, :], start=True,
                      stop=True).then_inc(prep_pe, 1)
            pe.wait_ge(prep_dve.sem, prep_steps[0])

            dft = const("dft")
            with pe.Fori(0, NG) as g:
                pe.wait_ge(f_norm, g + 1)
                for b in range(NB):
                    pe.matmul(psum[0][:, b * 128:b * 128 + 128], xn[:, b, :], dft, start=True, stop=True)
                    ins = pe.matmul(psum[1][:, b * 128:b * 128 + 128], ctx[:, b, :], dft[0:S, :], start=True,
                                    stop=True)
                ins.then_inc(f_spec, 1)
                pe.wait_ge(f_copied, g + 1)
                pe.wait_ge(s_spec, g + 1)
                for b in range(NB):
                    pe.matmul(psum[2][:, b * 128:b * 128 + 128], spec_t[:, 0, b, :], corr_w[:, 0, :], start=True,
                              stop=True)
                    ins = pe.matmul(psum[3][:, b * 128:b * 128 + 128], spec_t[:, 1, b, :], corr_w[:, 1, :],
                                    start=True, stop=True)
                ins.then_inc(f_proj, 1)
            pe.wait_ge(s_spec, NG + 1)
            pe.matmul(psum[0][0:B, 0:128], spec[:, :], const("inverse_dft"), start=True,
                      stop=True).then_inc(s_corr, 1)
            pe.wait_ge(s_delay, 1)
            pe.wait_ge(conv_loaded, 48)

            def turn(g, bk, name, parts, rows=128, width=128, idn=None, dt=None, read=()):
                bk.wait_for(pe, g, name, read)
                u = bk[name] if dt is None else bk[name][:, :].bitcast(dt)
                for n, part in enumerate(parts):
                    ins = pe.transpose(u[0:rows, n * width:(n + 1) * width], part,
                                       (ident if idn is None else idn)[0:width, 0:width])
                bk.fills(name, ins)

            def whole(g, bk, name, pairs, rows=128, cols=512, read=()):
                bk.wait_for(pe, g, name, read)
                for n, (lhsT, rhs) in enumerate(pairs):
                    ins = pe.matmul(bk[name][0:rows, 0:cols], lhsT, rhs, start=(n == 0),
                                    stop=(n == len(pairs) - 1))
                bk.fills(name, ins)

            def each(g, bk, name, products, rows=128, width=128, read=()):
                bk.wait_for(pe, g, name, read)
                for m, pairs in enumerate(products):
                    for n, (lhsT, rhs) in enumerate(pairs):
                        ins = pe.matmul(bk[name][0:rows, m * width:(m + 1) * width], lhsT, rhs,
                                        start=(n == 0), stop=(n == len(pairs) - 1))
                bk.fills(name, ins)

            def context_values(g):
                ctx_loaded.wait(pe, g, 1)
                each(g, banks, "vprime", [[(ctxT[:, b, :], wvo[:, :])] for b in range(NB)], rows=S)

            def correlated(g):
                hank_loaded.wait(pe, g, 1)
                each(g, banks, "agg", [[(hank[:, b, :], vprime[:, b, :])] for b in range(NB)], read=["vprime"])

            def tokens_in(g, l, pair):
                if l:
                    hbanks.wait_read(pe, g, ("down", l - 1, pair))
                else:
                    y_ready.wait(pe, g, 1)
                turn(g, banks, ("yT", l, pair), [y0[:, b, :] for b in range(2 * pair, 2 * pair + 2)])

            def qkv(g, i):
                l, b = divmod(i, NB)
                for n, name in enumerate(("q", "k", "v")):
                    whole(g, banks, (name, l, b), [(yT[:, b, :], wqkv[:, l, n * INNER:(n + 1) * INNER])],
                          read=[("yT", l, b // 2)] if n == 0 else ())

            def turns(g, i):
                for n, name in enumerate(("qT", "kT")):
                    qk_ready.wait(pe, g, 2 * i + n + 1)
                    turn(g, banks, (name, i), [qk[:, i % 2, n, a * 128:a * 128 + 128] for a in range(4)])

            def scores(g, i):
                names = [("sim", i, s) for s in range(2)]
                for s, name in enumerate(names):
                    banks.wait_for(pe, g, name, [("qT", i), ("kT", i)] if s == 0 else ())
                    pe.matmul(banks[name][:, :], ident_b[:, :], mask_b[:, :, :].rearrange("p h j -> p (h j)"),
                              start=True, stop=False, skip_group_check=True)
                for h in range(HALF):
                    for s, name in enumerate(names):
                        ins = pe.matmul(banks[name][:, h * 128:h * 128 + 128],
                                        qT[64 * s:64 * s + 64, i % 2, h, :],
                                        kT[64 * s:64 * s + 64, i % 2, h, :], start=False,
                                        stop=(h == HALF - 1), skip_group_check=True)
                        if h == HALF - 1:
                            banks.fills(name, ins)

            def weights_turned(g, i):
                for s in range(2):
                    turn(g, banks, ("pT", i, s), [prob[:, i % 2, s, h, :] for h in range(HALF)],
                         read=[("sim", i, s)])

            def weighted(g, i, s):
                l, b = divmod(i, NB)
                each(g, banks, ("o", i, s), [[(probT[:, s, h, :], vx[:, b, 2 * h + s, :])]
                                             for h in range(HALF)],
                     width=DH + 1, read=[("v", l, b), ("pT", i, s)])

            def out_turned(g, i):
                turn(g, banks, ("oT", i), [o[:, i % 2, 2 * a:2 * a + 2, :].rearrange("p h d -> p (h d)")
                                           for a in range(4)], read=[("o", i, 0), ("o", i, 1)])

            def project(g, i):
                whole(g, banks, ("wo", i), [(oT[:, i % 2, a, :], wo[:, i // NB, a, :]) for a in range(4)],
                      cols=128, read=[("oT", i)])

            def shift_tokens(g, l, pair):
                banks.wait_for(pe, g, read=[("wo", NB * l + 2 * pair + n) for n in range(2)])
                hbanks.wait_for(pe, g, ("hs", l, pair))
                u = hbanks[("hs", l, pair)][:, 0:256].rearrange("p (b d) -> p b d", b=2)
                at = CONST_COLS["ident"][0]
                for n, eye in enumerate((ident, cst[:, at - 1:at + 127])):
                    d = slice(64 * n, 64 * n + 64)
                    ins = pe.matmul(u[:, :, d], eye, y1[:, 2 * pair:2 * pair + 2, d], start=True, stop=True)
                hbanks.fills(("hs", l, pair), ins)

            def hidden_in(g, l, pair):
                turn(g, hbanks, ("hT", l, pair), [xn[:, b, :] for b in range(2 * pair, 2 * pair + 2)],
                     read=[("hs", l, pair)])

            def gate_and_up(g, l, pair, j):
                name = ("gu", l, pair, j)
                hbanks.wait_for(pe, g, name, [("hT", l, pair)])
                tokens = zT[:, 2 * pair:2 * pair + 2, :].rearrange("p b t -> p (b t)")
                for n, part in enumerate((1, 0)):
                    at = part * HID + j * 128
                    ins = pe.matmul(hbanks[name][0:HT[j], 256 * n:256 * n + 256], w1g[:, l, at:at + HT[j]],
                                    tokens, start=True, stop=True)
                hbanks.fills(name, ins)

            def down(g, l, pair):
                k3 = HT[2] + 1
                each(g, hbanks, ("down", l, pair),
                     [[(hid[:, 0, b * 128:b * 128 + 128], w2[:, l, 0, :]),
                       (hid[:, 1, b * 128:b * 128 + 128], w2[:, l, 1, :]),
                       (hid[0:k3, 2, b * 128:b * 128 + 128], w2[0:k3, l, 2, :])]
                      for b in range(2 * pair, 2 * pair + 2)], read=[("gu", l, pair, j) for j in range(3)])

            def tokens_turned(g):
                z_ready.wait(pe, g, 1)
                turn(g, fbanks, "zT", [zn[:, b, :] for b in range(NB)])

            def token_features(g, name, n):
                whole(g, fbanks, name, [(cw[:, n, :], znT[:, :, :].rearrange("p b t -> p (b t)"))], read=["zT"])

            def context_features(g, name, n):
                ctxF_loaded.wait(pe, g, 1)
                whole(g, fbanks, name, [(cw[:, n, :], ctxF[:, :, :].rearrange("p b s -> p (b s)"))], cols=NB * S)

            def context_rows(g):
                ctxF_loaded.wait(pe, g, 1)
                each(g, fbanks, "vs", [[(ctxF[:, b, :], cw[:, 2, :])] for b in range(NB)], rows=S)

            def token_rows(g):
                each(g, fbanks, "vc", [[(znT[:, b, :], cw[:, 5, :])] for b in range(NB)], read=["zT"])

            def scores_s1(g):
                each(g, fbanks, "s1", [[(qcT[:, b, :], ksT[:, b, :])] for b in range(NB)], width=S,
                     read=["qc", "ks"])

            def scores_s2(g):
                each(g, fbanks, "s2", [[(qsT[:, b, :], kcT[:, b, :])] for b in range(NB)], rows=S,
                     read=["qs", "kc"])

            def probabilities_turned(g):
                cprob_ready.wait(pe, g, 1)
                turn(g, fbanks, "p1T", [p1[:, b, :] for b in range(NB)], rows=S)

            def context_weighted(g):
                each(g, fbanks, "c2s", [[(vs[:, b, :], p1T[:, b, :])] for b in range(NB)],
                     read=["p1T", "vs"])

            def interpolated(g):
                cprob_ready.wait(pe, g, 2)
                each(g, fbanks, "a", [[(p2[:, b, :], const("interp", S))] for b in range(NB)])

            def tokens_weighted(g):
                each(g, fbanks, "s2c", [[(vc[:, b, :], aT[:, b, :])] for b in range(NB)],
                     read=["a", "vc"])

            def gate(g):
                whole(g, fbanks, "g", [(cw[:, 6, :], c2sT[:, :, :].rearrange("p b t -> p (b t)")),
                                       (cw[:, 7, :], s2cT[:, :, :].rearrange("p b t -> p (b t)"))],
                      read=["c2s", "s2c"])

            def mixed_turned(g):
                mix_ready.wait(pe, g, 1)
                turn(g, fbanks, "mixT", [gt[:, b, :] for b in range(NB)])

            def quantised_turned(g):
                yd_ready.wait(pe, g, 1)
                turn(g, fbanks, "dT", [yd[:, b, :] for b in range(NB)])

            def hidden(g, b):
                whole(g, fbanks, ("h", b), [(ydT[:, b, k:k + T], wc[:, k, :]) for k in range(3)]
                      + [(ones3[:, :], conv_b3[:, :])], read=["dT"])

            def hidden_turned(g, b):
                silq_ready.wait(pe, g, b + 1)
                turn(g, fbanks, ("hqT", b), [silb[:, b % 2, a * 128:a * 128 + 128] for a in range(4)],
                     idn=ident_b, dt=BF16)

            def output(g):
                each(g, fbanks, "ffn", [[(silT[:, b, a, :], q2T[:, a, :]) for a in range(4)] for b in range(NB)],
                     read=[("hqT", b) for b in range(NB)])

            work = {
                "vprime": context_values, "agg": correlated, "yT": tokens_in, "qkv": qkv, "turns": turns,
                "scores": scores, "pT": weights_turned, "o": weighted, "oT": out_turned, "wo": project,
                "hs": shift_tokens, "hT": hidden_in, "gu": gate_and_up, "down": down,
                "zT": tokens_turned, "qc": lambda g: token_features(g, "qc", 0),
                "ks": lambda g: context_features(g, "ks", 1), "vs": context_rows,
                "qs": lambda g: context_features(g, "qs", 3), "kc": lambda g: token_features(g, "kc", 4),
                "vc": token_rows, "s1": scores_s1, "s2": scores_s2, "p1T": probabilities_turned,
                "c2s": context_weighted, "a": interpolated, "s2c": tokens_weighted, "g": gate,
                "mixT": mixed_turned, "dT": quantised_turned, "h": hidden, "hqT": hidden_turned, "ffn": output}

            def group_turn(ga, gb):
                for part, name, *args in schedule():
                    before = part == "fin" or part == "ff" and tuple(args[0:2]) == (LAYERS - 1, PAIRS - 1)
                    g = gb if before else ga
                    if g is not None and name in work:
                        work[name](g, *args)

            group_turn(0, None)
            with pe.Fori(0, NG - 1) as g:
                group_turn(g + 1, g)
            group_turn(None, NG - 1)


_INS = ['x', 'ctx', 'ctxT', 'constants', 'weights', 'rows']
_OUTS = [((B, T, D), 'float32')]


def kernel(**inputs):
    import numpy as _np
    import concourse.bacc as _bacc
    from concourse import mybir as _mybir
    from concourse.bass_utils import run_bass_kernel_spmd as _run

    nc = _bacc.Bacc("TRN2", target_bir_lowering=False, num_devices=1)
    arrays, args = {}, []
    given = {k: _np.asarray(v) for k, v in inputs.items()}
    laid = {'x': given['x'], 'ctx': given['ctx_1024'], 'ctxT': given['ctx_1024'][:, ::-1].transpose(2, 0, 1),
            'constants': constant_array(), 'weights': weight_array(given), 'rows': row_array(given)}
    for name in _INS:
        a = _np.ascontiguousarray(laid[name])
        arrays[f"in_{name}_dram"] = a
        args.append(nc.dram_tensor(f"in_{name}_dram", a.shape, _mybir.dt.from_np(a.dtype), kind="ExternalInput").ap())
    for i, (shape, dtype) in enumerate(_OUTS):
        dt = _mybir.dt.from_np(_np.dtype(dtype))
        args.append(nc.dram_tensor(f"out_{i}_dram", shape, dt, kind="ExternalOutput").ap())
    xattn_ffn_stack_kernel(nc, *args)
    r = _run(nc, [arrays], core_ids=[0])
    return r.results[0]["out_0_dram"]
```

```python
from contextlib import ExitStack

import numpy as np

import concourse.bass as bass
from concourse import mybir

F32 = mybir.dt.float32
BF16 = mybir.dt.bfloat16
ALU = mybir.AluOpType
ACT = mybir.ActivationFunctionType
AX = mybir.AxisListType

B, T, D, S = 16, 128, 128, 77
NB = 4
NG = B // NB
LAYERS, HEADS, DH = 2, 8, 64
HALF = HEADS // 2
INNER = HEADS * DH
HID = 341
HT = (128, 128, HID - 256)
DHID = 512
TOPK = int(2 * np.log(T))
MAGIC = 1.5 * 2.0 ** 23
NEG = -1.0e30
LN_EPS = 1e-5
CORR_SCALE = 1.0 / np.sqrt(D)
NBANKS = 8

CONST_COLS = {}


def constant_array():
    t = np.arange(T, dtype=np.float64)
    cols = {}
    cols["zero"] = np.zeros((128, 1))
    cols["ident"] = np.eye(128)
    cosines = np.cos(2 * np.pi * np.outer(t, np.arange(T // 2 + 1)) / T)
    sines = np.sin(2 * np.pi * np.outer(t, np.arange(1, T // 2)) / T)
    dft = np.concatenate([cosines, sines], axis=1)
    cols["dft"] = dft
    weight = np.full(T, 2.0)
    weight[0] = weight[T // 2] = 1.0
    cols["inverse_dft"] = (dft * weight[None, :] / T / D).T
    half = np.arange(0, DH, 2, dtype=np.float64)
    freqs = np.concatenate([np.outer(t, 10000.0 ** (-half / DH))] * 2, axis=1)
    base = (half + 0.4 * DH) / (1.4 * DH)
    scale = base[None, :] ** ((t[:, None] - T // 2) / 32.0)
    scale = np.concatenate([scale, scale], axis=1)
    sign = np.where(np.arange(DH) < DH // 2, -1.0, 1.0)[None, :]
    cols["rope"] = np.concatenate([8 * np.cos(freqs) * scale, 8 * sign * np.sin(freqs) * scale,
                                   np.cos(freqs) / scale, sign * np.sin(freqs) / scale], axis=1)
    i, j = t[:, None], t[None, :]
    cols["mask"] = np.where((i < j) | (i > j + 64), NEG, 0.0)
    pos = np.clip((t + 0.5) * (S / T) - 0.5, 0.0, S - 1)
    lo = np.floor(pos).astype(int)
    hi = np.minimum(lo + 1, S - 1)
    interp = np.zeros((T, T))
    np.add.at(interp, (S - 1 - lo, np.arange(T)), 1 - (pos - lo))
    np.add.at(interp, (S - 1 - hi, np.arange(T)), pos - lo)
    cols["interp"] = interp
    sums = np.zeros((128, 2 * T))
    sums[0, :T] = dft.sum(0)
    sums[0, T:] = dft[:S].sum(0)
    cols["sums"] = sums
    at = 0
    for name, a in cols.items():
        CONST_COLS[name] = (at, at + a.shape[1])
        at += a.shape[1]
    return np.concatenate(list(cols.values()), axis=1).astype(np.float32)


constant_array()
CONST_WIDTH = max(b for _, b in CONST_COLS.values())


WEIGHTS = {"corr_w": 4 * 128, "corr_bv": 1, "lngb": 2 * LAYERS, "b1": LAYERS * 6, "cb": 7,
           "w1": LAYERS * 2 * HID, "q1": DHID, "q2": DHID, "cw": 8 * 128, "wqkv": LAYERS * 3 * INNER,
           "wo": LAYERS * 4 * 128, "w2": LAYERS * 3 * 128}
ROWS = {"bq": 128, "bk": 128, "conv_b": DHID, "bo": 128, "scales": 2 * LAYERS * DH, "conv_w": 3 * DHID}


def places(widths):
    ends = np.cumsum(list(widths.values()))
    return {name: (int(b) - w, int(b)) for (name, w), b in zip(widths.items(), ends)}


WEIGHT_AT, ROW_AT = places(WEIGHTS), places(ROWS)


def weight_array(i):
    a = np.zeros((128, sum(WEIGHTS.values())), np.float32)

    def put(name, at, block):
        at += WEIGHT_AT[name][0]
        a[0:block.shape[0], at:at + block.shape[1]] = block

    for n, w in enumerate((i["L0_xattn_Wq"], i["L0_xattn_Wk"], i["L0_xattn_Wv"].T, i["L0_xattn_Wo"])):
        put("corr_w", n * 128, w)
    put("corr_bv", 0, i["L0_xattn_bv"][:, None])
    put("lngb", 0, i["L0_ffn_ln_g"].T)
    put("lngb", LAYERS, i["L0_ffn_ln_b"].T)
    for l in range(LAYERS):
        for j, rows in enumerate(HT):
            for part in range(2):
                at = part * HID + 128 * j
                put("b1", 6 * l + 3 * part + j, i["L0_ffn_b1"][l, at:at + rows, None])
            put("w2", (3 * l + j) * 128, i["L0_ffn_w2"][l, 128 * j:128 * j + rows])
        a[HT[2], WEIGHT_AT["w2"][0] + (3 * l + 2) * 128:][:128] = i["L0_ffn_b2"][l]
        put("w1", 2 * HID * l, i["L0_ffn_w1"][l])
        put("wqkv", 3 * INNER * l, i["L0_ffn_wqkv"][l])
        for t in range(4):
            put("wo", (4 * l + t) * 128, i["L0_ffn_wo"][l, 128 * t:128 * t + 128])
    cross = ("q_c", "k_s", "v_s", "q_s", "k_c", "v_c", "g")
    for n, name in enumerate(cross):
        w = i["L1_xattn_W" + name]
        for m in range(w.shape[1] // 128):
            put("cw", (n + m) * 128, w[:, 128 * m:128 * m + 128].T)
        put("cb", n, i["L1_xattn_b" + name][:, None])
    put("q1", 0, i["L1_ffn_w1"].T)
    for t in range(4):
        put("q2", 128 * t, i["L1_ffn_w2"][:, 128 * t:128 * t + 128].T)
    return a


def row_array(i):
    return np.concatenate([i["L0_xattn_bq"], i["L0_xattn_bk"], i["L1_ffn_conv_b"], i["L0_xattn_bo"],
                           i["L0_ffn_q_scale"].reshape(-1), i["L0_ffn_k_scale"].reshape(-1),
                           i["L1_ffn_conv_w"][:, 0, :].T.reshape(-1)])[None, :]


class Signal:

    def __init__(self, sem, per_group, step=1):
        self.sem, self.per_group, self.step = sem, per_group * step, step

    def raised_by(self, ins):
        ins.then_inc(self.sem, self.step)
        return ins

    def wait(self, eng, g, n):
        eng.wait_ge(self.sem, g * self.per_group + n * self.step)


class Chain(Signal):

    def __init__(self, sem, per_group):
        super().__init__(sem, per_group)
        self.n = 0

    def link(self, eng, g, ins):
        self.n += 1
        self.raised_by(ins)
        self.wait(eng, g, self.n)


ATTN_BANKS, FF_BANKS, FINISH_BANKS = 5, 2, 1
PAIRS = NB // 2

ORDERS = {"usual": """
    norm ff:hs.1.1 yT.0.0 fin:vs yT.0.1 qkv.0 rot.0.0 qkv.1 rot.0.1 ff:hT.1.1 fin:ks rot.1.0 ff:gu.1.1.0
    turns.0 rot.1.1 ff:gu.1.1.1 ff:gu.1.1.2 qkv.2 scores.0 rot.2.0 fin:qs sm.0.0 sm.0.1 rot.2.1 ff:down.1.1
    turns.1 pT.0 fin:z_moments fin:zn turns.2 qkv.3 rot.3.0 fin:zT scores.1 fin:kc rot.3.1 sm.1.0 o.0.0
    sm.1.1 o.0.1 fin:qc oT.0 pT.1 turns.3 fin:s1 o.1.0 o.1.1 scores.2 oT.1 sm.2.0 sm.2.1 fin:p1 fin:s2
    scores.3 sm.3.0 sm.3.1 wo.0 wo.1 pre:vprime ff:hs.0.0 pT.2 fin:vc o.2.0 o.2.1 ff:hT.0.0 pT.3 ff:gu.0.0.0
    ff:gu.0.0.1 o.3.0 oT.2 o.3.1 ff:gu.0.0.2 fin:p2 fin:p1T oT.3 wo.2 ff:down.0.0 wo.3 yT.1.0 fin:c2s
    ff:hs.0.1 qkv.4 rot.4.0 fin:a rot.4.1 ff:hT.0.1 qkv.5 ff:gu.0.1.0 rot.5.0 ff:gu.0.1.1 fin:s2c
    ff:gu.0.1.2 turns.4 rot.5.1 fin:g ff:down.0.1 scores.4 yT.1.1 fin:mix sm.4.0 sm.4.1 fin:mixT turns.5
    fin:quant pT.4 qkv.6 scores.5 rot.6.0 fin:dT sm.5.0 sm.5.1 rot.6.1 o.4.0 fin:h.0 o.4.1 fin:hq.0 pT.5
    qkv.7 rot.7.0 rot.7.1 fin:h.1 oT.4 o.5.0 o.5.1 pre:agg turns.6 wo.4 oT.5 fin:hqT.0 scores.6 fin:hq.1
    turns.7 sm.6.0 sm.6.1 wo.5 fin:h.2 ff:hs.1.0 pT.6 scores.7 fin:hqT.1 sm.7.0 sm.7.1 o.6.0 fin:hq.2
    ff:hT.1.0 fin:h.3 o.6.1 pT.7 fin:hq.3 ff:gu.1.0.0 fin:hqT.2 oT.6 o.7.0 o.7.1 ff:gu.1.0.1 fin:hqT.3
    ff:gu.1.0.2 oT.7 wo.6 fin:ffn wo.7 ff:down.1.0
""", "last": """
    ff:hs.1.1 fin:ks ff:hT.1.1 ff:gu.1.1.0 fin:qs ff:gu.1.1.1 ff:gu.1.1.2 fin:vs ff:down.1.1 fin:z_moments
    fin:zn fin:zT fin:qc fin:kc fin:s1 fin:s2 fin:p1 fin:vc fin:p1T fin:p2 fin:a fin:c2s fin:s2c fin:g
    fin:mix fin:mixT fin:quant fin:dT fin:h.0 fin:h.1 fin:hq.0 fin:hq.1 fin:hqT.0 fin:h.2 fin:hqT.1 fin:hq.2
    fin:h.3 fin:hq.3 fin:hqT.2 fin:hqT.3 fin:ffn
"""}


def schedule(turn):
    for word in ORDERS[turn].split():
        part, _, step = word.rpartition(":")
        name, *numbers = step.split(".")
        yield (part or "attn", name, *(int(n) for n in numbers))


def psum_units(part, turn):
    units = []
    for p, name, *args in schedule(turn):
        if p != part:
            continue
        if name == "qkv":
            l, b = divmod(args[0], NB)
            units += [("q", l, b), ("k", l, b), ("v", l, b)]
        elif name == "turns":
            units += [("qT", args[0]), ("kT", args[0])]
        elif name == "scores":
            units += [("sim", args[0], s) for s in range(2)]
        elif name == "pT":
            units += [("pT", args[0], s) for s in range(2)]
        elif name in ("o", "oT", "wo", "yT", "hs", "hT", "gu", "down", "h", "hqT"):
            units.append((name, *args))
        elif name not in ("norm", "rot", "sm", "z_moments", "zn", "p1", "p2", "mix", "quant", "hq"):
            units.append(name)
    if part == "ff":
        last = [u for u in units if u[1:3] == (LAYERS - 1, PAIRS - 1)]
        units = [u for u in units if u not in last] + last
    return units


VECTOR_STEPS = 4 * NB * LAYERS
PRE_STEPS = 3 * PAIRS - 1
FIRST_FIN = psum_units("fin", "usual")[0]
POOL_STEPS = 2 * NB * LAYERS
FINISH_STEPS = 35


def bank_changes():
    changes, before = {}, ("pre", "agg")
    for part, name, *args in schedule("usual"):
        if part in ("pre", "fin"):
            unit = (name, *args) if name in ("h", "hqT") else name
            if unit in psum_units(part, "usual"):
                if before[0] != part:
                    changes[(part, name, *args)] = before
                before = (part, unit)
    return changes


BANK_CHANGES = bank_changes()


def first_group(g):
    return isinstance(g, int) and g == 0


class Banks:

    def __init__(self, order, tensors, filled, freed, before=None):
        self.at = {name: n for n, name in enumerate(order)}
        self.tensors, self.filled, self.freed = tensors, filled, freed
        self.nbanks = len(tensors)
        self.uses = [len(range(k, len(order), self.nbanks)) for k in range(self.nbanks)]
        self.base = [0 if before is None else NG * before.uses[k] - (NG - 1) * self.uses[k]
                     for k in range(self.nbanks)]

    def __getitem__(self, name):
        return self.tensors[self.at[name] % self.nbanks]

    def wait_for(self, pe, g, free=None, read=()):
        need = {}
        for name, more in [(name, 2) for name in read] + ([(free, 1)] if free is not None else []):
            k, n = self.at[name] % self.nbanks, self.at[name] // self.nbanks
            need[k] = max(need.get(k, 0), n + more)
        for k, n in need.items():
            pe.wait_ge(self.freed[k], g * self.uses[k] + self.base[k] + n)

    def fills(self, name, ins):
        ins.then_inc(self.filled[self.at[name] % self.nbanks], 1)

    def wait_read(self, eng, g, name):
        k, n = self.at[name] % self.nbanks, self.at[name] // self.nbanks
        eng.wait_ge(self.freed[k], g * self.uses[k] + self.base[k] + n + 2)

    def wait_filled(self, eng, g, name):
        k, n = self.at[name] % self.nbanks, self.at[name] // self.nbanks
        eng.wait_ge(self.filled[k], g * self.uses[k] + self.base[k] + n + 1)

    def frees(self, name, ins):
        ins.then_inc(self.freed[self.at[name] % self.nbanks], 1)


def xattn_ffn_stack_kernel(nc, x, ctx_in, ctxT_in, consts, weights, rows_in, out):
    stack = ExitStack()
    with stack:
        def sb(name, shape, dt=F32):
            return stack.enter_context(nc.sbuf_tensor(name, shape, dt))

        def sem(name):
            return stack.enter_context(nc.semaphore(name))

        cst = sb("cst", [128, CONST_WIDTH])

        def const(name, rows=128):
            a, b = CONST_COLS[name]
            return cst[0:rows, a:b]

        ident = const("ident")
        ident_b = sb("ident_b", [128, 128], BF16)
        mask_b = sb("mask_b", [128, HALF, 128], BF16)
        ones = sb("ones", [128, 128])
        first = WEIGHT_AT["q2"][1]
        late = sb("late_weights", [128, sum(WEIGHTS.values()) - first])
        early = sb("early_weights", [128, WEIGHT_AT["cb"][1]])

        def weight(name):
            a, b = WEIGHT_AT[name]
            return early[:, a:b] if b <= WEIGHT_AT["cb"][1] else late[:, a - first:b - first]

        corr_w = weight("corr_w").rearrange("p (n o) -> p n o", n=4)
        corr_bv = weight("corr_bv")
        lngb = weight("lngb").rearrange("p (a l) -> p a l", a=2)
        b1 = weight("b1").rearrange("p (l a j) -> p l a j", l=LAYERS, a=2)
        cb = weight("cb")
        cw = weight("cw").rearrange("p (n o) -> p n o", n=8)
        wqkv = weight("wqkv").rearrange("p (l f) -> p l f", l=LAYERS)
        wo = weight("wo").rearrange("p (l a d) -> p l a d", l=LAYERS, a=4)
        w2 = weight("w2").rearrange("p (l a d) -> p l a d", l=LAYERS, a=3)
        corr_rows = sb("corr_rows", [1, 2, 128])
        bv_cols = sb("bv_cols", [128, S])
        wvo = sb("wvo", [128, 128])
        bvo = sb("bvo", [S, 128])
        bias_f = sb("bias_f", [128, 2, 128])
        scales = sb("scales", [128, 2, LAYERS, DH])
        rope = sb("rope", [128, LAYERS, 2, 2, DH])
        w1g = sb("w1g", [128, LAYERS, 2 * HID])
        cbs = sb("cbs", [128, 3])
        qsum = sb("qsum", [128, 2])
        qscale = sb("qscale", [128, 6])
        conv_parts = sb("conv_parts", [1, 3, DHID], BF16)
        conv_b3 = sb("conv_b3", [3, DHID], BF16)
        ones3 = sb("ones3", [3, 128], BF16)
        wc = sb("wc", [128, 3, DHID])
        q2T = sb("q2T", [128, 4, 128], BF16)

        search_stats = sb("search_stats", [128, B, 6])
        search_moments = sb("search_moments", [128, B, 2])
        search_vareps = sb("search_vareps", [128, B])
        search_rstd = sb("search_rstd", [128, B])
        spec = sb("spec", [128, B])
        corr = sb("corr", [B, 128])
        left = sb("left", [B, 2, 128])
        top8 = sb("top8", [B, 3, 8])
        corr_e = sb("corr_e", [B, 2, 128])
        corr_s = sb("corr_s", [B, 4])
        delay_w = sb("delay_w", [B, 2, 128])

        x0 = sb("x0", [128, NB, 128])
        hank = sb("hank", [S + 1, NB, 128])
        ctxT = sb("ctxT", [128, NB, S])
        ctxF = sb("ctxF", [128, NB, S])
        vprime = sb("vprime", [S + 1, NB, 128])
        x1 = sb("x1", [128, NB, 128])
        x2 = sb("x2", [128, NB, 128])
        x3 = sb("x3", [128, NB, 128])
        xs = sb("xs", [128, NB, 128])
        xn = sb("xn", [128, NB, 128])
        y0 = sb("y0", [128, NB, 128])
        y1 = sb("y1", [128, NB, 128])
        stats = sb("stats", [128, NB, 6])
        meanvar = sb("meanvar", [128, NB, 2])
        hstats = sb("hstats", [128, NB, 6])
        hmeanvar = sb("hmeanvar", [128, NB, 2])
        hvareps = sb("hvareps", [128, NB])
        hrstd = sb("hrstd", [128, NB])
        fstats = sb("fstats", [128, NB, 6])
        fmeanvar = sb("fmeanvar", [128, NB, 2])
        fvareps = sb("fvareps", [128, NB])
        frstd = sb("frstd", [128, NB])
        zn = sb("zn", [128, NB, 128])
        znT = sb("znT", [128, NB, 128])
        pause = sb("pause", [128, 1])
        vareps = sb("vareps", [128, NB])
        rstd = sb("rstd", [128, NB])
        minus_half = sb("minus_half", [128, 2 * HEADS])
        yT = sb("yT", [128, NB, 128])
        sq = sb("sq", [128, 2, 2, INNER])
        ssq = sb("ssq", [128, 2, 2 * HEADS])
        ssqc = sb("ssqc", [128, 2, 2 * HEADS])
        rnorm = sb("rnorm", [128, 2, 2 * HEADS])
        t_cos = sb("t_cos", [128, 2, 2, INNER])
        t_sin = sb("t_sin", [128, 2, 2, INNER])
        qk = sb("qk", [128, 2, 2, INNER])
        vx = sb("vx", [128, NB, HEADS, DH + 1])
        qT = sb("qT", [128, 2, 4, 128])
        kT = sb("kT", [128, 2, 4, 128])
        nmax = sb("nmax", [128, 2, HEADS])
        prob = sb("prob", [128, 2, 2, HALF, 128])
        probT = sb("probT", [128, 2, HALF, 128])
        rsum = sb("rsum", [128, 2, HEADS])
        o = sb("o", [128, 2, HEADS, DH])
        oT = sb("oT", [128, 2, 4, 128])
        gel = sb("gel", [128, 3, NB * 128])
        hid = sb("hid", [128, 3, NB * 128])
        zT = sb("zT", [128, NB, 128])
        nm1 = sb("nm1", [128, 4, NB])
        amax = sb("amax", [128, 4, NB])
        ydT = sb("ydT", [128, NB, 130])
        silb = sb("silb", [128, 2, DHID], BF16)
        silT = sb("silT", [128, NB, 4, 128], BF16)
        amax2 = sb("amax2", [128, 4, NB])

        def within(tensor, at, shape, dt=F32):
            letters = "abcd"[:len(tensor.shape) - 1]
            flat = tensor[:, :] if len(tensor.shape) == 2 else \
                tensor[tuple([slice(None)] * len(tensor.shape))].rearrange(
                    f"p {' '.join(letters)} -> p ({' '.join(letters)})")
            size = int(np.prod(shape[1:]))
            flat = flat[0:shape[0], at:at + size]
            if len(shape) == 2:
                return flat
            letters = "abcd"[:len(shape) - 1]
            return flat.rearrange(f"p ({' '.join(letters)}) -> p {' '.join(letters)}",
                                  **{c: n for c, n in zip(letters, shape[1:])})

        w1 = within(t_cos, 0, [128, LAYERS, 2 * HID])
        x_all = within(qk, 0, [128, B, 128])
        ctx_all = within(prob, 0, [S, B, 128])
        cross = sb("cross", [128, 4 * 512])
        gated = sb("gated", [128, 5 * 512])
        attn = sb("attn", [128, 3 * NB * S + 3 * 512])
        qcT, kcT, vc, aT = (within(cross, 512 * n, [128, NB, 128]) for n in range(4))
        c2sT, s2cT, gt = (within(gated, 512 * n, [128, NB, 128]) for n in range(3))
        mix = within(gated, 3 * 512, [128, 2, NB, 128])
        ksT, qsT, p1 = (within(attn, NB * S * n, [128, NB, S]) for n in range(3))
        vs, p1T, p2 = (within(attn, 3 * NB * S + 512 * n, [S, NB, 128]) for n in range(3))
        xn_all = within(cross, 0, [128, B, 128])
        spec_t = [within(buffer, 1024 * n, [128, 2, NB, 128]) for buffer in (gated, attn) for n in range(2)]
        spec_q, spec_k = (within(probT, 512 * n, [128, NB, 128]) for n in range(2))
        spec_product = within(oT, 0, [128, NB, 128])
        conv_w = within(gated, 0, [128, 3, DHID])
        q1, q2 = (within(gated, (3 + n) * DHID, [128, DHID]) for n in range(2))
        conv_b = within(cross, 0, [1, DHID])
        conv_tmp = within(cross, DHID, [1, 2, DHID])
        yq, yd = (within(gated, 512 * n, [128, NB, 128]) for n in range(2))
        sil = within(cross, 0, [128, 2, DHID])
        silq = within(cross, 1024, [128, 2, DHID])

        psum = [stack.enter_context(nc.psum_tensor(f"bank{k}", [128, 512], F32)) for k in range(NBANKS)]
        filled = [sem(f"bank{k}_filled") for k in range(NBANKS)]
        freed = [sem(f"bank{k}_freed") for k in range(NBANKS)]
        at = (0, ATTN_BANKS, ATTN_BANKS + FF_BANKS, NBANKS)
        banks, hbanks, fbanks = (Banks(psum_units(part, "usual"), psum[a:b], filled[a:b], freed[a:b])
                                 for part, a, b in zip(("attn", "ff", "fin"), at, at[1:]))
        fbanks_last = Banks(psum_units("fin", "last"), *(t[0:at[1]] for t in (psum, filled, freed)), before=banks)
        pbanks = Banks(psum_units("pre", "usual"), psum[NBANKS - 1:], [sem("next_group_bank_filled")],
                       [sem("next_group_bank_freed")])
        parts = {"fin": fbanks}

        delays = nc.dram_tensor("delay_weights", [B, 2 * 128], F32, kind="Internal").ap()

        w_loaded = sem("weights_loaded")
        c_loaded = sem("constants_loaded")
        conv_loaded = sem("conv_bias_parts_loaded")
        pool_set = sem("pool_constants_set")
        w1_loaded = sem("ff_weights_loaded")
        q_loaded = sem("quantised_weights_loaded")
        late_loaded = sem("late_weights_loaded")
        prep_pe = sem("set_up_products_ready")
        prep_sums = sem("magnitude_sums_ready")
        bv_ready = sem("bv_columns_ready")
        qsum_ready = sem("magnitude_row_sums_ready")
        conv_split = sem("conv_bias_split")
        sums_taken = sem("magnitude_sums_taken")
        prep_taken = sem("set_up_products_taken")
        prep_dve = Chain(sem("prep_vector_steps"), 0)
        f_loaded = sem("search_tokens_loaded")
        f_ctx_loaded = sem("search_context_loaded")
        f_var = sem("search_variance_ready")
        f_rstd = sem("search_rstd_ready")
        f_norm = sem("search_tokens_normalised")
        f_spec = sem("search_tokens_transformed")
        f_copied = sem("search_transform_copied")
        f_proj = sem("search_projected")
        s_spec = sem("spectra_ready")
        s_corr = sem("correlation_ready")
        s_shift = sem("correlation_shift_ready")
        s_exp = sem("delay_exponentials_ready")
        s_delay = sem("delay_weights_ready")
        s_stored = sem("delay_weights_stored")
        x_loaded = Signal(sem("x_loaded"), 1, 16)
        ctx_loaded = Signal(sem("ctx_loaded"), 1, 16)
        hank_loaded = Signal(sem("hankel_loaded"), 1, 16)
        ctxF_loaded = Signal(sem("last_part_ctx_loaded"), 1, 16)
        var_ready = Signal(sem("variance_ready"), PAIRS)
        rstd_ready = Signal(sem("rstd_ready"), PAIRS)
        hvar_ready = Signal(sem("feed_forward_variance_ready"), LAYERS * PAIRS)
        hrstd_ready = Signal(sem("feed_forward_rstd_ready"), LAYERS * PAIRS)
        gel_ready = Signal(sem("gate_ready"), 3 * LAYERS * PAIRS)
        xs_ready = Signal(sem("x1_added"), PAIRS)
        fvar_ready = Signal(sem("last_part_variance_ready"), 2)
        frstd_ready = Signal(sem("last_part_rstd_ready"), 2)
        y_ready = Signal(sem("stack_input_ready"), PAIRS)
        sq_ready = Signal(sem("squares_ready"), 2 * NB * LAYERS)
        ssq_ready = Signal(sem("square_sums_ready"), 2 * NB * LAYERS)
        sum_ready = Signal(sem("rotated_sums_ready"), 2 * NB * LAYERS)
        qk_ready = Signal(sem("qk_ready"), 2 * NB * LAYERS)
        nmax_ready = Signal(sem("score_max_ready"), 2 * NB * LAYERS)
        z_ready = Signal(sem("z_ready"), 1)
        cmax_ready = Signal(sem("cross_max_ready"), 2)
        cprob_ready = Signal(sem("cross_prob_ready"), 2)
        diff_ready = Signal(sem("cross_difference_ready"), 1)
        mix_ready = Signal(sem("mix_ready"), 1)
        yd_ready = Signal(sem("quantised_input_ready"), 1)
        silq_ready = Signal(sem("quantised_hidden_ready"), NB)
        x3_stored = Signal(sem("result_stored"), 1, 16)
        steps = Chain(sem("vector_steps"), VECTOR_STEPS)
        psteps = Chain(sem("next_group_vector_steps"), PRE_STEPS)
        hsteps = Chain(sem("feed_forward_vector_steps"), 2 * LAYERS * PAIRS)
        fsteps = Chain(sem("last_part_vector_steps"), FINISH_STEPS)
        pool_steps = Chain(sem("pool_steps"), POOL_STEPS)

        block = stack.enter_context(nc.Block())
        weight_loads = [0]

        @block.sync
        def _(sp):
            def load(dst, src, loaded=w_loaded):
                sp.dma_start(dst, src).then_inc(loaded, 16)
                if loaded is w_loaded:
                    weight_loads[0] += 1

            def packed(name, last=None):
                return weights[:, WEIGHT_AT[name][0]:WEIGHT_AT[last or name][1]]

            def row(name):
                return rows_in[:, ROW_AT[name][0]:ROW_AT[name][1]]

            load(x_all, x.rearrange("b t d -> t b d"), f_loaded)
            load(cst[:, :], consts, c_loaded)
            load(early[:, :], packed("corr_w", "cb"))
            load(corr_rows[:, :, :].rearrange("p a n -> p (a n)"), rows_in[:, 0:256])
            load(ctx_all, ctx_in.rearrange("b t d -> t b d"), f_ctx_loaded)
            load(w1.rearrange("p l f -> p (l f)"), packed("w1"), w1_loaded)
            load(scales[:, :, :, :].rearrange("p a l d -> p (a l d)"), row("scales")[0].partition_broadcast(128),
                 w1_loaded)
            for b in range(NB):
                load(vprime[S:S + 1, b, :], row("bo"), late_loaded)
            load(late[:, :], packed("cw", "w2"), late_loaded)

            def load_tokens(g):
                x_loaded.raised_by(sp.dma_start(
                    x0[:, :, :], bass.AP(x.tensor, g[0], [[D, T], [T * D, NB], [1, D]])))

            def load_delays(g):
                hank_loaded.raised_by(sp.dma_start(
                    hank[0:S, :, :], bass.AP(delays.tensor, g[1], [[1, S], [2 * T, NB], [1, T]])))

            def load_context(g, dst, loaded):
                loaded.raised_by(sp.dma_start(
                    dst[:, :, :], bass.AP(ctxT_in.tensor, g[2], [[B * S, D], [S, NB], [1, S]])))

            def addresses(g, hold=lambda v: v):
                return hold(g * (NB * T * D)), hold(g * (NB * 2 * T) + T - S), hold(g * (NB * S))

            def turn(ga, gb, more):
                parts["fin"] = fbanks_last if ga is None else fbanks
                hold = sp.snap if more and gb is not None else (lambda v: v)
                if gb is not None:
                    out_at = addresses(gb, hold)
                if ga is not None:
                    here = addresses(ga, hold)
                if more:
                    ahead = addresses(ga + 1, hold)
                if ga is not None:
                    if more:
                        pbanks.wait_read(sp, ga, "vprime")
                        load_context(ahead, ctxT, ctx_loaded)
                        pbanks.wait_read(sp, ga, "agg")
                        load_tokens(ahead)
                        load_delays(ahead)
                    if gb is not None:
                        parts["fin"].wait_read(sp, gb, "g")
                        load_context(here, ctxF, ctxF_loaded)
                if gb is not None:
                    parts["fin"].wait_read(sp, gb, "ffn")
                    x3_stored.raised_by(sp.dma_start(
                        bass.AP(out.tensor, out_at[0], [[D, T], [T * D, NB], [1, D]]), x3[:, :, :]))

            load_tokens(addresses(0))
            load_context(addresses(0), ctxT, ctx_loaded)
            load_context(addresses(0), ctxF, ctxF_loaded)
            sp.wait_ge(s_delay, 1)
            sp.dma_start(delays, delay_w[:, :, :].rearrange("b a t -> b (a t)")).then_inc(s_stored, 16)
            sp.wait_ge(pool_set, 1)
            sp.wait_ge(s_stored, 16)
            load_delays(addresses(0))
            load(q1, packed("q1"), q_loaded)
            load(q2, packed("q2"), q_loaded)
            load(conv_w.rearrange("p k c -> p (k c)"), row("conv_w")[0].partition_broadcast(128), q_loaded)
            load(conv_b[:, :], row("conv_b"), q_loaded)
            turn(0, None, True)
            sp.wait_ge(conv_split, 1)
            for n in range(3):
                sp.dma_start(conv_b3[n:n + 1, :], conv_parts[:, n, :]).then_inc(conv_loaded, 16)
            with sp.Fori(0, NG - 2) as g:
                turn(g + 1, g, True)
            turn(NG - 1, NG - 2, False)
            turn(None, NG - 1, False)
            sp.wait_ge(x3_stored.sem, 16 * (NG + 1))

        @block.gpsimd
        def _(pool):
            for k in range(NBANKS):
                pool.sem_inc(freed[k], 1)
            pool.sem_inc(pbanks.freed[0], 1)
            pool.sem_inc(x3_stored.sem, 16)
            pool.memset(minus_half[:, :], -0.5)
            pool.memset(ones[:, :], 1.0)
            pool.memset(ones3[:, :], 1.0)
            pool.memset(hank[:, :, :], 1.0)
            pool.memset(vx[:, :, :, :], 1.0)
            pool.memset(hid[:, 2, :], 1.0)
            pool.memset(yT[:, :, :], 0.0)
            pool.memset(ydT[:, :, :], 0.0).then_inc(pool_set, 1)

            pool.wait_ge(pool_set, 1)
            pool.wait_ge(f_var, 1)
            pool.tensor_tensor(search_rstd[:, :], search_vareps[:, :], minus_half[:, :], ALU.pow).then_inc(f_rstd, 1)

            def deviation(g, n, ready, ve, rs, raised, a, b):
                ready.wait(pool, g, n)
                raised.raised_by(pool.tensor_tensor(rs[:, a:b], ve[:, a:b], minus_half[:, a:b], ALU.pow))

            def rotated(g, i, part):
                p = i % 2
                heads = slice(part * HEADS, part * HEADS + HEADS)
                ssq_ready.wait(pool, g, 2 * i + part + 1)
                pool_steps.link(pool, g, pool.tensor_tensor(rnorm[:, p, heads], ssqc[:, p, heads],
                                                            minus_half[:, 0:HEADS], ALU.pow))
                sum_ready.wait(pool, g, 2 * i + part + 1)
                if i >= 2:
                    banks.wait_read(pool, g, (("qT", "kT")[part], i - 2))
                qk_ready.raised_by(pool.tensor_tensor(
                    qk[:, p, part, :].rearrange("p (h d) -> p h d", h=HEADS),
                    t_cos[:, p, part, :].rearrange("p (h d) -> p h d", d=DH),
                    rnorm[:, p, heads].unsqueeze(2).to_broadcast([128, HEADS, DH]),
                    ALU.mult))

            def with_first_residual(g, l, pair):
                if l == 0:
                    hbanks.wait_read(pool, g, ("down", 0, pair))
                    a, b = 2 * pair, 2 * pair + 2
                    xs_ready.raised_by(pool.tensor_tensor(xs[:, a:b, :], x1[:, a:b, :], y0[:, a:b, :], ALU.add))

            def difference(g):
                parts["fin"].wait_read(pool, g, "s2c")
                diff_ready.raised_by(pool.tensor_tensor(mix[:, 0, :, :], c2sT[:, :, :], s2cT[:, :, :],
                                                        ALU.subtract))

            def input_deviations(g):
                for pair in range(PAIRS):
                    deviation(g, pair + 1, var_ready, vareps, rstd, rstd_ready, 2 * pair, 2 * pair + 2)

            work = {
                "agg": input_deviations,
                "rot": rotated,
                "hs": lambda g, l, pair: deviation(g, PAIRS * l + pair + 1, hvar_ready, hvareps, hrstd,
                                                   hrstd_ready, 2 * pair, 2 * pair + 2),
                "down": with_first_residual,
                "z_moments": lambda g: deviation(g, 1, fvar_ready, fvareps, frstd, frstd_ready, 0, NB),
                "s2c": difference,
                "mixT": lambda g: deviation(g, 2, fvar_ready, fvareps, frstd, frstd_ready, 0, NB)}

            def group_turn(ga, gb, gn):
                pool_steps.n = 0
                parts["fin"] = fbanks_last if ga is None else fbanks
                for part, name, *args in schedule("last" if ga is None else "usual"):
                    before = part == "fin" or part == "ff" and tuple(args[0:2]) == (LAYERS - 1, PAIRS - 1)
                    g = gb if before else gn if part == "pre" else ga
                    if g is not None and name in work:
                        work[name](g, *args)
                assert ga is None or pool_steps.n == POOL_STEPS, pool_steps.n

            work["agg"](0)
            group_turn(0, None, 1)
            with pool.Fori(0, NG - 2) as g:
                group_turn(g + 1, g, g + 2)
            group_turn(NG - 1, NG - 2, None)
            group_turn(None, NG - 1, None)

        @block.vector
        def _(dve):
            def link0(ins):
                prep_dve.n += 1
                ins.then_inc(prep_dve.sem, 1)
                dve.wait_ge(prep_dve.sem, prep_dve.n)

            dve.wait_ge(f_loaded, 16)
            for b in range(B):
                last = dve.bn_stats(search_stats[:, b, :], x_all[:, b, :])
            link0(last)
            for b in range(B):
                last = dve.bn_aggr(search_moments[:, b, :], search_stats[:, b, :])
            link0(last)
            dve.tensor_scalar(search_vareps[:, :], search_moments[:, :, 1], LN_EPS, None, ALU.add).then_inc(f_var, 1)
            dve.wait_ge(w_loaded, 16 * weight_loads[0])
            dve.tensor_copy(bv_cols[:, :], corr_bv[:, 0:1].to_broadcast([128, S])).then_inc(bv_ready, 1)
            dve.wait_ge(f_rstd, 1)
            for g in range(NG):
                for b in range(NB * g, NB * g + NB):
                    last = dve.tensor_scalar(xn_all[:, b, :], x_all[:, b, :], search_moments[:, b, 0:1],
                                             search_rstd[:, b:b + 1], ALU.subtract, ALU.mult)
                last.then_inc(f_norm, 1)
            dve.wait_ge(prep_pe, 1)
            link0(dve.tensor_copy(bias_f[:, :, :].rearrange("p a o -> p (a o)"), psum[6][:, 0:256]))
            dve.tensor_copy(wvo[:, :], psum[6][:, 256:384])
            dve.tensor_copy(bvo[:, :], psum[6][0:S, 384:512])
            for l in range(LAYERS):
                for part in range(2):
                    at = 6 * l + 3 * part
                    dve.tensor_tensor(b1[:, l, part, 0:2], b1[:, l, part, 0:2],
                                      psum[7][:, at:at + 2], ALU.add)
                    last = dve.tensor_tensor(b1[0:HT[2], l, part, 2:3], b1[0:HT[2], l, part, 2:3],
                                             psum[7][0:HT[2], at + 2:at + 3], ALU.add)
            last.then_inc(prep_taken, 1)
            dve.wait_ge(w1_loaded, 32)
            table = const("rope").rearrange("p (a c d) -> p a c d", a=2, c=2)
            for l in range(LAYERS):
                for part in range(2):
                    dve.tensor_tensor(rope[:, l, part, 0, :], table[:, part, 0, :], scales[:, part, l, :],
                                      ALU.mult)
                    dve.tensor_tensor(
                        rope[:, l, part, 1, :].rearrange("p (c d) -> p c d", c=2),
                        table[:, part, 1, :].rearrange("p (c d) -> p c d", c=2),
                        scales[:, part, l, :].rearrange("p (c d) -> p c d", c=2)[:, ::-1, :], ALU.mult)
                dve.tensor_scalar(w1g[:, l, :], w1[:, l, :], lngb[:, 0, l:l + 1], None, ALU.mult)
            for g in range(NG):
                dve.wait_ge(f_proj, g + 1)
                dve.tensor_tensor(spec_q[:, :, :], psum[2 * g][:, :].rearrange("p (b c) -> p b c", b=NB),
                                  bias_f[:, 0, :].unsqueeze(1).to_broadcast([128, NB, 128]), ALU.add)
                link0(dve.tensor_tensor(
                    spec_k[:, :, :], psum[2 * g + 1][:, :].rearrange("p (b c) -> p b c", b=NB),
                    bias_f[:, 1, :].unsqueeze(1).to_broadcast([128, NB, 128]), ALU.add))
                link0(dve.tensor_tensor(spec_product[:, :, :], spec_q[:, :, :], spec_k[:, :, :], ALU.mult))
                dve.tensor_reduce(spec[:, g * NB:(g + 1) * NB], spec_product[:, :, :], AX.X,
                                  ALU.add).then_inc(s_spec, 1)
            dve.tensor_copy(ident_b[:, :], ident)
            dve.tensor_copy(mask_b[:, :, :], const("mask").unsqueeze(1).to_broadcast([128, HALF, 128]))
            dve.tensor_scalar(cbs[:, 0:1], cb[:, 0:1], CORR_SCALE, None, ALU.mult)
            dve.tensor_scalar(cbs[:, 1:2], cb[:, 3:4], CORR_SCALE, None, ALU.mult)
            dve.tensor_scalar(cbs[:, 2:3], cb[:, 6:7], 0.5, None, ALU.mult)
            dve.wait_ge(s_corr, 1)
            link0(dve.tensor_copy(corr[:, :], psum[0][0:B, 0:128]))
            link0(dve.max(top8[:, 0, :], corr[:, :]))
            link0(dve.match_replace(left[:, 0, :], top8[:, 0, :], corr[:, :], -3.0e38))
            link0(dve.max(top8[:, 1, :], left[:, 0, :]))
            link0(dve.memset(top8[:, 2, :], -3.0e38))
            link0(dve.tensor_copy(top8[:, 2, 0:TOPK - 8], top8[:, 1, 0:TOPK - 8]))
            link0(dve.match_replace(left[:, 1, :], top8[:, 2, :], left[:, 0, :], -3.0e38))
            dve.tensor_scalar(corr_s[:, 0:1], top8[:, 0, 0:1], -1.0, None, ALU.mult).then_inc(s_shift, 1)
            dve.wait_ge(s_exp, 1)
            link0(dve.scalar_tensor_tensor(corr_e[:, 1, :], left[:, 1, :], -2.9e38, corr_e[:, 0, :],
                                           ALU.is_le, ALU.mult))
            link0(dve.tensor_reduce(corr_s[:, 1:2], corr_e[:, 1, :], AX.X, ALU.add))
            link0(dve.reciprocal(corr_s[:, 2:3], corr_s[:, 1:2]))
            dve.tensor_scalar(delay_w[:, :, :], corr_e[:, 1, ::-1].unsqueeze(1).to_broadcast([B, 2, 128]),
                              corr_s[:, 2:3], None, ALU.mult).then_inc(s_delay, 1)

            def magnitudes():
                dve.wait_ge(q_loaded, 64)
                for n, w in enumerate((q1, q2)):
                    last = dve.tensor_reduce(qsum[:, n:n + 1], w, AX.X, ALU.add, apply_absolute_value=True)
                last.then_inc(qsum_ready, 1)
                link0(dve.tensor_copy(conv_parts[:, 0, :], conv_b[:, :]))
                link0(dve.tensor_tensor(conv_tmp[:, 0, :], conv_b[:, :], conv_parts[:, 0, :], ALU.subtract))
                link0(dve.tensor_copy(conv_parts[:, 1, :], conv_tmp[:, 0, :]))
                link0(dve.tensor_tensor(conv_tmp[:, 1, :], conv_tmp[:, 0, :], conv_parts[:, 1, :], ALU.subtract))
                dve.tensor_copy(conv_parts[:, 2, :], conv_tmp[:, 1, :]).then_inc(conv_split, 1)

            def rounded_weights():
                dve.wait_ge(prep_sums, 1)
                dve.tensor_scalar(qscale[:, 0:2], psum[NBANKS - 1][:, 0:2], 1.0 / (DHID * D), 1e-5, ALU.mult,
                                  ALU.max).then_inc(sums_taken, 1)
                dve.wait_ge(sums_taken, 1)
                link0(dve.reciprocal(qscale[:, 2:4], qscale[:, 0:2]))
                for n, w in enumerate((q1, q2)):
                    link0(dve.tensor_scalar(w, w, qscale[:, 2 + n:3 + n], MAGIC, ALU.mult, ALU.add))
                    link0(dve.tensor_scalar(w, w, MAGIC, 1.0, ALU.subtract, ALU.min))
                link0(dve.tensor_scalar(q1, q1, -1.0, None, ALU.max))

            def tap_weights():
                dve.tensor_scalar(q2T[:, :, :].rearrange("p a o -> p (a o)"), q2, -1.0, None, ALU.max)
                dve.tensor_scalar(qscale[:, 4:5], qscale[:, 1:2], 1.0 / 127.0, None, ALU.mult)
                link0(dve.tensor_scalar(conv_w, conv_w, qscale[:, 0:1], None, ALU.mult))
                for k in range(3):
                    last = dve.tensor_tensor(wc[:, k, :], q1, conv_w[:, k, :], ALU.mult)
                link0(last)

            def moments(g, src, chain, st, mv, ve, ready, batches=range(NB)):
                for b in batches:
                    last = dve.bn_stats(st[:, b, :], src(b))
                chain.link(dve, g, last)
                dve.memset(pause[:, :], 0.0)
                for b in batches:
                    last = dve.bn_aggr(mv[:, b, :], st[:, b, :])
                chain.link(dve, g, last)
                ready.raised_by(dve.tensor_scalar(ve[:, batches[0]:batches[-1] + 1],
                                                  mv[:, batches[0]:batches[-1] + 1, 1], LN_EPS, None, ALU.add))

            def normalise(g, n, src, dst, mv, rs, rs_ready, batches=range(NB)):
                rs_ready.wait(dve, g, n)
                for b in batches:
                    last = dve.tensor_scalar(dst[:, b, :], src(b), mv[:, b, 0:1], rs[:, b:b + 1],
                                             ALU.subtract, ALU.mult)
                return last

            def context_values(g):
                pbanks.wait_filled(dve, g, "vprime")
                u = pbanks["vprime"]
                ins = dve.tensor_tensor(vprime[0:S, :, :], u[0:S, :].rearrange("p (b e) -> p b e", b=NB),
                                        bvo[:, :].unsqueeze(1).to_broadcast([S, NB, 128]), ALU.add)
                pbanks.frees("vprime", ins)

            def correlated(g):
                pbanks.wait_filled(dve, g, "agg")
                x_loaded.wait(dve, g, 1)
                psteps.n = 0
                if not first_group(g):
                    xs_ready.wait(dve, g - 1, PAIRS)
                for pair in range(PAIRS):
                    a, b = 2 * pair, 2 * pair + 2
                    ins = dve.tensor_tensor(
                        x1[:, a:b, :].rearrange("p b d -> p (b d)"), pbanks["agg"][:, a * 128:b * 128],
                        x0[:, a:b, :].rearrange("p b d -> p (b d)"), ALU.add)
                    if pair < PAIRS - 1:
                        psteps.link(dve, g, ins)
                    else:
                        pbanks.frees("agg", ins)
                        pbanks.wait_read(dve, g, "agg")
                    moments(g, lambda b: x1[:, b, :], psteps, stats, meanvar, vareps, var_ready, range(a, b))

            def normalised_input(g):
                if not first_group(g):
                    banks.wait_for(dve, g - 1, read=[("wo", NB * LAYERS - 1 - b) for b in range(NB)])
                for pair in range(PAIRS):
                    y_ready.raised_by(normalise(g, pair + 1, lambda b: x1[:, b, :], y0, meanvar, rstd, rstd_ready,
                                                range(2 * pair, 2 * pair + 2)))

            def rotary(g, i, part):
                (l, b), p = divmod(i, NB), i % 2
                heads = slice(part * HEADS, part * HEADS + HEADS)
                sq_ready.wait(dve, g, 2 * i + part + 1)
                steps.link(dve, g, dve.tensor_reduce(
                    ssq[:, p, heads], sq[:, p, part, :].rearrange("p (h d) -> p h d", h=HEADS), AX.X, ALU.add))
                if i >= 2:
                    qk_ready.wait(dve, g, 2 * i + part - 3)
                ssq_ready.raised_by(dve.tensor_scalar(ssqc[:, p, heads], ssq[:, p, heads], 1e-24, None, ALU.max))
                name = ("q", "k")[part]
                banks.wait_filled(dve, g, (name, l, b))
                u = banks[(name, l, b)]
                cos = rope[:, l, part, 0, :].unsqueeze(1).to_broadcast([128, HEADS, DH])
                sin = rope[:, l, part, 1, :].rearrange("p (c d) -> p c d", c=2)\
                    .unsqueeze(1).to_broadcast([128, HEADS, 2, DH // 2])
                dve.tensor_tensor(t_cos[:, p, part, :].rearrange("p (h d) -> p h d", d=DH),
                                  u[:, :].rearrange("p (h d) -> p h d", d=DH), cos, ALU.mult)
                ins = dve.tensor_tensor(
                    t_sin[:, p, part, :].rearrange("p (h c d) -> p h c d", c=2, d=DH // 2),
                    u[:, :].rearrange("p (h c d) -> p h c d", c=2, d=DH // 2)[:, :, ::-1, :], sin, ALU.mult)
                banks.frees((name, l, b), ins)
                banks.wait_read(dve, g, (name, l, b))
                sum_ready.raised_by(dve.tensor_tensor(t_cos[:, p, part, :], t_cos[:, p, part, :],
                                                      t_sin[:, p, part, :], ALU.add))

            def largest(g, i, s):
                banks.wait_filled(dve, g, ("sim", i, s))
                nmax_ready.raised_by(dve.tensor_reduce(
                    nmax[:, i % 2, HALF * s:HALF * s + HALF],
                    banks[("sim", i, s)][:, :].rearrange("p (h j) -> p h j", h=HALF), AX.X, ALU.max, negate=True))

            def outputs(g, i, s):
                p = i % 2
                banks.wait_filled(dve, g, ("o", i, s))
                u = banks[("o", i, s)][:, 0:HALF * (DH + 1)].rearrange("p (h d) -> p h d", h=HALF)
                steps.link(dve, g, dve.reciprocal(rsum[:, p, HALF * s:HALF * s + HALF], u[:, :, DH]))
                ins = dve.tensor_tensor(
                    o[:, p, s::2, :], u[:, :, 0:DH],
                    rsum[:, p, HALF * s:HALF * s + HALF].unsqueeze(2).to_broadcast([128, HALF, DH]), ALU.mult)
                banks.frees(("o", i, s), ins)

            def attended(g, i):
                l, b = divmod(i, NB)
                banks.wait_filled(dve, g, ("wo", i))
                u = banks[("wo", i)][:, 0:128]
                if l == LAYERS - 1:
                    xs_ready.wait(dve, g, b // 2 + 1)
                    dve.tensor_tensor(xs[:, b, :], u, xs[:, b, :], ALU.add)
                ins = dve.tensor_tensor(y1[:, b, :], u, y0[:, b, :], ALU.add)
                banks.frees(("wo", i), ins)

            def shifted_norm(g, l, pair):
                hsteps.n = 2 * (PAIRS * l + pair)
                batches = range(2 * pair, 2 * pair + 2)
                hbanks.wait_filled(dve, g, ("hs", l, pair))

                def src(b):
                    return hbanks[("hs", l, pair)][:, (b % 2) * 128:(b % 2) * 128 + 128]

                moments(g, src, hsteps, hstats, hmeanvar, hvareps, hvar_ready, batches)
                hbanks.frees(("hs", l, pair), normalise(g, PAIRS * l + pair + 1, src, xn, hmeanvar, hrstd,
                                                        hrstd_ready, batches))

            def gated_hidden(g, l, pair, j):
                rows, a = HT[j], 256 * pair
                name = ("gu", l, pair, j)
                gel_ready.wait(dve, g, 3 * (PAIRS * l + pair) + j + 1)
                ins = dve.scalar_tensor_tensor(
                    hid[0:rows, j, a:a + 256], hbanks[name][0:rows, 256:512], b1[0:rows, l, 0, j:j + 1],
                    gel[0:rows, j, a:a + 256], ALU.add, ALU.mult)
                hbanks.frees(name, ins)

            def stack_output(g, l, pair):
                name, a, b = ("down", l, pair), 2 * pair, 2 * pair + 2
                hbanks.wait_filled(dve, g, name)
                dst, src = (y0, y1) if l < LAYERS - 1 else (x2, xs)
                ins = dve.tensor_tensor(dst[:, a:b, :].rearrange("p b d -> p (b d)"), hbanks[name][:, 0:256],
                                        src[:, a:b, :].rearrange("p b d -> p (b d)"), ALU.add)
                hbanks.frees(name, ins)

            def z_moments(g):
                hbanks.wait_read(dve, g, ("down", LAYERS - 1, PAIRS - 1))
                moments(g, lambda b: x2[:, b, :], fsteps, fstats, fmeanvar, fvareps, fvar_ready)

            def cross_tokens(g):
                z_ready.raised_by(normalise(g, 1, lambda b: x2[:, b, :], zn, fmeanvar, frstd, frstd_ready))

            def largest_scores(g, n):
                name, rows, keys = (("s1", 128, S), ("s2", S, 128))[n]
                parts["fin"].wait_filled(dve, g, name)
                cmax_ready.raised_by(dve.tensor_reduce(
                    nm1[0:rows, n, :], parts["fin"][name][0:rows, 0:NB * keys].rearrange("p (b j) -> p b j", b=NB),
                    AX.X, ALU.max, negate=True))

            def probabilities(g, n):
                p, rows, keys = ((p1, 128, S), (p2, S, 128))[n]
                parts["fin"].wait_read(dve, g, ("s1", "s2")[n])
                fsteps.link(dve, g, dve.tensor_reduce(amax[0:rows, 2 * n, :], p[:, :, :], AX.X, ALU.add))
                fsteps.link(dve, g, dve.reciprocal(amax[0:rows, 2 * n + 1, :], amax[0:rows, 2 * n, :]))
                cprob_ready.raised_by(dve.tensor_tensor(
                    p[:, :, :], p[:, :, :],
                    amax[0:rows, 2 * n + 1, :].unsqueeze(2).to_broadcast([rows, NB, keys]), ALU.mult))

            def gated_sum(g):
                parts["fin"].wait_read(dve, g, "g")
                diff_ready.wait(dve, g, 1)
                fsteps.link(dve, g, dve.scalar_tensor_tensor(mix[:, 1, :, :], gt[:, :, :], 1.0, mix[:, 0, :, :],
                                                            ALU.add, ALU.mult))
                mix_ready.raised_by(dve.scalar_tensor_tensor(gt[:, :, :], mix[:, 1, :, :], 0.5, s2cT[:, :, :],
                                                             ALU.mult, ALU.add))

            def mixed(g):
                parts["fin"].wait_filled(dve, g, "mixT")
                x3_stored.wait(dve, g, 1)
                ins = dve.tensor_tensor(x3[:, :, :].rearrange("p b d -> p (b d)"), parts["fin"]["mixT"][:, :],
                                        x2[:, :, :].rearrange("p b d -> p (b d)"), ALU.add)
                parts["fin"].frees("mixT", ins)
                parts["fin"].wait_read(dve, g, "mixT")
                moments(g, lambda b: x3[:, b, :], fsteps, fstats, fmeanvar, fvareps, fvar_ready)

            def token_scales(g, am):
                fsteps.link(dve, g, dve.tensor_scalar(am[:, 0, :], am[:, 0, :], 1e-5, None, ALU.max))
                fsteps.link(dve, g, dve.reciprocal(am[:, 2, :], am[:, 0, :]))
                dve.tensor_scalar(am[:, 1, :], am[:, 2, :], 127.0, None, ALU.mult)

            def quantised_tokens(g):
                fsteps.link(dve, g, normalise(g, 2, lambda b: x3[:, b, :], zn, fmeanvar, frstd, frstd_ready))

                fsteps.link(dve, g, dve.tensor_reduce(amax[:, 0, :], zn[:, :, :], AX.X, ALU.max,
                                                     apply_absolute_value=True))
                token_scales(g, amax)
                fsteps.link(dve, g, dve.tensor_scalar(amax[:, 3, :], amax[:, 0, :], 1.0 / 127.0, None, ALU.mult))
                for b in range(NB):
                    last = dve.tensor_scalar(yq[:, b, :], zn[:, b, :], amax[:, 1, b:b + 1], MAGIC,
                                             ALU.mult, ALU.add)
                fsteps.link(dve, g, last)
                for b in range(NB):
                    last = dve.tensor_scalar(yd[:, b, :], yq[:, b, :], MAGIC, amax[:, 3, b:b + 1],
                                             ALU.subtract, ALU.mult)
                yd_ready.raised_by(last)

            def quantised_hidden(g, b):
                p = b % 2
                am = amax2[:, :, b:b + 1]
                parts["fin"].wait_read(dve, g, ("h", b))
                fsteps.link(dve, g, dve.tensor_reduce(am[:, 0, :], sil[:, p, :], AX.X, ALU.max,
                                                     apply_absolute_value=True))
                token_scales(g, am)
                fsteps.link(dve, g, dve.tensor_scalar(am[:, 3, :], am[:, 0, :], qscale[:, 4:5], None, ALU.mult))
                fsteps.link(dve, g, dve.tensor_scalar(silq[:, p, :], sil[:, p, :], am[:, 1, :], MAGIC,
                                                     ALU.mult, ALU.add))
                silq_ready.raised_by(dve.tensor_scalar(silb[:, p, :], silq[:, p, :], MAGIC, 127.0,
                                                       ALU.subtract, ALU.min))

            def result(g):
                parts["fin"].wait_filled(dve, g, "ffn")
                for b in range(NB):
                    last = dve.scalar_tensor_tensor(x3[:, b, :], parts["fin"]["ffn"][:, b * 128:b * 128 + 128],
                                                    amax2[:, 3, b:b + 1], x3[:, b, :], ALU.mult, ALU.add)
                parts["fin"].frees("ffn", last)

            work = {
                "vprime": context_values, "agg": correlated, "norm": normalised_input, "rot": rotary, "sm": largest, "o": outputs,
                "wo": attended, "hs": shifted_norm, "gu": gated_hidden, "down": stack_output,
                "z_moments": z_moments, "zn": cross_tokens,
                "s1": lambda g: largest_scores(g, 0), "s2": lambda g: largest_scores(g, 1),
                "p1": lambda g: probabilities(g, 0), "p2": lambda g: probabilities(g, 1),
                "mix": gated_sum, "mixT": mixed, "quant": quantised_tokens, "hq": quantised_hidden,
                "ffn": result}

            first_turn = {1: magnitudes, 2: rounded_weights, 3: tap_weights}

            def group_turn(ga, gb, gn):
                steps.n = fsteps.n = 0
                parts["fin"] = fbanks_last if ga is None else fbanks
                for part, name, *args in schedule("last" if ga is None else "usual"):
                    before = part == "fin" or part == "ff" and tuple(args[0:2]) == (LAYERS - 1, PAIRS - 1)
                    g = gb if before else gn if part == "pre" else ga
                    if gb is None and name == "turns" and args[0] in first_turn:
                        first_turn[args[0]]()
                    if g is not None and name in work:
                        work[name](g, *args)
                assert ga is None or steps.n == VECTOR_STEPS, steps.n
                assert gb is None or fsteps.n == FINISH_STEPS, fsteps.n

            work["vprime"](0)
            work["agg"](0)
            group_turn(0, None, 1)
            with dve.Fori(0, NG - 2) as g:
                group_turn(g + 1, g, g + 2)
            group_turn(NG - 1, NG - 2, None)
            group_turn(None, NG - 1, None)

        @block.scalar
        def _(act):
            for g in range(NG):
                act.wait_ge(f_spec, g + 1)
                for n in range(2):
                    ins = act.activation(spec_t[g][:, n, :, :].rearrange("p b f -> p (b f)"),
                                         psum[2 * g + n][:, :], ACT.Copy)
                ins.then_inc(f_copied, 1)
            act.wait_ge(s_shift, 1)
            act.activation(corr_e[:, 0, :], corr[:, :], ACT.Exp, bias=corr_s[:, 0:1]).then_inc(s_exp, 1)

            def copy(g, bk, name, dst, rows=128, cols=512):
                bk.wait_filled(act, g, name)
                ins = act.activation(dst, bk[name][0:rows, 0:cols], ACT.Copy)
                bk.frees(name, ins)

            def tokens_in(g, l, pair):
                name, a, b = ("yT", l, pair), 2 * pair, 2 * pair + 2
                banks.wait_filled(act, g, name)
                u = banks[name]
                act.activation(yT[0:64, a:b, :].rearrange("p b t -> p (b t)"), u[0:64, 0:256], ACT.Copy)
                ins = act.activation(yT[64:128, a:b, 1:T],
                                     u[64:128, 0:256].rearrange("p (b t) -> p b t", b=2)[:, :, 0:T - 1], ACT.Copy)
                banks.frees(name, ins)

            def squares(g, i):
                (l, b), p = divmod(i, NB), i % 2
                for part, name in enumerate(("q", "k")):
                    if i >= 2:
                        ssq_ready.wait(act, g, 2 * i + part - 3)
                    banks.wait_filled(act, g, (name, l, b))
                    sq_ready.raised_by(act.activation(sq[:, p, part, :], banks[(name, l, b)][:, :], ACT.Square))
                banks.wait_filled(act, g, ("v", l, b))
                ins = act.activation(vx[:, b, :, 0:DH],
                                     banks[("v", l, b)][:, :].rearrange("p (h d) -> p h d", h=HEADS), ACT.Copy)
                banks.frees(("v", l, b), ins)

            def turned(g, i):
                copy(g, banks, ("qT", i), qT[:, i % 2, :, :].rearrange("p a t -> p (a t)"))
                copy(g, banks, ("kT", i), kT[:, i % 2, :, :].rearrange("p a t -> p (a t)"))

            def weights(g, i, s):
                p = i % 2
                nmax_ready.wait(act, g, 2 * i + s + 1)
                for h in range(HALF):
                    ins = act.activation(prob[:, p, s, h, :], banks[("sim", i, s)][:, h * 128:h * 128 + 128],
                                         ACT.Exp, bias=nmax[:, p, HALF * s + h:HALF * s + h + 1])
                banks.frees(("sim", i, s), ins)

            def weights_turned(g, i):
                for s in range(2):
                    copy(g, banks, ("pT", i, s), probT[:, s, :, :].rearrange("p h i -> p (h i)"))

            def out_turned(g, i):
                copy(g, banks, ("oT", i), oT[:, i % 2, :, :].rearrange("p a t -> p (a t)"))

            def hidden_in(g, l, pair):
                copy(g, hbanks, ("hT", l, pair), zT[:, 2 * pair:2 * pair + 2, :].rearrange("p b t -> p (b t)"),
                     cols=256)

            def gates(g, l, pair, j):
                rows, a = HT[j], 256 * pair
                hbanks.wait_filled(act, g, ("gu", l, pair, j))
                gel_ready.raised_by(act.activation(
                    gel[0:rows, j, a:a + 256], hbanks[("gu", l, pair, j)][0:rows, 0:256], ACT.Gelu,
                    bias=b1[0:rows, l, 1, j:j + 1]))

            def shifted_copy(g, name, dst, bias, cols=512, scale=1.0):
                parts["fin"].wait_filled(act, g, name)
                ins = act.activation(dst.rearrange("p b t -> p (b t)"), parts["fin"][name][:, 0:cols], ACT.Identity,
                                     bias=bias, scale=scale)
                parts["fin"].frees(name, ins)

            def exponentials(g, n):
                name, p, rows, keys = (("s1", p1, 128, S), ("s2", p2, S, 128))[n]
                cmax_ready.wait(act, g, n + 1)
                for b in range(NB):
                    ins = act.activation(p[:, b, :], parts["fin"][name][0:rows, b * keys:(b + 1) * keys], ACT.Exp,
                                         bias=nm1[0:rows, n, b:b + 1])
                parts["fin"].frees(name, ins)

            def gate(g):
                parts["fin"].wait_filled(act, g, "g")
                ins = act.activation(gt[:, :, :].rearrange("p b t -> p (b t)"), parts["fin"]["g"][:, :], ACT.Tanh,
                                     bias=cbs[:, 2:3], scale=0.5)
                parts["fin"].frees("g", ins)

            def quantised_turned(g):
                parts["fin"].wait_filled(act, g, "dT")
                ins = act.activation(ydT[:, :, 1:T + 1], parts["fin"]["dT"][:, :].rearrange("p (b t) -> p b t", b=NB),
                                     ACT.Copy)
                parts["fin"].frees("dT", ins)

            def hidden_turned(g, b):
                parts["fin"].wait_filled(act, g, ("hqT", b))
                ins = act.activation(silT[:, b, :, :].rearrange("p a t -> p (a t)"),
                                     parts["fin"][("hqT", b)][:, :].bitcast(BF16)[:, 0:512], ACT.Copy)
                parts["fin"].frees(("hqT", b), ins)

            def hidden(g, b):
                parts["fin"].wait_filled(act, g, ("h", b))
                if b >= 2:
                    silq_ready.wait(act, g, b - 1)
                ins = act.activation(sil[:, b % 2, :], parts["fin"][("h", b)][:, :], ACT.Silu)
                parts["fin"].frees(("h", b), ins)

            def flat(t):
                return t[:, :, :].rearrange("p b t -> p (b t)")

            work = {
                "yT": tokens_in, "qkv": squares, "turns": turned, "sm": weights, "pT": weights_turned,
                "oT": out_turned, "hT": hidden_in, "gu": gates,
                "zT": lambda g: copy(g, parts["fin"], "zT", flat(znT)),
                "qc": lambda g: shifted_copy(g, "qc", qcT, cbs[:, 0:1], scale=CORR_SCALE),
                "ks": lambda g: shifted_copy(g, "ks", ksT, cb[:, 1:2], cols=NB * S),
                "vs": lambda g: copy(g, parts["fin"], "vs", flat(vs), rows=S),
                "qs": lambda g: shifted_copy(g, "qs", qsT, cbs[:, 1:2], cols=NB * S, scale=CORR_SCALE),
                "kc": lambda g: shifted_copy(g, "kc", kcT, cb[:, 4:5]),
                "vc": lambda g: copy(g, parts["fin"], "vc", flat(vc)),
                "s1": lambda g: exponentials(g, 0), "s2": lambda g: exponentials(g, 1),
                "p1T": lambda g: copy(g, parts["fin"], "p1T", flat(p1T), rows=S),
                "c2s": lambda g: shifted_copy(g, "c2s", c2sT, cb[:, 2:3]),
                "a": lambda g: copy(g, parts["fin"], "a", flat(aT)),
                "s2c": lambda g: shifted_copy(g, "s2c", s2cT, cb[:, 5:6]),
                "g": gate, "dT": quantised_turned, "h": hidden, "hqT": hidden_turned}

            def group_turn(ga, gb, gn):
                parts["fin"] = fbanks_last if ga is None else fbanks
                for part, name, *args in schedule("last" if ga is None else "usual"):
                    before = part == "fin" or part == "ff" and tuple(args[0:2]) == (LAYERS - 1, PAIRS - 1)
                    g = gb if before else gn if part == "pre" else ga
                    if g is not None and name in work:
                        work[name](g, *args)

            group_turn(0, None, 1)
            with act.Fori(0, NG - 2) as g:
                group_turn(g + 1, g, g + 2)
            group_turn(NG - 1, NG - 2, None)
            group_turn(None, NG - 1, None)

        @block.tensor
        def _(pe):
            pe.wait_ge(c_loaded, 16)
            pe.wait_ge(w_loaded, 16 * weight_loads[0])
            sums = const("sums", 1)
            for n in range(2):
                pe.matmul(psum[6][:, n * 128:n * 128 + 128], sums[:, n * 128:n * 128 + 128],
                          corr_rows[:, n, :], start=True, stop=True)
            pe.matmul(psum[6][:, 256:384], corr_w[:, 2, :], corr_w[:, 3, :], start=True, stop=True)
            pe.wait_ge(bv_ready, 1)
            pe.matmul(psum[6][0:S, 384:512], bv_cols[:, :], corr_w[:, 3, :], start=True, stop=True)
            pe.wait_ge(w1_loaded, 32)
            for l in range(LAYERS):
                for part in range(2):
                    for j in range(3):
                        at, c = part * HID + j * 128, 6 * l + 3 * part + j
                        ins = pe.matmul(psum[7][0:HT[j], c:c + 1], w1[:, l, at:at + HT[j]], lngb[:, 1, l:l + 1],
                                        start=True, stop=True)
            ins.then_inc(prep_pe, 1)

            dft = const("dft")

            def transform(g):
                pe.wait_ge(f_norm, g + 1)
                if g == 0:
                    pe.wait_ge(f_ctx_loaded, 16)
                if g == NG - 1:
                    pe.wait_ge(prep_taken, 1)
                for b in range(NB):
                    at, u = slice(b * 128, b * 128 + 128), NB * g + b
                    pe.matmul(psum[2 * g][:, at], xn_all[:, u, :], dft, start=True, stop=True)
                    ins = pe.matmul(psum[2 * g + 1][:, at], ctx_all[:, u, :], dft[0:S, :], start=True, stop=True)
                ins.then_inc(f_spec, 1)

            def projected(g):
                pe.wait_ge(f_copied, g + 1)
                for b in range(NB):
                    for n in range(2):
                        ins = pe.matmul(psum[2 * g + n][:, b * 128:b * 128 + 128], spec_t[g][:, n, b, :],
                                        corr_w[:, n, :], start=True, stop=True)
                ins.then_inc(f_proj, 1)

            transform(0)
            for g in range(1, NG):
                transform(g)
                projected(g - 1)
            projected(NG - 1)
            pe.wait_ge(s_spec, NG)
            pe.matmul(psum[0][0:B, 0:128], spec[:, :], const("inverse_dft"), start=True,
                      stop=True).then_inc(s_corr, 1)
            pe.wait_ge(pool_set, 1)
            pe.wait_ge(late_loaded, 16 * (NB + 1))

            def turn(g, bk, name, parts, rows=128, width=128, idn=None, dt=None, read=()):
                bk.wait_for(pe, g, name, read)
                u = bk[name] if dt is None else bk[name][:, :].bitcast(dt)
                for n, part in enumerate(parts):
                    ins = pe.transpose(u[0:rows, n * width:(n + 1) * width], part,
                                       (ident if idn is None else idn)[0:width, 0:width])
                bk.fills(name, ins)

            def whole(g, bk, name, pairs, rows=128, cols=512, read=()):
                bk.wait_for(pe, g, name, read)
                for n, (lhsT, rhs) in enumerate(pairs):
                    ins = pe.matmul(bk[name][0:rows, 0:cols], lhsT, rhs, start=(n == 0),
                                    stop=(n == len(pairs) - 1))
                bk.fills(name, ins)

            def each(g, bk, name, products, rows=128, width=128, read=()):
                bk.wait_for(pe, g, name, read)
                for m, pairs in enumerate(products):
                    for n, (lhsT, rhs) in enumerate(pairs):
                        ins = pe.matmul(bk[name][0:rows, m * width:(m + 1) * width], lhsT, rhs,
                                        start=(n == 0), stop=(n == len(pairs) - 1))
                bk.fills(name, ins)

            def context_values(g):
                ctx_loaded.wait(pe, g, 1)
                each(g, pbanks, "vprime", [[(ctxT[:, b, :], wvo[:, :])] for b in range(NB)], rows=S)

            def correlated(g):
                hank_loaded.wait(pe, g, 1)
                each(g, pbanks, "agg", [[(hank[:, b, :], vprime[:, b, :])] for b in range(NB)], read=["vprime"])

            def tokens_in(g, l, pair):
                if l:
                    hbanks.wait_read(pe, g, ("down", l - 1, pair))
                else:
                    y_ready.wait(pe, g, pair + 1)
                turn(g, banks, ("yT", l, pair), [y0[:, b, :] for b in range(2 * pair, 2 * pair + 2)])

            def qkv(g, i):
                l, b = divmod(i, NB)
                for n, name in enumerate(("q", "k", "v")):
                    whole(g, banks, (name, l, b), [(yT[:, b, :], wqkv[:, l, n * INNER:(n + 1) * INNER])],
                          read=[("yT", l, b // 2)] if n == 0 else ())

            def turns(g, i):
                for n, name in enumerate(("qT", "kT")):
                    qk_ready.wait(pe, g, 2 * i + n + 1)
                    turn(g, banks, (name, i), [qk[:, i % 2, n, a * 128:a * 128 + 128] for a in range(4)])

            def scores(g, i):
                names = [("sim", i, s) for s in range(2)]
                for s, name in enumerate(names):
                    banks.wait_for(pe, g, name, [("qT", i), ("kT", i)] if s == 0 else ())
                    pe.matmul(banks[name][:, :], ident_b[:, :], mask_b[:, :, :].rearrange("p h j -> p (h j)"),
                              start=True, stop=False, skip_group_check=True)
                for h in range(HALF):
                    for s, name in enumerate(names):
                        ins = pe.matmul(banks[name][:, h * 128:h * 128 + 128],
                                        qT[64 * s:64 * s + 64, i % 2, h, :],
                                        kT[64 * s:64 * s + 64, i % 2, h, :], start=False,
                                        stop=(h == HALF - 1), skip_group_check=True)
                        if h == HALF - 1:
                            banks.fills(name, ins)

            def weights_turned(g, i):
                for s in range(2):
                    turn(g, banks, ("pT", i, s), [prob[:, i % 2, s, h, :] for h in range(HALF)],
                         read=[("sim", i, s)])

            def weighted(g, i, s):
                l, b = divmod(i, NB)
                each(g, banks, ("o", i, s), [[(probT[:, s, h, :], vx[:, b, 2 * h + s, :])]
                                             for h in range(HALF)],
                     width=DH + 1, read=[("v", l, b), ("pT", i, s)])

            def out_turned(g, i):
                turn(g, banks, ("oT", i), [o[:, i % 2, 2 * a:2 * a + 2, :].rearrange("p h d -> p (h d)")
                                           for a in range(4)], read=[("o", i, 0), ("o", i, 1)])

            def project(g, i):
                whole(g, banks, ("wo", i), [(oT[:, i % 2, a, :], wo[:, i // NB, a, :]) for a in range(4)],
                      cols=128, read=[("oT", i)])

            def shift_tokens(g, l, pair):
                banks.wait_for(pe, g, read=[("wo", NB * l + 2 * pair + n) for n in range(2)])
                hbanks.wait_for(pe, g, ("hs", l, pair))
                u = hbanks[("hs", l, pair)][:, 0:256].rearrange("p (b d) -> p b d", b=2)
                at = CONST_COLS["ident"][0]
                for n, eye in enumerate((ident, cst[:, at - 1:at + 127])):
                    d = slice(64 * n, 64 * n + 64)
                    ins = pe.matmul(u[:, :, d], eye, y1[:, 2 * pair:2 * pair + 2, d], start=True, stop=True)
                hbanks.fills(("hs", l, pair), ins)

            def hidden_in(g, l, pair):
                turn(g, hbanks, ("hT", l, pair), [xn[:, b, :] for b in range(2 * pair, 2 * pair + 2)],
                     read=[("hs", l, pair)])

            def gate_and_up(g, l, pair, j):
                name = ("gu", l, pair, j)
                hbanks.wait_for(pe, g, name, [("hT", l, pair)])
                tokens = zT[:, 2 * pair:2 * pair + 2, :].rearrange("p b t -> p (b t)")
                for n, part in enumerate((1, 0)):
                    at = part * HID + j * 128
                    ins = pe.matmul(hbanks[name][0:HT[j], 256 * n:256 * n + 256], w1g[:, l, at:at + HT[j]],
                                    tokens, start=True, stop=True)
                hbanks.fills(name, ins)

            def down(g, l, pair):
                k3 = HT[2] + 1
                each(g, hbanks, ("down", l, pair),
                     [[(hid[:, 0, b * 128:b * 128 + 128], w2[:, l, 0, :]),
                       (hid[:, 1, b * 128:b * 128 + 128], w2[:, l, 1, :]),
                       (hid[0:k3, 2, b * 128:b * 128 + 128], w2[0:k3, l, 2, :])]
                      for b in range(2 * pair, 2 * pair + 2)], read=[("gu", l, pair, j) for j in range(3)])

            def tokens_turned(g):
                z_ready.wait(pe, g, 1)
                turn(g, parts["fin"], "zT", [zn[:, b, :] for b in range(NB)])

            def token_features(g, name, n):
                whole(g, parts["fin"], name, [(cw[:, n, :], znT[:, :, :].rearrange("p b t -> p (b t)"))], read=["zT"])

            def context_features(g, name, n):
                ctxF_loaded.wait(pe, g, 1)
                whole(g, parts["fin"], name, [(cw[:, n, :], ctxF[:, :, :].rearrange("p b s -> p (b s)"))], cols=NB * S)

            def context_rows(g):
                ctxF_loaded.wait(pe, g, 1)
                each(g, parts["fin"], "vs", [[(ctxF[:, b, :], cw[:, 2, :])] for b in range(NB)], rows=S)

            def token_rows(g):
                each(g, parts["fin"], "vc", [[(znT[:, b, :], cw[:, 5, :])] for b in range(NB)], read=["zT"])

            def scores_s1(g):
                each(g, parts["fin"], "s1", [[(qcT[:, b, :], ksT[:, b, :])] for b in range(NB)], width=S,
                     read=["qc", "ks"])

            def scores_s2(g):
                each(g, parts["fin"], "s2", [[(qsT[:, b, :], kcT[:, b, :])] for b in range(NB)], rows=S,
                     read=["qs", "kc"])

            def probabilities_turned(g):
                cprob_ready.wait(pe, g, 1)
                turn(g, parts["fin"], "p1T", [p1[:, b, :] for b in range(NB)], rows=S)

            def context_weighted(g):
                each(g, parts["fin"], "c2s", [[(vs[:, b, :], p1T[:, b, :])] for b in range(NB)],
                     read=["p1T", "vs"])

            def interpolated(g):
                cprob_ready.wait(pe, g, 2)
                each(g, parts["fin"], "a", [[(p2[:, b, :], const("interp", S))] for b in range(NB)])

            def tokens_weighted(g):
                each(g, parts["fin"], "s2c", [[(vc[:, b, :], aT[:, b, :])] for b in range(NB)],
                     read=["a", "vc"])

            def gate(g):
                whole(g, parts["fin"], "g", [(cw[:, 6, :], c2sT[:, :, :].rearrange("p b t -> p (b t)")),
                                       (cw[:, 7, :], s2cT[:, :, :].rearrange("p b t -> p (b t)"))],
                      read=["c2s", "s2c"])

            def mixed_turned(g):
                mix_ready.wait(pe, g, 1)
                turn(g, parts["fin"], "mixT", [gt[:, b, :] for b in range(NB)])

            def quantised_turned(g):
                yd_ready.wait(pe, g, 1)
                turn(g, parts["fin"], "dT", [yd[:, b, :] for b in range(NB)])

            def hidden(g, b):
                whole(g, parts["fin"], ("h", b), [(ydT[:, b, k:k + T], wc[:, k, :]) for k in range(3)]
                      + [(ones3[:, :], conv_b3[:, :])], read=["dT"])

            def hidden_turned(g, b):
                silq_ready.wait(pe, g, b + 1)
                turn(g, parts["fin"], ("hqT", b), [silb[:, b % 2, a * 128:a * 128 + 128] for a in range(4)],
                     idn=ident_b, dt=BF16)

            def output(g):
                each(g, parts["fin"], "ffn", [[(silT[:, b, a, :], q2T[:, a, :]) for a in range(4)] for b in range(NB)],
                     read=[("hqT", b) for b in range(NB)])

            work = {
                "vprime": context_values, "agg": correlated, "yT": tokens_in, "qkv": qkv, "turns": turns,
                "scores": scores, "pT": weights_turned, "o": weighted, "oT": out_turned, "wo": project,
                "hs": shift_tokens, "hT": hidden_in, "gu": gate_and_up, "down": down,
                "zT": tokens_turned, "qc": lambda g: token_features(g, "qc", 0),
                "ks": lambda g: context_features(g, "ks", 1), "vs": context_rows,
                "qs": lambda g: context_features(g, "qs", 3), "kc": lambda g: token_features(g, "kc", 4),
                "vc": token_rows, "s1": scores_s1, "s2": scores_s2, "p1T": probabilities_turned,
                "c2s": context_weighted, "a": interpolated, "s2c": tokens_weighted, "g": gate,
                "mixT": mixed_turned, "dT": quantised_turned, "h": hidden, "hqT": hidden_turned, "ffn": output}

            def magnitude_sums():
                pe.wait_ge(qsum_ready, 1)
                pe.matmul(psum[NBANKS - 1][:, 0:2], ones[:, :], qsum[:, :], start=True,
                          stop=True).then_inc(prep_sums, 1)

            first_turn = {2: magnitude_sums}

            def group_turn(ga, gb, gn):
                parts["fin"] = fbanks_last if ga is None else fbanks
                for part, name, *args in schedule("last" if ga is None else "usual"):
                    before = part == "fin" or part == "ff" and tuple(args[0:2]) == (LAYERS - 1, PAIRS - 1)
                    g = gb if before else gn if part == "pre" else ga
                    if gb is None and name == "turns" and args[0] in first_turn:
                        first_turn[args[0]]()
                    change = BANK_CHANGES.get((part, name, *args)) if ga is not None else None
                    if change is not None and g is not None:
                        if change[0] == "pre":
                            of = ga if name == FIRST_FIN else gn
                            if of is not None:
                                pbanks.wait_for(pe, of, read=[change[1]])
                        elif gb is not None:
                            parts["fin"].wait_for(pe, gb, read=[change[1]])
                        else:
                            pe.wait_ge(sums_taken, 1)
                    if g is not None and name in work:
                        work[name](g, *args)

            work["vprime"](0)
            work["agg"](0)
            group_turn(0, None, 1)
            pe.wait_ge(conv_loaded, 48)
            with pe.Fori(0, NG - 2) as g:
                group_turn(g + 1, g, g + 2)
            group_turn(NG - 1, NG - 2, None)
            group_turn(None, NG - 1, None)


_INS = ['x', 'ctx', 'ctxT', 'constants', 'weights', 'rows']
_OUTS = [((B, T, D), 'float32')]


def kernel(**inputs):
    import numpy as _np
    import concourse.bacc as _bacc
    from concourse import mybir as _mybir
    from concourse.bass_utils import run_bass_kernel_spmd as _run

    nc = _bacc.Bacc("TRN2", target_bir_lowering=False, num_devices=1)
    arrays, args = {}, []
    given = {k: _np.asarray(v) for k, v in inputs.items()}
    laid = {'x': given['x'], 'ctx': given['ctx_1024'], 'ctxT': given['ctx_1024'][:, ::-1].transpose(2, 0, 1),
            'constants': constant_array(), 'weights': weight_array(given), 'rows': row_array(given)}
    for name in _INS:
        a = _np.ascontiguousarray(laid[name])
        arrays[f"in_{name}_dram"] = a
        args.append(nc.dram_tensor(f"in_{name}_dram", a.shape, _mybir.dt.from_np(a.dtype), kind="ExternalInput").ap())
    for i, (shape, dtype) in enumerate(_OUTS):
        dt = _mybir.dt.from_np(_np.dtype(dtype))
        args.append(nc.dram_tensor(f"out_{i}_dram", shape, dt, kind="ExternalOutput").ap())
    xattn_ffn_stack_kernel(nc, *args)
    r = _run(nc, [arrays], core_ids=[0])
    return r.results[0]["out_0_dram"]
```
